# Optimizing a Trainium2 kernel written in Bass

```python
import numpy as np
import jax
import jax.numpy as jnp

def _softmax(x, axis=-1):
    return jax.nn.softmax(x, axis=axis)

def _gelu(x):
    return jax.nn.gelu(x, approximate=True)

def _silu(x):
    return jax.nn.silu(x)

def _sigmoid(x):
    return jax.nn.sigmoid(x)

def _layernorm(x, axis=-1, eps=1e-05):
    m = jnp.mean(x, axis=axis, keepdims=True)
    v = jnp.var(x, axis=axis, keepdims=True)
    return (x - m) / jnp.sqrt(v + eps)

def _scatter_add(tgt, idx, src, axis=0):
    return tgt.at[idx].add(src)

def _segment_sum(src, seg, n):
    return jax.ops.segment_sum(src, seg, n)
kernel_name = 'mk_decoder_preln_d4_seqx_r4_181b19'

def setup_inputs(seed: int=0):
    np.random.seed(seed)
    _w = jnp.asarray

    def _rec_inputs():
        import jax
        import jax.numpy as jnp
        _rk = jax.random.key(seed)
        x = 7.22e-05 + 1 * jax.random.normal(jax.random.fold_in(_rk, 1), (2, 512, 256), jnp.float32)
        _lenS = 512 - jax.random.randint(jax.random.fold_in(_rk, 7), (2,), 0, max(1, 512 // 4) + 1, jnp.int32)
        _lenS2 = 1024 - jax.random.randint(jax.random.fold_in(_rk, 8), (2,), 0, max(1, 1024 // 4) + 1, jnp.int32)
        _ctx_1024P = jax.random.normal(jax.random.fold_in(_rk, 11), (2, 16, 256), jnp.float32)
        _ctx_1024c = jax.random.dirichlet(jax.random.fold_in(_rk, 511), 0.3 * jnp.ones((16,), jnp.float32), (2, 1024))
        _ctx_1024t = jnp.einsum('bsk,bkd->bsd', _ctx_1024c, _ctx_1024P)
        _ctx_1024t = _ctx_1024t * jax.lax.rsqrt(jnp.mean(jnp.square(_ctx_1024t)) + 1e-12) * 0.953939
        ctx_1024 = -4.77421e-07 + 0.031248 * (_ctx_1024t + 0.3 * jax.random.normal(jax.random.fold_in(_rk, 611), (2, 1024, 256), jnp.float32))
        fside_BxSxS2_0 = jax.random.uniform(jax.random.fold_in(_rk, 13), (2, 512, 1024), jnp.float32, 0.0, 1)
        _validS = jnp.arange(512)[None, :] < _lenS[:, None]
        _validS2 = jnp.arange(1024)[None, :] < _lenS2[:, None]
        _causal = jnp.tril(jnp.ones((512, 512), dtype=bool))
        mask_BxS2_if1 = jnp.where(jnp.ones((2, 1024), dtype=bool), 1, 0).astype(jnp.int32)
        mask_BxSxS2_ik1 = jnp.where(jnp.broadcast_to(_validS2[:, None, :], (2, 512, 1024)), 1, 0).astype(jnp.int32)
        return (x, ctx_1024, fside_BxSxS2_0, mask_BxS2_if1, mask_BxSxS2_ik1)
    x, ctx_1024, fside_BxSxS2_0, mask_BxS2_if1, mask_BxSxS2_ik1 = _rec_inputs()

    def _L0_attn_setup():
        import jax, jax.numpy as jnp
        import numpy as np
        B, T, D_MODEL = (2, 1024, 256)
        HD, H = (256, 16)
        HDIM = HD // H
        FF = 1024
        KS = 4

        def _ln(x, w, b, eps=1e-05):
            m = x.mean(-1, keepdims=True)
            v = ((x - m) ** 2).mean(-1, keepdims=True)
            return (x - m) / jnp.sqrt(v + eps) * w + b
        key = jax.random.key(seed)
        ks = jax.random.split(key, 8)
        s = 0.02
        return {'x': jax.random.normal(ks[0], (B, T, D_MODEL), dtype=jnp.float32), 'ln1_w': jnp.ones(D_MODEL), 'ln1_b': jnp.zeros(D_MODEL), 'conv_w': jax.random.normal(ks[1], (D_MODEL, 1, KS)) * s, 'conv_b': jnp.zeros(D_MODEL), 'qk_w': jax.random.normal(ks[2], (HD, D_MODEL)) * s, 'v_w': jnp.eye(HD, D_MODEL), 'g_w': jax.random.normal(ks[3], (HD, D_MODEL)) * s, 'g_b': jnp.full((HD,), 2.0), 'o_w': jax.random.normal(ks[4], (D_MODEL, HD)) * s, 'onorm_w': jnp.ones(D_MODEL), 'onorm_b': jnp.zeros(D_MODEL), 'gamma_attn': (jnp.ones((H, 1, 1)) * 0.999).at[0].set(1.0), 'ln2_w': jnp.ones(D_MODEL), 'ln2_b': jnp.zeros(D_MODEL), 'gate_w': jax.random.normal(ks[5], (FF, D_MODEL)) * s, 'up_w': jax.random.normal(ks[6], (FF, D_MODEL)) * s, 'down_w': jax.random.normal(ks[7], (D_MODEL, FF)) * s, 'gamma1': jnp.ones(D_MODEL) * 0.1, 'gamma2': jnp.ones(D_MODEL) * 0.1}
    _L0_attn_all = _L0_attn_setup()
    _L0_attn_in = {k: v for k, v in _L0_attn_all.items() if k in ('ln1_w', 'ln1_b', 'conv_w', 'conv_b', 'qk_w', 'v_w', 'g_w', 'g_b', 'o_w', 'onorm_w', 'onorm_b', 'gamma_attn', 'ln2_w', 'ln2_b', 'gate_w', 'up_w', 'down_w', 'gamma1', 'gamma2')}
    del _L0_attn_all

    def _L0_xattn_setup():
        import jax, jax.numpy as jnp
        import numpy as np
        E, T, H, F = (8, 256, 256, 1024)
        key = jax.random.key(seed)
        k1, k2, k3 = jax.random.split(key, 3)
        x = jax.random.normal(k1, (E, T, H), dtype=jnp.float32)
        w1 = jax.random.normal(k2, (E, F, H), dtype=jnp.float32) * (1.0 / np.sqrt(H))
        w2 = jax.random.normal(k3, (E, F, H), dtype=jnp.float32) * (1.0 / np.sqrt(F))
        return {'x': x, 'w1': w1, 'w2': w2}
    _L0_xattn_all = _L0_xattn_setup()
    _L0_xattn_in = {k: v for k, v in _L0_xattn_all.items() if k in ()}
    del _L0_xattn_all

    def _L0_ffn_setup():
        import jax, jax.numpy as jnp
        import numpy as np
        from jax import lax
        TOP_K = 1
        key = jax.random.key(seed)
        ks = jax.random.split(key, 9)
        B, N, C = (4, 512, 256)
        E, L, R = (6, 100, 16)
        return {'feats': jax.random.normal(ks[0], (B, N, C), jnp.float32), 'A': jax.random.normal(ks[1], (E, L, R), jnp.float32) * 0.05, 'B': jax.random.normal(ks[2], (E, R, C), jnp.float32) * 0.05, 'w_gate': jax.random.normal(ks[3], (C, E), jnp.float32) * 0.02, 'wt_w': jax.random.normal(ks[4], (C, C), jnp.float32) * (1.0 / np.sqrt(C)), 'wt_b': jax.random.normal(ks[5], (C,), jnp.float32) * 0.01, 'wd_w': jax.random.normal(ks[6], (C, C), jnp.float32) * (1.0 / np.sqrt(C)), 'wd_b': jax.random.normal(ks[7], (C,), jnp.float32) * 0.01, 'scale': jnp.full((1,), 0.001, jnp.float32)}
    _L0_ffn_all = _L0_ffn_setup()
    _L0_ffn_in = {k: v for k, v in _L0_ffn_all.items() if k in ('A', 'B', 'w_gate', 'wt_w', 'wt_b', 'wd_w', 'wd_b', 'scale')}
    del _L0_ffn_all

    def _L1_attn_setup():
        import jax, jax.numpy as jnp
        import numpy as np
        B, T, D = (4, 1024, 256)
        NEG_CLAMP = -30.0
        EPS = 1e-09

        def _wkv_scan(k, v, w, u):
            Bn, Tn, Dn = k.shape
            p0 = jnp.full((Bn, Dn), -jnp.inf, k.dtype)
            q0 = jnp.zeros((Bn, Dn), k.dtype)

            def step(carry, kv_t):
                p, q = carry
                k_t, v_t = kv_t
                new_p = jnp.maximum(p, u + k_t)
                scale_old = jnp.exp(jnp.maximum(p - new_p, NEG_CLAMP))
                scale_cur = jnp.exp(jnp.maximum(u + k_t - new_p, NEG_CLAMP))
                wkv_t = (scale_old * q + scale_cur * v_t) / (scale_old + scale_cur + EPS)
                new_p2 = jnp.maximum(p + w, k_t)
                scale_prev = jnp.exp(jnp.maximum(p + w - new_p2, NEG_CLAMP))
                scale_new = jnp.exp(jnp.maximum(k_t - new_p2, NEG_CLAMP))
                q2 = scale_prev * q + scale_new * v_t
                return ((new_p2, q2), wkv_t)
            kT = jnp.swapaxes(k, 0, 1)
            vT = jnp.swapaxes(v, 0, 1)
            _, wkvT = jax.lax.scan(step, (p0, q0), (kT, vT))
            return jnp.swapaxes(wkvT, 0, 1)
        key = jax.random.key(seed)
        ks = jax.random.split(key, 10)
        s = 0.02
        return {'x': jax.random.normal(ks[0], (B, T, D), jnp.float32), 'time_mix_k': jax.random.uniform(ks[1], (D,), jnp.float32), 'time_mix_v': jax.random.uniform(ks[2], (D,), jnp.float32), 'time_mix_r': jax.random.uniform(ks[3], (D,), jnp.float32), 'W_k': jax.random.normal(ks[4], (D, D), jnp.float32) * s, 'W_v': jax.random.normal(ks[5], (D, D), jnp.float32) * s, 'W_r': jax.random.normal(ks[6], (D, D), jnp.float32) * s, 'W_o': jax.random.normal(ks[7], (D, D), jnp.float32) * s, 'time_decay': -(1.0 + jax.random.uniform(ks[8], (D,), jnp.float32)), 'time_first': 0.1 * jax.random.normal(ks[9], (D,), jnp.float32)}
    _L1_attn_all = _L1_attn_setup()
    _L1_attn_in = {k: v for k, v in _L1_attn_all.items() if k in ('time_mix_k', 'time_mix_v', 'time_mix_r', 'W_k', 'W_v', 'W_r', 'W_o', 'time_decay', 'time_first')}
    del _L1_attn_all

    def _L1_xattn_setup():
        import jax, jax.numpy as jnp
        import numpy as np
        B, L, P, D = (32, 512, 64, 256)
        MAX_HOP = 2
        key = jax.random.key(seed)
        k1, k2, k3, k4 = jax.random.split(key, 4)
        return {'context': jax.random.normal(k1, (B, L, D), dtype=jnp.float32), 'mem0': jax.random.normal(k2, (B, P, D), dtype=jnp.float32), 'W0': jax.random.normal(k3, (D, D), dtype=jnp.float32) * 0.02, 'W1': jax.random.normal(k4, (D, D), dtype=jnp.float32) * 0.02, 'mask': jnp.ones((B, L), dtype=jnp.int32)}
    _L1_xattn_all = _L1_xattn_setup()
    _L1_xattn_in = {k: v for k, v in _L1_xattn_all.items() if k in ('W0', 'W1')}
    del _L1_xattn_all

    def _L1_ffn_setup():
        import jax, jax.numpy as jnp
        import numpy as np
        QP = 127.0
        MIN_RANGE = 1e-06

        def _ste_round(x):
            return x + jax.lax.stop_gradient(jnp.round(x) - x)

        def _quant_per_tensor(x):
            scale = jnp.maximum(jnp.max(jnp.abs(x)), MIN_RANGE) / QP
            return (_ste_round(x / scale), scale)

        def _qlinear(x2d, w, b):
            xq, sx = _quant_per_tensor(x2d)
            wq, sw = _quant_per_tensor(w)
            out = jnp.matmul(xq, wq.T) + b[None, :]
            return out * (sw * sx)
        key = jax.random.key(seed)
        k = jax.random.split(key, 5)
        B, N, D, H = (8, 256, 256, 1024)
        return {'x': jax.random.normal(k[0], (B, N, D), dtype=jnp.float32), 'w1': jax.random.normal(k[1], (H, D), dtype=jnp.float32) * 0.02, 'b1': jax.random.normal(k[2], (H,), dtype=jnp.float32) * 0.02, 'w2': jax.random.normal(k[3], (D, H), dtype=jnp.float32) * 0.02, 'b2': jax.random.normal(k[4], (D,), dtype=jnp.float32) * 0.02}
    _L1_ffn_all = _L1_ffn_setup()
    _L1_ffn_in = {k: v for k, v in _L1_ffn_all.items() if k in ('w1', 'b1', 'w2', 'b2')}
    del _L1_ffn_all

    def _L2_attn_setup():
        import jax, jax.numpy as jnp
        import numpy as np
        CLIP_VAL = 8
        FRACTION_BITS = 12
        SCALE = float(2 ** FRACTION_BITS)
        EPS = 1.0 / SCALE
        HEADS = 16
        DIM_HEAD = 64

        def make_fxp(x):
            c = CLIP_VAL - EPS
            x = jnp.clip(x, -c, c)
            return jnp.trunc(x * SCALE) / SCALE
        key = jax.random.key(seed)
        k1, k2, k3, k4 = jax.random.split(key, 4)
        B, N, D = (4, 512, 256)
        inner = HEADS * DIM_HEAD
        x = jax.random.normal(k1, (B, N, D), dtype=jnp.float32)
        w_qkv = jax.random.normal(k2, (3 * inner, D), dtype=jnp.float32) * D ** (-0.5)
        w_proj = jax.random.normal(k3, (D, inner), dtype=jnp.float32) * inner ** (-0.5)
        b_proj = jax.random.normal(k4, (D,), dtype=jnp.float32) * 0.01
        return {'x': x, 'w_qkv': w_qkv, 'w_proj': w_proj, 'b_proj': b_proj}
    _L2_attn_all = _L2_attn_setup()
    _L2_attn_in = {k: v for k, v in _L2_attn_all.items() if k in ('w_qkv', 'w_proj', 'b_proj')}
    del _L2_attn_all

    def _L2_xattn_setup():
        import jax, jax.numpy as jnp
        import numpy as np
        NUM_HEADS = 16
        HIDDEN = 256
        B, S = (2, 512)

        def _split_heads(x, H):
            b, s, d = x.shape
            return x.reshape(b, s, H, d // H).transpose(0, 2, 1, 3)
        key = jax.random.key(seed)
        ks = jax.random.split(key, 14)
        D = HIDDEN
        scale = 1.0 / np.sqrt(D)
        inp = {'query': jax.random.normal(ks[0], (B, S, D), jnp.float32), 'key_in': jax.random.normal(ks[1], (B, S, D), jnp.float32), 'value': jax.random.normal(ks[2], (B, S, D), jnp.float32), 'group_prob': jax.random.uniform(ks[3], (B, S, S), jnp.float32), 'mask': jax.random.randint(ks[4], (B, S, S), 0, 2, jnp.int32), 'wq_k': jax.random.normal(ks[5], (D, D), jnp.float32) * scale, 'wq_b': jnp.zeros((D,), jnp.float32), 'wk_k': jax.random.normal(ks[6], (D, D), jnp.float32) * scale, 'wk_b': jnp.zeros((D,), jnp.float32), 'wv_k': jax.random.normal(ks[7], (D, D), jnp.float32) * scale, 'wv_b': jnp.zeros((D,), jnp.float32), 'wo_k': jax.random.normal(ks[8], (D, D), jnp.float32) * scale, 'wo_b': jnp.zeros((D,), jnp.float32)}
        return inp
    _L2_xattn_all = _L2_xattn_setup()
    _L2_xattn_in = {k: v for k, v in _L2_xattn_all.items() if k in ('wq_k', 'wq_b', 'wk_k', 'wk_b', 'wv_k', 'wv_b', 'wo_k', 'wo_b')}
    del _L2_xattn_all

    def _L2_ffn_setup():
        import jax, jax.numpy as jnp
        import numpy as np
        D_MODEL = 256
        M = 64
        INNER = 16
        key = jax.random.key(seed)
        ks = jax.random.split(key, 9)

        def init(k, shape, fan_in):
            bound = 1.0 / np.sqrt(fan_in)
            return jax.random.uniform(k, shape, jnp.float32, -bound, bound)
        x = jax.random.normal(ks[0], (16, 1024, D_MODEL), dtype=jnp.float32)
        Win = init(ks[1], (D_MODEL, M), D_MODEL)
        bin_ = init(ks[2], (M,), D_MODEL)
        W1 = init(ks[3], (M, INNER), 1)
        b1 = init(ks[4], (M, INNER), 1)
        W2 = init(ks[5], (M, INNER), INNER)
        b2 = init(ks[6], (M,), INNER)
        Wout = init(ks[7], (M, D_MODEL), M)
        bout = init(ks[8], (D_MODEL,), M)
        return {'x': x, 'Win': Win, 'bin_': bin_, 'W1': W1, 'b1': b1, 'W2': W2, 'b2': b2, 'Wout': Wout, 'bout': bout}
    _L2_ffn_all = _L2_ffn_setup()
    _L2_ffn_in = {k: v for k, v in _L2_ffn_all.items() if k in ('Win', 'bin_', 'W1', 'b1', 'W2', 'b2', 'Wout', 'bout')}
    del _L2_ffn_all

    def _L3_attn_setup():
        import jax, jax.numpy as jnp
        import numpy as np
        import math
        B, T, C = (2, 512, 256)
        H = 16
        D = C // H

        def alibi_slopes(n_heads):
            start = 2.0 ** (-2.0 ** (-(math.log2(n_heads) - 3)))
            return jnp.asarray([start * start ** i for i in range(n_heads)], dtype=jnp.float32)
        key = jax.random.key(seed)
        ks = jax.random.split(key, 6)
        x = jax.random.normal(ks[0], (B, T, C), dtype=jnp.float32)
        W_attn = jax.random.normal(ks[1], (C, 3 * C), dtype=jnp.float32) * 0.02
        b_attn = jnp.zeros((3 * C,), dtype=jnp.float32)
        W_proj = jax.random.normal(ks[2], (C, C), dtype=jnp.float32) * 0.02
        b_proj = jnp.zeros((C,), dtype=jnp.float32)
        temperature = jnp.ones((1,), dtype=jnp.float32) * 2.0
        return {'x': x, 'W_attn': W_attn, 'b_attn': b_attn, 'W_proj': W_proj, 'b_proj': b_proj, 'temperature': temperature}
    _L3_attn_all = _L3_attn_setup()
    _L3_attn_in = {k: v for k, v in _L3_attn_all.items() if k in ('W_attn', 'b_attn', 'W_proj', 'b_proj', 'temperature')}
    del _L3_attn_all

    def _L3_xattn_setup():
        import jax, jax.numpy as jnp
        import numpy as np
        B, S, D = (1, 1024, 256)
        H, DK, DV = (16, 64, 64)
        key = jax.random.key(seed)
        ks = jax.random.split(key, 12)
        s = 0.02
        return {'queries': jax.random.normal(ks[0], (B, S, D), jnp.float32), 'keys': jax.random.normal(ks[1], (B, S, D), jnp.float32), 'values': jax.random.normal(ks[2], (B, S, D), jnp.float32), 'Wq': jax.random.normal(ks[3], (H * DK, D), jnp.float32) * s, 'bq': jnp.zeros((H * DK,), jnp.float32), 'Wk': jax.random.normal(ks[4], (H * DK, D), jnp.float32) * s, 'bk': jnp.zeros((H * DK,), jnp.float32), 'Wv': jax.random.normal(ks[5], (H * DV, D), jnp.float32) * s, 'bv': jnp.zeros((H * DV,), jnp.float32), 'Wo': jax.random.normal(ks[6], (D, H * DV), jnp.float32) * s, 'bo': jnp.zeros((D,), jnp.float32)}
    _L3_xattn_all = _L3_xattn_setup()
    _L3_xattn_in = {k: v for k, v in _L3_xattn_all.items() if k in ('Wq', 'bq', 'Wk', 'bk', 'Wv', 'bv', 'Wo', 'bo')}
    del _L3_xattn_all

    def _L3_ffn_setup():
        import jax, jax.numpy as jnp
        import numpy as np
        EMB = 256
        FF = 4 * EMB

        def _ternary(w):
            scale = jnp.maximum(jnp.mean(jnp.abs(w)), 1e-08)
            w_t = jnp.clip(jnp.round(w / scale), -1.0, 1.0)
            return w + jax.lax.stop_gradient(w_t - w)
        key = jax.random.key(seed)
        kx, k1, k2, kb1, kb2 = jax.random.split(key, 5)
        x = jax.random.normal(kx, (4, 512, EMB), dtype=jnp.float32)
        lim1 = 1.0 / np.sqrt(EMB)
        lim2 = 1.0 / np.sqrt(FF)
        W1 = jax.random.uniform(k1, (FF, EMB), jnp.float32, -lim1, lim1)
        b1 = jax.random.uniform(kb1, (FF,), jnp.float32, -lim1, lim1)
        W2 = jax.random.uniform(k2, (EMB, FF), jnp.float32, -lim2, lim2)
        b2 = jax.random.uniform(kb2, (EMB,), jnp.float32, -lim2, lim2)
        return {'x': x, 'W1': W1, 'b1': b1, 'W2': W2, 'b2': b2}
    _L3_ffn_all = _L3_ffn_setup()
    _L3_ffn_in = {k: v for k, v in _L3_ffn_all.items() if k in ('W1', 'b1', 'W2', 'b2')}
    del _L3_ffn_all
    return {'x': x, 'ctx_1024': ctx_1024, 'fside_BxSxS2_0': fside_BxSxS2_0, 'mask_BxS2_if1': mask_BxS2_if1, 'mask_BxSxS2_ik1': mask_BxSxS2_ik1, 'L0_attn_ln1_w': _L0_attn_in['ln1_w'], 'L0_attn_ln1_b': _L0_attn_in['ln1_b'], 'L0_attn_conv_w': _L0_attn_in['conv_w'], 'L0_attn_conv_b': _L0_attn_in['conv_b'], 'L0_attn_qk_w': _L0_attn_in['qk_w'], 'L0_attn_v_w': _L0_attn_in['v_w'], 'L0_attn_g_w': _L0_attn_in['g_w'], 'L0_attn_g_b': _L0_attn_in['g_b'], 'L0_attn_o_w': _L0_attn_in['o_w'], 'L0_attn_onorm_w': _L0_attn_in['onorm_w'], 'L0_attn_onorm_b': _L0_attn_in['onorm_b'], 'L0_attn_gamma_attn': _L0_attn_in['gamma_attn'], 'L0_attn_ln2_w': _L0_attn_in['ln2_w'], 'L0_attn_ln2_b': _L0_attn_in['ln2_b'], 'L0_attn_gate_w': _L0_attn_in['gate_w'], 'L0_attn_up_w': _L0_attn_in['up_w'], 'L0_attn_down_w': _L0_attn_in['down_w'], 'L0_attn_gamma1': _L0_attn_in['gamma1'], 'L0_attn_gamma2': _L0_attn_in['gamma2'], 'L0_ffn_A': _L0_ffn_in['A'], 'L0_ffn_B': _L0_ffn_in['B'], 'L0_ffn_w_gate': _L0_ffn_in['w_gate'], 'L0_ffn_wt_w': _L0_ffn_in['wt_w'], 'L0_ffn_wt_b': _L0_ffn_in['wt_b'], 'L0_ffn_wd_w': _L0_ffn_in['wd_w'], 'L0_ffn_wd_b': _L0_ffn_in['wd_b'], 'L0_ffn_scale': _L0_ffn_in['scale'], 'L1_attn_time_mix_k': _L1_attn_in['time_mix_k'], 'L1_attn_time_mix_v': _L1_attn_in['time_mix_v'], 'L1_attn_time_mix_r': _L1_attn_in['time_mix_r'], 'L1_attn_W_k': _L1_attn_in['W_k'], 'L1_attn_W_v': _L1_attn_in['W_v'], 'L1_attn_W_r': _L1_attn_in['W_r'], 'L1_attn_W_o': _L1_attn_in['W_o'], 'L1_attn_time_decay': _L1_attn_in['time_decay'], 'L1_attn_time_first': _L1_attn_in['time_first'], 'L1_xattn_W0': _L1_xattn_in['W0'], 'L1_xattn_W1': _L1_xattn_in['W1'], 'L1_ffn_w1': _L1_ffn_in['w1'], 'L1_ffn_b1': _L1_ffn_in['b1'], 'L1_ffn_w2': _L1_ffn_in['w2'], 'L1_ffn_b2': _L1_ffn_in['b2'], 'L2_attn_w_qkv': _L2_attn_in['w_qkv'], 'L2_attn_w_proj': _L2_attn_in['w_proj'], 'L2_attn_b_proj': _L2_attn_in['b_proj'], 'L2_xattn_wq_k': _L2_xattn_in['wq_k'], 'L2_xattn_wq_b': _L2_xattn_in['wq_b'], 'L2_xattn_wk_k': _L2_xattn_in['wk_k'], 'L2_xattn_wk_b': _L2_xattn_in['wk_b'], 'L2_xattn_wv_k': _L2_xattn_in['wv_k'], 'L2_xattn_wv_b': _L2_xattn_in['wv_b'], 'L2_xattn_wo_k': _L2_xattn_in['wo_k'], 'L2_xattn_wo_b': _L2_xattn_in['wo_b'], 'L2_ffn_Win': _L2_ffn_in['Win'], 'L2_ffn_bin_': _L2_ffn_in['bin_'], 'L2_ffn_W1': _L2_ffn_in['W1'], 'L2_ffn_b1': _L2_ffn_in['b1'], 'L2_ffn_W2': _L2_ffn_in['W2'], 'L2_ffn_b2': _L2_ffn_in['b2'], 'L2_ffn_Wout': _L2_ffn_in['Wout'], 'L2_ffn_bout': _L2_ffn_in['bout'], 'L3_attn_W_attn': _L3_attn_in['W_attn'], 'L3_attn_b_attn': _L3_attn_in['b_attn'], 'L3_attn_W_proj': _L3_attn_in['W_proj'], 'L3_attn_b_proj': _L3_attn_in['b_proj'], 'L3_attn_temperature': _L3_attn_in['temperature'], 'L3_xattn_Wq': _L3_xattn_in['Wq'], 'L3_xattn_bq': _L3_xattn_in['bq'], 'L3_xattn_Wk': _L3_xattn_in['Wk'], 'L3_xattn_bk': _L3_xattn_in['bk'], 'L3_xattn_Wv': _L3_xattn_in['Wv'], 'L3_xattn_bv': _L3_xattn_in['bv'], 'L3_xattn_Wo': _L3_xattn_in['Wo'], 'L3_xattn_bo': _L3_xattn_in['bo'], 'L3_ffn_W1': _L3_ffn_in['W1'], 'L3_ffn_b1': _L3_ffn_in['b1'], 'L3_ffn_W2': _L3_ffn_in['W2'], 'L3_ffn_b2': _L3_ffn_in['b2']}

def reference(x, ctx_1024, fside_BxSxS2_0, mask_BxS2_if1, mask_BxSxS2_ik1, L0_attn_ln1_w, L0_attn_ln1_b, L0_attn_conv_w, L0_attn_conv_b, L0_attn_qk_w, L0_attn_v_w, L0_attn_g_w, L0_attn_g_b, L0_attn_o_w, L0_attn_onorm_w, L0_attn_onorm_b, L0_attn_gamma_attn, L0_attn_ln2_w, L0_attn_ln2_b, L0_attn_gate_w, L0_attn_up_w, L0_attn_down_w, L0_attn_gamma1, L0_attn_gamma2, L0_ffn_A, L0_ffn_B, L0_ffn_w_gate, L0_ffn_wt_w, L0_ffn_wt_b, L0_ffn_wd_w, L0_ffn_wd_b, L0_ffn_scale, L1_attn_time_mix_k, L1_attn_time_mix_v, L1_attn_time_mix_r, L1_attn_W_k, L1_attn_W_v, L1_attn_W_r, L1_attn_W_o, L1_attn_time_decay, L1_attn_time_first, L1_xattn_W0, L1_xattn_W1, L1_ffn_w1, L1_ffn_b1, L1_ffn_w2, L1_ffn_b2, L2_attn_w_qkv, L2_attn_w_proj, L2_attn_b_proj, L2_xattn_wq_k, L2_xattn_wq_b, L2_xattn_wk_k, L2_xattn_wk_b, L2_xattn_wv_k, L2_xattn_wv_b, L2_xattn_wo_k, L2_xattn_wo_b, L2_ffn_Win, L2_ffn_bin_, L2_ffn_W1, L2_ffn_b1, L2_ffn_W2, L2_ffn_b2, L2_ffn_Wout, L2_ffn_bout, L3_attn_W_attn, L3_attn_b_attn, L3_attn_W_proj, L3_attn_b_proj, L3_attn_temperature, L3_xattn_Wq, L3_xattn_bq, L3_xattn_Wk, L3_xattn_bk, L3_xattn_Wv, L3_xattn_bv, L3_xattn_Wo, L3_xattn_bo, L3_ffn_W1, L3_ffn_b1, L3_ffn_W2, L3_ffn_b2):
    import jax
    import jax.numpy as jnp

    def _L0_attn_ref(x, ln1_w, ln1_b, conv_w, conv_b, qk_w, v_w, g_w, g_b, o_w, onorm_w, onorm_b, gamma_attn, ln2_w, ln2_b, gate_w, up_w, down_w, gamma1, gamma2):
        import jax, jax.numpy as jnp
        import numpy as np
        B, T, D_MODEL = (2, 1024, 256)
        HD, H = (256, 16)
        HDIM = HD // H
        FF = 1024
        KS = 4

        def _ln(x, w, b, eps=1e-05):
            m = x.mean(-1, keepdims=True)
            v = ((x - m) ** 2).mean(-1, keepdims=True)
            return (x - m) / jnp.sqrt(v + eps) * w + b
        Bx, Tx, C = x.shape
        h = _ln(x, ln1_w, ln1_b)
        xc = jax.lax.conv_general_dilated(h.transpose(0, 2, 1), conv_w, (1,), [(KS - 1, 0)], dimension_numbers=('NCH', 'OIH', 'NCH'), feature_group_count=C)
        xc = (xc + conv_b[None, :, None]).transpose(0, 2, 1)
        qk = (xc @ qk_w.T).reshape(Bx, Tx, H, HDIM)
        k = qk / jnp.maximum(jnp.linalg.norm(qk, axis=-1, keepdims=True), 1e-12)
        q = k
        v = (xc @ v_w.T).reshape(Bx, Tx, H, HDIM)
        g = jax.nn.sigmoid(xc @ g_w.T + g_b).reshape(Bx, Tx, H, HDIM)
        t = jnp.arange(Tx, dtype=jnp.float32)[None, :, None, None]
        idx = jnp.linspace(0.0, 1.0, HDIM)
        freqs = (10.0 ** idx)[None, :] * jnp.arange(H, dtype=jnp.float32)[:, None]
        angles = t * freqs[None, None]
        rotors = jnp.cos(angles) + 1j * jnp.sin(angles)
        path_a = v * rotors
        k_shift = jnp.concatenate([jnp.zeros_like(k[:, :1]), k[:, :-1]], axis=1)
        path_b = v * k_shift
        state = (path_a + path_b) * g
        gamma = gamma_attn.reshape(1, 1, H, 1)
        decay = gamma ** t
        memory = jnp.cumsum(state * decay, axis=1) / (decay + 1e-06)
        out = jnp.real(memory * q).reshape(Bx, Tx, HD)
        attn_out = _ln(out @ o_w.T, onorm_w, onorm_b)
        x = x + gamma1 * attn_out
        h2 = _ln(x, ln2_w, ln2_b)
        mlp = jax.nn.silu(h2 @ gate_w.T) * (h2 @ up_w.T) @ down_w.T
        return x + gamma2 * mlp

    def _L0_xattn_ref(x, w1, w2):
        import jax, jax.numpy as jnp
        import numpy as np
        E, T, H, F = (8, 256, 256, 1024)
        h = jnp.einsum('eth,efh->etf', x, w1)
        g = jax.nn.gelu(h, approximate=True)
        out = jnp.einsum('etf,efh->eth', g, w2)
        return out

    def _L0_ffn_ref(feats, A, B, w_gate, wt_w, wt_b, wd_w, wd_b, scale):
        import jax, jax.numpy as jnp
        import numpy as np
        from jax import lax
        TOP_K = 1
        Bsz, N, C = feats.shape
        x = feats.reshape(-1, C)
        n = x.shape[0]
        logits = x @ w_gate
        top_vals, top_idx = lax.top_k(logits, TOP_K)
        top_g = jax.nn.softmax(top_vals, axis=-1)
        gates = jnp.zeros_like(logits).at[jnp.arange(n)[:, None], top_idx].set(top_g)
        tokens = jnp.einsum('elr,erc->elc', A, B)
        attn = jnp.einsum('nc,elc->nel', x, tokens) * C ** (-0.5)
        attn = jax.nn.softmax(attn, axis=-1)
        val = jnp.einsum('elc,dc->eld', tokens, wt_w) + wt_b
        delta_f = jnp.einsum('nel,eld->ned', attn[:, :, 1:], val[:, 1:, :])
        delta = (jnp.einsum('ned,cd->nec', delta_f + x[:, None, :], wd_w) + wd_b) * scale[0]
        combined = jnp.sum(jnp.exp(delta) * gates[:, :, None], axis=1)
        combined = jnp.where(combined == 0, jnp.finfo(jnp.float32).eps, combined)
        out = jnp.log(combined)
        return feats + out.reshape(Bsz, N, C)

    def _L1_attn_ref(x, time_mix_k, time_mix_v, time_mix_r, W_k, W_v, W_r, W_o, time_decay, time_first):
        import jax, jax.numpy as jnp
        import numpy as np
        B, T, D = (4, 1024, 256)
        NEG_CLAMP = -30.0
        EPS = 1e-09

        def _wkv_scan(k, v, w, u):
            Bn, Tn, Dn = k.shape
            p0 = jnp.full((Bn, Dn), -jnp.inf, k.dtype)
            q0 = jnp.zeros((Bn, Dn), k.dtype)

            def step(carry, kv_t):
                p, q = carry
                k_t, v_t = kv_t
                new_p = jnp.maximum(p, u + k_t)
                scale_old = jnp.exp(jnp.maximum(p - new_p, NEG_CLAMP))
                scale_cur = jnp.exp(jnp.maximum(u + k_t - new_p, NEG_CLAMP))
                wkv_t = (scale_old * q + scale_cur * v_t) / (scale_old + scale_cur + EPS)
                new_p2 = jnp.maximum(p + w, k_t)
                scale_prev = jnp.exp(jnp.maximum(p + w - new_p2, NEG_CLAMP))
                scale_new = jnp.exp(jnp.maximum(k_t - new_p2, NEG_CLAMP))
                q2 = scale_prev * q + scale_new * v_t
                return ((new_p2, q2), wkv_t)
            kT = jnp.swapaxes(k, 0, 1)
            vT = jnp.swapaxes(v, 0, 1)
            _, wkvT = jax.lax.scan(step, (p0, q0), (kT, vT))
            return jnp.swapaxes(wkvT, 0, 1)
        x_prev = jnp.pad(x[:, :-1, :], ((0, 0), (1, 0), (0, 0)))
        xk = x * time_mix_k + x_prev * (1.0 - time_mix_k)
        xv = x * time_mix_v + x_prev * (1.0 - time_mix_v)
        xr = x * time_mix_r + x_prev * (1.0 - time_mix_r)
        k = jnp.einsum('btd,ed->bte', xk, W_k)
        v = jnp.einsum('btd,ed->bte', xv, W_v)
        r = jax.nn.sigmoid(jnp.einsum('btd,ed->bte', xr, W_r))
        wkv = _wkv_scan(k, v, time_decay, time_first)
        y = r * wkv
        return jnp.einsum('btd,ed->bte', y, W_o)

    def _L1_xattn_ref(context, mem0, W0, W1, mask):
        import jax, jax.numpy as jnp
        import numpy as np
        B, L, P, D = (32, 512, 64, 256)
        MAX_HOP = 2
        m = (mask == 0)[:, None, :]
        neg_inf = jnp.finfo(context.dtype).min
        u = mem0
        for W in (W0, W1):
            key_ = jnp.einsum('bpd,md->bpm', u, W)
            attn = jnp.einsum('bpm,blm->bpl', key_, context)
            attn = jnp.where(m, neg_inf, attn)
            w = jax.nn.softmax(attn, axis=-1)
            o = jnp.einsum('bpl,bld->bpd', w, context)
            u = u + o
        return u

    def _L1_ffn_ref(x, w1, b1, w2, b2):
        import jax, jax.numpy as jnp
        import numpy as np
        QP = 127.0
        MIN_RANGE = 1e-06

        def _ste_round(x):
            return x + jax.lax.stop_gradient(jnp.round(x) - x)

        def _quant_per_tensor(x):
            scale = jnp.maximum(jnp.max(jnp.abs(x)), MIN_RANGE) / QP
            return (_ste_round(x / scale), scale)

        def _qlinear(x2d, w, b):
            xq, sx = _quant_per_tensor(x2d)
            wq, sw = _quant_per_tensor(w)
            out = jnp.matmul(xq, wq.T) + b[None, :]
            return out * (sw * sx)
        B, N, D = x.shape
        h = _qlinear(x.reshape(-1, D), w1, b1)
        h = jax.nn.gelu(h, approximate=False)
        o = _qlinear(h, w2, b2)
        return o.reshape(B, N, -1)

    def _L2_attn_ref(x, w_qkv, w_proj, b_proj):
        import jax, jax.numpy as jnp
        import numpy as np
        CLIP_VAL = 8
        FRACTION_BITS = 12
        SCALE = float(2 ** FRACTION_BITS)
        EPS = 1.0 / SCALE
        HEADS = 16
        DIM_HEAD = 64

        def make_fxp(x):
            c = CLIP_VAL - EPS
            x = jnp.clip(x, -c, c)
            return jnp.trunc(x * SCALE) / SCALE
        B, N, D = x.shape
        h, d = (HEADS, DIM_HEAD)
        scale = d ** (-0.5)
        qkv = jnp.einsum('bnd,ed->bne', x, w_qkv)
        q, k, v = jnp.split(qkv, 3, axis=-1)
        tohd = lambda t: t.reshape(B, N, h, d).transpose(0, 2, 1, 3)
        q, k, v = (make_fxp(tohd(q)), make_fxp(tohd(k)), make_fxp(tohd(v)))
        dots = make_fxp(jnp.einsum('bhnd,bhmd->bhnm', q, k) * scale)
        attn = make_fxp(jax.nn.softmax(dots, axis=-1))
        attn = make_fxp(attn)
        out = make_fxp(jnp.einsum('bhnm,bhmd->bhnd', attn, v))
        out = out.transpose(0, 2, 1, 3).reshape(B, N, h * d)
        out = make_fxp(jnp.einsum('bne,de->bnd', out, w_proj) + b_proj)
        out = make_fxp(out)
        return out

    def _L2_xattn_ref(query, key_in, value, group_prob, mask, wq_k, wq_b, wk_k, wk_b, wv_k, wv_b, wo_k, wo_b):
        import jax, jax.numpy as jnp
        import numpy as np
        NUM_HEADS = 16
        HIDDEN = 256
        B, S = (2, 512)

        def _split_heads(x, H):
            b, s, d = x.shape
            return x.reshape(b, s, H, d // H).transpose(0, 2, 1, 3)
        H = NUM_HEADS
        dh = query.shape[-1] // H
        q = _split_heads(query @ wq_k + wq_b, H)
        k = _split_heads(key_in @ wk_k + wk_b, H)
        v = _split_heads(value @ wv_k + wv_b, H)
        logits = jnp.einsum('bhqd,bhkd->bhqk', q, k) / jnp.sqrt(jnp.asarray(dh, q.dtype))
        neg = (1.0 - mask.astype(q.dtype)) * -1000000000.0
        logits = logits + neg[:, None, :, :]
        attn = jax.nn.softmax(logits, axis=-1)
        attn = attn * group_prob[:, None, :, :]
        out = jnp.einsum('bhqk,bhkd->bhqd', attn, v)
        out = out.transpose(0, 2, 1, 3).reshape(query.shape[0], -1, H * dh)
        return out @ wo_k + wo_b

    def _L2_ffn_ref(x, Win, bin_, W1, b1, W2, b2, Wout, bout):
        import jax, jax.numpy as jnp
        import numpy as np
        D_MODEL = 256
        M = 64
        INNER = 16
        s = jnp.einsum('btd,dm->btm', x, Win) + bin_
        h = jax.nn.relu(s[..., None] * W1 + b1)
        g = jnp.einsum('btmh,mh->btm', h, W2) + b2
        out = jnp.einsum('btm,md->btd', g, Wout) + bout
        return out

    def _L3_attn_ref(x, W_attn, b_attn, W_proj, b_proj, temperature):
        import jax, jax.numpy as jnp
        import numpy as np
        import math
        B, T, C = (2, 512, 256)
        H = 16
        D = C // H

        def alibi_slopes(n_heads):
            start = 2.0 ** (-2.0 ** (-(math.log2(n_heads) - 3)))
            return jnp.asarray([start * start ** i for i in range(n_heads)], dtype=jnp.float32)
        Bc, Tc, Cc = x.shape
        qkv = x @ W_attn + b_attn
        q, k, v = jnp.split(qkv, 3, axis=-1)
        q = q.reshape(Bc, Tc, H, D)
        k = k.reshape(Bc, Tc, H, D)
        v = v.reshape(Bc, Tc, H, D)
        scale = 1.0 / math.sqrt(D)
        att = jnp.einsum('bqhd,bkhd->bhqk', q, k) * scale
        att = att / temperature
        pos = jnp.arange(Tc, dtype=jnp.float32)
        rel = pos[None, :] - pos[:, None]
        slopes = alibi_slopes(H)
        bias = slopes[:, None, None] * rel[None, :, :]
        causal = pos[None, :] <= pos[:, None]
        bias = jnp.where(causal[None, :, :], bias, -jnp.inf)
        att = att + bias[None, :, :, :]
        w = jax.nn.softmax(att, axis=-1)
        y = jnp.einsum('bhqk,bkhd->bqhd', w, v).reshape(Bc, Tc, Cc)
        return y @ W_proj + b_proj

    def _L3_xattn_ref(queries, keys, values, Wq, bq, Wk, bk, Wv, bv, Wo, bo):
        import jax, jax.numpy as jnp
        import numpy as np
        B, S, D = (1, 1024, 256)
        H, DK, DV = (16, 64, 64)
        b, sq, _ = queries.shape
        sk = keys.shape[1]
        q = (queries @ Wq.T + bq).reshape(b, sq, H, DK).transpose(0, 2, 1, 3)
        k = (keys @ Wk.T + bk).reshape(b, sk, H, DK).transpose(0, 2, 1, 3)
        v = (values @ Wv.T + bv).reshape(b, sk, H, DV).transpose(0, 2, 1, 3)
        scores = jnp.einsum('bhqd,bhkd->bhqk', q, k) / jnp.sqrt(jnp.float32(DK))
        causal = jnp.triu(jnp.ones((sq, sk), bool), k=1)
        scores = jnp.where(causal, jnp.float32(-jnp.inf), scores)
        attn = jax.nn.softmax(scores, axis=-1)
        out = jnp.einsum('bhqk,bhkd->bhqd', attn, v)
        out = out.transpose(0, 2, 1, 3).reshape(b, sq, H * DV)
        return out @ Wo.T + bo

    def _L3_ffn_ref(x, W1, b1, W2, b2):
        import jax, jax.numpy as jnp
        import numpy as np
        EMB = 256
        FF = 4 * EMB

        def _ternary(w):
            scale = jnp.maximum(jnp.mean(jnp.abs(w)), 1e-08)
            w_t = jnp.clip(jnp.round(w / scale), -1.0, 1.0)
            return w + jax.lax.stop_gradient(w_t - w)
        h = jnp.einsum('bsd,fd->bsf', x, _ternary(W1)) + b1
        h = jax.nn.gelu(h, approximate=False)
        out = jnp.einsum('bsf,df->bsd', h, _ternary(W2)) + b2
        return out
    x = x + _L0_attn_ref(_layernorm(x, axis=-1), L0_attn_ln1_w, L0_attn_ln1_b, L0_attn_conv_w, L0_attn_conv_b, L0_attn_qk_w, L0_attn_v_w, L0_attn_g_w, L0_attn_g_b, L0_attn_o_w, L0_attn_onorm_w, L0_attn_onorm_b, L0_attn_gamma_attn, L0_attn_ln2_w, L0_attn_ln2_b, L0_attn_gate_w, L0_attn_up_w, L0_attn_down_w, L0_attn_gamma1, L0_attn_gamma2)
    x = x + _L0_xattn_ref(_layernorm(x, axis=-1), ctx_1024, ctx_1024)
    x = x + _L0_ffn_ref(_layernorm(x, axis=-1), L0_ffn_A, L0_ffn_B, L0_ffn_w_gate, L0_ffn_wt_w, L0_ffn_wt_b, L0_ffn_wd_w, L0_ffn_wd_b, L0_ffn_scale)
    x = x + _L1_attn_ref(_layernorm(x, axis=-1), L1_attn_time_mix_k, L1_attn_time_mix_v, L1_attn_time_mix_r, L1_attn_W_k, L1_attn_W_v, L1_attn_W_r, L1_attn_W_o, L1_attn_time_decay, L1_attn_time_first)
    x = x + _L1_xattn_ref(ctx_1024, _layernorm(x, axis=-1), L1_xattn_W0, L1_xattn_W1, mask_BxS2_if1)
    x = x + _L1_ffn_ref(_layernorm(x, axis=-1), L1_ffn_w1, L1_ffn_b1, L1_ffn_w2, L1_ffn_b2)
    x = x + _L2_attn_ref(_layernorm(x, axis=-1), L2_attn_w_qkv, L2_attn_w_proj, L2_attn_b_proj)
    x = x + _L2_xattn_ref(_layernorm(x, axis=-1), ctx_1024, ctx_1024, fside_BxSxS2_0, mask_BxSxS2_ik1, L2_xattn_wq_k, L2_xattn_wq_b, L2_xattn_wk_k, L2_xattn_wk_b, L2_xattn_wv_k, L2_xattn_wv_b, L2_xattn_wo_k, L2_xattn_wo_b)
    x = x + _L2_ffn_ref(_layernorm(x, axis=-1), L2_ffn_Win, L2_ffn_bin_, L2_ffn_W1, L2_ffn_b1, L2_ffn_W2, L2_ffn_b2, L2_ffn_Wout, L2_ffn_bout)
    x = x + _L3_attn_ref(_layernorm(x, axis=-1), L3_attn_W_attn, L3_attn_b_attn, L3_attn_W_proj, L3_attn_b_proj, L3_attn_temperature)
    x = x + _L3_xattn_ref(_layernorm(x, axis=-1), ctx_1024, ctx_1024, L3_xattn_Wq, L3_xattn_bq, L3_xattn_Wk, L3_xattn_bk, L3_xattn_Wv, L3_xattn_bv, L3_xattn_Wo, L3_xattn_bo)
    x = x + _L3_ffn_ref(_layernorm(x, axis=-1), L3_ffn_W1, L3_ffn_b1, L3_ffn_W2, L3_ffn_b2)
    return x

_drawn_inputs = setup_inputs


def setup_inputs(seed=0):
    import zlib

    import numpy as np

    out = dict(_drawn_inputs(seed))
    spreads = {'L0_attn_ln1_w': (1.0, 0.2),
     'L0_attn_ln1_b': (0.0, 0.1),
     'L0_attn_conv_b': (0.0, 0.1),
     'L0_attn_g_b': (2.0, 0.2),
     'L0_attn_onorm_w': (1.0, 0.2),
     'L0_attn_onorm_b': (0.0, 0.1),
     'L0_attn_ln2_w': (1.0, 0.2),
     'L0_attn_ln2_b': (0.0, 0.1),
     'L0_attn_gamma1': (0.10000000149011612, 0.2),
     'L0_attn_gamma2': (0.10000000149011612, 0.2),
     'L2_xattn_wq_b': (0.0, 0.1),
     'L2_xattn_wk_b': (0.0, 0.1),
     'L2_xattn_wv_b': (0.0, 0.1),
     'L2_xattn_wo_b': (0.0, 0.1),
     'L3_attn_b_attn': (0.0, 0.1),
     'L3_attn_b_proj': (0.0, 0.1),
     'L3_xattn_bq': (0.0, 0.1),
     'L3_xattn_bk': (0.0, 0.1),
     'L3_xattn_bv': (0.0, 0.1),
     'L3_xattn_bo': (0.0, 0.1)}
    factors = {}
    for name, (base, spread) in spreads.items():
        noise = np.random.default_rng([zlib.crc32(name.encode()), seed]).standard_normal(out[name].shape)
        drawn = base * np.exp(spread * noise) if base else spread * noise
        out[name] = jnp.asarray(drawn.astype(out[name].dtype))
    for name, factor in factors.items():
        out[name] = (out[name] * factor).astype(out[name].dtype)
    return out
```

```python
from contextlib import ExitStack, contextmanager

import concourse.bass as bass
import concourse.mybir as mybir
import numpy as np
from concourse.alu_op_type import AluOpType as OP

ACT = mybir.ActivationFunctionType
AX = mybir.AxisListType
F32 = mybir.dt.float32
BF16 = mybir.dt.bfloat16
I32 = mybir.dt.int32

B, S, D, S2 = 2, 512, 256, 1024
NT = B * S
P = 128
DC = D // P
FF = 1024
FC = FF // P
H = 16
E_, L_, R_ = 6, 100, 16
LN_EPS = 1e-5
BIG = 1e30
FMIN = float(np.finfo(np.float32).min)
ROUND = 12582912.0
FX = 4096.0
FXMAX = 8 * FX - 1
HALF = 0.49998

VEC256 = ["L0_attn_ln1_w", "L0_attn_ln1_b", "L0_attn_conv_b", "L0_attn_g_b", "L0_attn_onorm_w",
          "L0_attn_onorm_b", "L0_attn_ln2_w", "L0_attn_ln2_b", "L0_attn_gamma1", "L0_attn_gamma2",
          "cw0", "cw1", "cw2", "cw3", "gamma", "L0_ffn_wd_b",
          "L1_attn_time_mix_k", "L1_attn_time_mix_v", "L1_attn_time_mix_r", "L1_attn_time_decay",
          "L1_attn_time_first", "L1_ffn_b2", "L2_attn_b_proj", "L2_xattn_wo_b", "L2_ffn_bout",
          "L3_attn_b_proj", "L3_xattn_bo", "L3_ffn_b2"]
VEC1024 = ["L1_ffn_b1", "L2_ffn_b1", "L3_ffn_b1"]
VCOL, _n = {}, 0
for _v in VEC256:
    VCOL[_v] = _n
    _n += 2
for _v in VEC1024:
    VCOL[_v] = _n
    _n += 8
for _v in ("L2_ffn_bin_", "L2_ffn_b2", "L0_ffn_scale", "L3_attn_temperature"):
    VCOL[_v] = _n
    _n += 1
NVEC = _n

MHA = {
    "L2_attn": dict(groups=8, heads=2, rows=64, dh=64, keys=S, causal=False, kind="fixed"),
    "L2_xattn": dict(groups=4, heads=4, rows=32, dh=16, keys=S2, causal=False, kind="grouped"),
    "L3_attn": dict(groups=4, heads=4, rows=32, dh=16, keys=S, causal=True, kind="alibi"),
    "L3_xattn": dict(groups=8, heads=2, rows=64, dh=64, keys=S, causal=True, kind="causal"),
}


class Tok:

    def __init__(self, ch, n):
        self.ch, self.n = ch, n


class Chan:

    def __init__(self, nc, ctx, name, step=1):
        self.sem, self.step, self.n, self.name = ctx.enter_context(nc.semaphore(name)), step, 0, name


class Prog:

    def __init__(self, nc, ctx, aps):
        self.nc, self.ctx, self.a = nc, ctx, aps
        self.pe, self.dve, self.act, self.pool, self.sp = nc.tensor, nc.vector, nc.scalar, nc.gpsimd, nc.sync
        self.c = {n: Chan(nc, ctx, "s_" + n) for n in ("pe", "dve", "act", "pool")}
        self.inner = {n: Chan(nc, ctx, "l_" + n) for n in ("pe", "dve", "act", "pool")}
        self.d_st = Chan(nc, ctx, "l_dma", 16)
        self.d_st2 = Chan(nc, ctx, "l_dma_2", 16)
        self.waited = {}

    def mark(self, eng, ins):
        ch = self.c[eng]
        ins.then_inc(ch.sem, 1)
        ch.n += 1
        return Tok(ch, ch.n)

    def E(self, ins):
        return self.mark("pe", ins)

    def V(self, ins):
        return self.mark("dve", ins)

    def A(self, ins):
        return self.mark("act", ins)

    def G(self, ins):
        return self.mark("pool", ins)

    def dma_chan(self, name):
        return Chan(self.nc, self.ctx, "d_" + name, 16)

    def dma(self, ch, out, in_, eng=None):
        (eng or self.sp).dma_start(out, in_).then_inc(ch.sem, 16)
        ch.n += 16
        return Tok(ch, ch.n)

    def W(self, eng, *toks):
        todo = list(toks)
        last = {}
        while todo:
            t = todo.pop()
            if isinstance(t, (list, tuple)):
                todo += t
            elif t is not None and t.n > last.get(t.ch.name, (0,))[0]:
                last[t.ch.name] = t.n, t.ch
        for name, (n, ch) in last.items():
            if n > self.waited.get((id(eng), name), 0):
                self.waited[id(eng), name] = n
                eng.wait_ge(ch.sem, n)

    def now(self, *names):
        return [Tok(self.c[n], self.c[n].n) for n in names if self.c[n].n]

    def meet(self, *dma):
        toks = self.now("pe", "dve", "act", "pool")
        for eng in (self.pe, self.dve, self.act, self.pool, self.sp):
            self.W(eng, toks, *dma)

    @contextmanager
    def fori(self, trips):
        self.meet()
        outer, outer_waited, self.c = self.c, self.waited, self.inner
        with self.nc.Fori(0, trips) as i:
            self.waited = {}
            every = list(self.inner.values()) + [self.d_st, self.d_st2]
            for ch in every:
                ch.n = 0
            yield i
            self.meet()
            self.nc.all_engine_barrier(sems_to_clear=range(every[0].sem.num, every[-1].sem.num + 1))
        self.c, self.waited = outer, outer_waited
        self.ring = [None] * 4


def view(t, off, *dims):
    n = int(np.prod(dims))
    ap = t[:, off:off + n]
    if len(dims) == 1:
        return ap
    names = "abcd"[:len(dims)]
    pat = "p (" + " ".join(names) + ") -> p " + " ".join(names)
    return ap.rearrange(pat, **{k: v for k, v in zip(names[1:], dims[1:])})


def decoder(nc, a, stages):
    ctx = ExitStack()
    with ctx:
        def sb(name, cols, dt=F32):
            return ctx.enter_context(nc.sbuf_tensor(name, [P, cols], dt))

        g = Prog(nc, ctx, a)
        g.X = view(sb("resid", DC * NT), 0, DC, NT)
        g.Hn = view(sb("normed", DC * NT), 0, DC, NT)
        g.ctxK = view(sb("ctx_keys", 16 * D), 0, 16, D)
        g.ctxT = view(sb("ctx_feat", DC * B * S2), 0, DC, B * S2)
        g.WA = sb("arena_a", 8192)
        g.WB = sb("arena_b", 8192)
        g.work = sb("work", 19 * 1024)
        g.wst = sb("head_weights", 3 * DC * P + P + 8)
        g.wst2 = sb("head_weights_2", 3 * DC * P)
        g.extra = sb("extra", 2048)
        g.vec = sb("vecs", NVEC)
        g.one = sb("mean_matrix", P)
        g.ones = sb("ones_matrix", P)
        g.iden = sb("identity", P)
        g.small = sb("small", 256)
        g.ps = ctx.enter_context(nc.psum_tensor("ps", [P, 4096], F32))
        g.ring = [None] * 4
        g.ring_i = 0

        g.d_in = g.dma_chan("in")
        g.d_ctx = g.dma_chan("ctx")
        g.d_w = g.dma_chan("w")
        g.d_w2 = g.dma_chan("w2")
        g.d_out = g.dma_chan("out")

        g.dma(g.d_in, g.vec[:, :], a["vecs"])
        g.dma(g.d_in, g.iden[:, :], a["ident"])
        t_in = g.dma(g.d_in, g.X, a["xT"].rearrange("(c p) t -> p c t", p=P))
        g.dma(g.d_ctx, g.ctxK, a["ctx_keys"].rearrange("(k p) d -> p k d", p=P), nc.scalar)
        g.t_ctx = g.dma(g.d_ctx, g.ctxT, a["ctxT"].rearrange("(c p) t -> p c t", p=P), nc.scalar)
        g.V(nc.vector.memset(g.one[:, :], 1.0 / D))
        g.V(nc.vector.memset(g.ones[:, :], 1.0))
        const = sb("constants", 3)
        g.eps, g.ln15, g.e9 = (const[:, j:j + 1] for j in range(3))
        for ap, value in ((g.eps, LN_EPS), (g.ln15, 15 * float(np.log(2.0))), (g.e9, 1e-9)):
            g.V(nc.vector.memset(ap, value))
        g.meet(t_in, g.t_ctx)
        g.resid = [t_in, t_in]

        for s in stages:
            STAGES[s](g)
            g.meet()
            g.ring = [None] * 4

        t_out = g.dma(g.d_out, a["out"].rearrange("(c p) t -> p c t", p=P), g.X)
        g.W(nc.sync, t_out)



def vcol(g, name, c=0):
    return g.vec[:, VCOL[name] + c:VCOL[name] + c + 1]


def slot(g):
    i = g.ring_i
    g.ring_i = (i + 1) % 4
    g.W(g.pe, g.ring[i])
    return i, g.ps[:, i * 1024:(i + 1) * 1024]


def half(n):
    return slice(n * S, (n + 1) * S)


def layernorm(g, src, dst, ready, sq, tmp, w=None, b=None, put=None):
    one = g.one[:, :]
    im, mean = slot(g)
    iv, var = slot(g)
    t1 = []
    for n in range(B):
        g.W(g.pe, ready[n])
        for c in range(DC):
            mm = g.pe.matmul(mean[:, half(n)], one, src[:, c, half(n)], start=c == 0, stop=c == DC - 1)
        t1.append(g.E(mm))
    t2 = []
    for n in range(B):
        g.W(g.dve, t1[n], ready[n])
        for c in range(DC):
            t = g.V(g.dve.tensor_tensor(dst[:, c, half(n)], src[:, c, half(n)], mean[:, half(n)], OP.subtract))
        t2.append(t)
    g.ring[im] = t2[-1]
    t3 = []
    for n in range(B):
        g.W(g.act, t2[n])
        t3.append(g.A(g.act.activation(sq[:, :, half(n)], dst[:, :, half(n)], ACT.Square)))
    t4 = []
    for n in range(B):
        g.W(g.pe, t3[n])
        for c in range(DC):
            mm = g.pe.matmul(var[:, half(n)], one, sq[:, c, half(n)], start=c == 0, stop=c == DC - 1)
        t4.append(g.E(mm))
    t6 = []
    for n in range(B):
        g.W(g.act, t4[n])
        t5 = g.A(g.act.activation(tmp[:, half(n)], var[:, half(n)], ACT.Ln, bias=g.eps))
        g.W(g.act, t5)
        t6.append(g.A(g.act.activation(tmp[:, half(n)], tmp[:, half(n)], ACT.Exp, scale=-0.5)))
    g.ring[iv] = t6[-1]
    out = []
    for n in range(B):
        g.W(g.dve, t6[n])
        for c in range(DC):
            last = w is None
            o = put(c, n) if last and put is not None else dst[:, c, half(n)]
            t = g.V(g.dve.tensor_tensor(o, dst[:, c, half(n)], tmp[:, half(n)], OP.mult))
            if not last:
                g.W(g.dve, t)
                o = put(c, n) if put is not None else dst[:, c, half(n)]
                t = g.V(g.dve.tensor_scalar(o, dst[:, c, half(n)], vcol(g, w, c), vcol(g, b, c), OP.mult, OP.add))
        out.append(t)
    return tuple(out)


def project(g, wT, src, kts, mts, evac, ready, src_ap=None):
    out = []
    for m in range(mts):
        i, ps = slot(g)
        for n in range(B):
            g.W(g.pe, ready[n] if isinstance(ready, tuple) else ready)
            for k in range(kts):
                rhs = src_ap(k, n) if src_ap else src[:, k, half(n)]
                mm = g.pe.matmul(ps[:, half(n)], wT[:, k, m * P:(m + 1) * P], rhs, start=k == 0, stop=k == kts - 1)
        t = g.E(mm)
        g.ring[i] = evac(m, ps, t)
        out.append(g.ring[i])
    return out


def add_resid(g, bias=None, scale=None):
    toks = []

    def evac(m, ps, t):
        g.W(g.dve, t)
        if bias is None:
            t = g.V(g.dve.tensor_tensor(g.X[:, m, :], ps, g.X[:, m, :], OP.add))
        else:
            t = g.V(g.dve.scalar_tensor_tensor(out=g.X[:, m, :], in0=ps, scalar=vcol(g, bias, m),
                                               in1=g.X[:, m, :], op0=OP.add, op1=OP.add))
        g.resid = [t, t]
        return t
    return evac


def load(g, ch, dst, src, *after):
    g.W(g.sp, *after)
    return g.dma(ch, dst, src)



def l0_attn(g):
    a = g.a
    A, Bt, w = g.WA, g.WB, g.work
    tw = load(g, g.d_w, A[:, :], a["w_l0_attn"])
    W = {n: view(A, i * 512, 2, 256) for i, n in enumerate(("qk", "v", "g", "o"))}
    Wg, Wu, Wd = view(A, 2048, 2, FF), view(A, 4096, 2, FF), view(A, 6144, FC, D)
    cosT = view(Bt, 0, 2, S)
    tcos = load(g, g.d_w2, cosT, a["cos"].rearrange("(c p) t -> p c t", p=P))
    blk = view(Bt, 1024, P)
    tcos = load(g, g.d_w2, blk, a["blockdiag"])
    K = 1024
    tmp, sq = view(w, 0, NT), view(w, K, 2, NT)
    hin = view(w, 3 * K, 2, NT)
    hpad = view(Bt, 2048, 2, B, S + 3)
    xc = view(w, 5 * K, 2, B, S)
    kk, v, gate = view(w, 7 * K, 2, NT), view(w, 9 * K, 2, NT), view(w, 11 * K, 2, NT)
    dec, rdec = view(w, 13 * K, 2, S), view(w, 14 * K, 2, S)
    ones, gam = view(w, 15 * K, S), view(w, 15 * K + S, S)
    cs = view(w, 16 * K, 2, B, S)

    t1 = layernorm(g, g.X, hin, g.resid, sq, tmp)
    z = g.G(g.pool.memset(hpad[:, :, :, 0:3], 0.0))
    t2 = layernorm(g, hin, g.Hn, t1, sq, tmp, "L0_attn_ln1_w", "L0_attn_ln1_b",
                   put=lambda c, n: hpad[:, c, n, 3:])
    g.W(g.dve, z)
    tx = []
    for c in range(DC):
        g.W(g.dve, t2)
        t = g.V(g.dve.tensor_scalar(xc[:, c], hpad[:, c, :, 0:S], vcol(g, "cw0", c), vcol(g, "L0_attn_conv_b", c),
                                    OP.mult, OP.add))
        for j in range(1, 4):
            g.W(g.dve, t)
            t = g.V(g.dve.scalar_tensor_tensor(out=xc[:, c], in0=hpad[:, c, :, j:j + S], scalar=vcol(g, f"cw{j}", c),
                                               in1=xc[:, c], op0=OP.mult, op1=OP.add))
        tx.append(t)
    t = g.V(g.dve.memset(ones, 1.0))
    g.W(g.dve, t)
    td = []
    for c in range(DC):
        t = g.V(g.dve.tensor_scalar(gam, ones, vcol(g, "gamma", c), None, OP.mult))
        m = g.V(g.dve.memset(dec[:, c, 0:1], 1.0))
        g.W(g.dve, t, m)
        t = g.V(g.dve.tensor_tensor_scan(dec[:, c, 1:S], gam[:, 1:S], ones[:, 1:S], 1.0, OP.mult, OP.mult))
        g.W(g.dve, t)
        td.append(t)
    t = g.V(g.dve.tensor_scalar(rdec, dec, 1e-6, None, OP.add))
    g.W(g.dve, t)
    trd = g.V(g.dve.reciprocal(rdec, rdec))
    xcf = xc.rearrange("p c b s -> p c (b s)")
    g.W(g.pe, tw, tcos)

    def ev_qk(m, ps, t):
        g.W(g.act, t)
        g.A(g.act.activation(kk[:, m, :], ps, ACT.Copy))
        return g.A(g.act.activation(sq[:, m, :], ps, ACT.Square))
    tq = project(g, W["qk"], xcf, DC, DC, ev_qk, tx[-1])

    def ev_v(m, ps, t):
        g.W(g.act, t)
        return g.A(g.act.activation(v[:, m, :], ps, ACT.Copy))
    tv = project(g, W["v"], xcf, DC, DC, ev_v, tx[-1])
    for m in range(DC):
        i, ps = slot(g)
        g.W(g.pe, tq[m])
        for n in range(B):
            mm = g.pe.matmul(ps[:, half(n)], blk, sq[:, m, half(n)], start=True, stop=True)
        t = g.E(mm)
        g.W(g.dve, t)
        t = g.V(g.dve.tensor_scalar(tmp, ps, 1e-24, None, OP.max))
        g.ring[i] = t
        g.W(g.act, t)
        t = g.A(g.act.activation(tmp, tmp, ACT.Ln, scale=2.0 ** 30))
        g.W(g.act, t)
        t = g.A(g.act.activation(tmp, tmp, ACT.Exp, scale=-0.5, bias=g.ln15))
        g.W(g.dve, t)
        tk = g.V(g.dve.tensor_tensor(kk[:, m, :], kk[:, m, :], tmp, OP.mult))
        g.W(g.dve, tk)

    def ev_g(m, ps, t):
        g.W(g.act, t)
        return g.A(g.act.activation(gate[:, m, :], ps, ACT.Sigmoid, bias=vcol(g, "L0_attn_g_b", m)))
    tg = project(g, W["g"], xcf, DC, DC, ev_g, tx[-1])
    g.W(g.dve, tcos, tv, tk)
    kb = kk.rearrange("p c (b s) -> p c b s", b=B)
    for c in range(DC):
        for b in range(B):
            g.V(g.dve.tensor_tensor(cs[:, c, b, 1:S], cosT[:, c, 1:S], kb[:, c, b, 0:S - 1], OP.add))
            t = g.V(g.dve.tensor_copy(cs[:, c, b, 0:1], cosT[:, c, 0:1]))
    g.W(g.dve, t)
    csf = cs.rearrange("p c b s -> p c (b s)")
    t = g.V(g.dve.tensor_tensor(csf, csf, v, OP.mult))
    g.W(g.dve, t, tg)
    t = g.V(g.dve.tensor_tensor(csf, csf, gate, OP.mult))
    g.W(g.dve, t)
    for c in range(DC):
        for b in range(B):
            t = g.V(g.dve.tensor_tensor(cs[:, c, b], cs[:, c, b], dec[:, c], OP.mult))
            g.W(g.dve, t)
            t = g.V(g.dve.tensor_tensor_scan(gate[:, c, half(b)], ones, cs[:, c, b], 0.0, OP.mult, OP.add))
            g.W(g.dve, t, trd)
            t = g.V(g.dve.tensor_tensor(gate[:, c, half(b)], gate[:, c, half(b)], rdec[:, c], OP.mult))
            g.W(g.dve, t)
            t = g.V(g.dve.tensor_tensor(gate[:, c, half(b)], gate[:, c, half(b)], kk[:, c, half(b)], OP.mult))
    ao = v

    def ev_o(m, ps, t):
        g.W(g.act, t)
        return g.A(g.act.activation(ao[:, m, :], ps, ACT.Copy))
    to = project(g, W["o"], gate, DC, DC, ev_o, t)
    tn = layernorm(g, ao, g.Hn, [to[-1]] * 2, sq, tmp, "L0_attn_onorm_w", "L0_attn_onorm_b")
    x2 = hin
    g.W(g.dve, tn)
    for c in range(DC):
        t = g.V(g.dve.scalar_tensor_tensor(out=x2[:, c, :], in0=g.Hn[:, c, :], scalar=vcol(g, "L0_attn_gamma1", c),
                                           in1=x2[:, c, :], op0=OP.mult, op1=OP.add))
    h2 = view(w, 5 * K, 2, NT)
    tn = layernorm(g, x2, h2, [t, t], sq, tmp, "L0_attn_ln2_w", "L0_attn_ln2_b")
    hid = view(w, 7 * K, FC, NT)
    sil = [view(w, 15 * K, NT), view(w, 16 * K, NT)]
    ts = [None, None]
    th = None
    for m in range(FC):
        def ev_gate(_, ps, t):
            g.W(g.act, t, ts[m % 2])
            g.tsil = g.A(g.act.activation(sil[m % 2], ps, ACT.Silu))
            return g.tsil

        def ev_up(_, ps, t):
            g.W(g.dve, t, g.tsil)
            ts[m % 2] = g.V(g.dve.tensor_tensor(hid[:, m, :], ps, sil[m % 2], OP.mult))
            return ts[m % 2]
        project(g, Wg[:, :, m * P:(m + 1) * P], h2, DC, 1, ev_gate, tn)
        th = project(g, Wu[:, :, m * P:(m + 1) * P], h2, DC, 1, ev_up, tn)[0]

    def ev_d(m, ps, t):
        g.W(g.dve, t)
        t = g.V(g.dve.scalar_tensor_tensor(out=x2[:, m, :], in0=ps, scalar=vcol(g, "L0_attn_gamma2", m),
                                           in1=x2[:, m, :], op0=OP.mult, op1=OP.add))
        g.W(g.dve, t)
        t2 = g.V(g.dve.tensor_tensor(g.X[:, m, :], g.X[:, m, :], x2[:, m, :], OP.add))
        g.resid = [t2, t2]
        return t
    project(g, Wd, hid, FC, DC, ev_d, th)


def l0_xattn(g):
    w, K = g.work, 1024
    sq, tmp = view(w, 0, 2, NT), view(w, 2 * K, NT)
    hid = [view(w, (3 + 4 * b) * K, 8, S) for b in range(B)]
    t1 = layernorm(g, g.X, g.Hn, g.resid, sq, tmp)
    for b in range(B):
        for k2 in range(4):
            i, ps = slot(g)
            g.W(g.pe, t1[b])
            for j in range(2):
                kt = 2 * k2 + j
                for c in range(DC):
                    mm = g.pe.matmul(ps[:, half(j)], g.ctxT[:, c, b * S2 + kt * P:b * S2 + (kt + 1) * P],
                                     g.Hn[:, c, half(b)], start=c == 0, stop=c == DC - 1)
            t = g.E(mm)
            g.W(g.act, t)
            g.ring[i] = g.A(g.act.activation(hid[b][:, 2 * k2:2 * k2 + 2, :],
                                             ps.rearrange("p (a s) -> p a s", a=2), ACT.Gelu_apprx_tanh))
    for b in range(B):
        i, ps = slot(g)
        g.W(g.pe, g.now("act"))
        for m in range(DC):
            for kt in range(8):
                mm = g.pe.matmul(ps[:, half(m)], g.ctxK[:, b * 8 + kt, m * P:(m + 1) * P], hid[b][:, kt, :],
                                 start=kt == 0, stop=kt == 7)
        t = g.E(mm)
        g.W(g.dve, t)
        t = g.V(g.dve.tensor_tensor(g.X[:, :, half(b)], ps.rearrange("p (c s) -> p c s", c=2),
                                    g.X[:, :, half(b)], OP.add))
        g.ring[i] = t
        g.resid[b] = t


def l0_ffn(g):
    a, w, K = g.a, g.work, 1024
    Bt = g.WB
    n = E_ * L_
    AT, Bm = view(Bt, 0, n), view(Bt, 600, E_, D)
    tokg = view(Bt, 2200, 2, n + E_)
    WT, WD = view(Bt, 3500, 2, D), view(Bt, 4100, 2, D)
    wtb = view(Bt, 4700, D)
    rank = view(Bt, 5000, E_)
    val = view(Bt, 5100, E_, D)
    tw = load(g, g.d_w, AT[0:R_, :], a["l0f_AT"])
    load(g, g.d_w, Bm[0:R_], a["l0f_B"])
    load(g, g.d_w, tokg[:, :, n:n + E_], a["l0f_gate"])
    load(g, g.d_w, WT, a["l0f_wt"])
    load(g, g.d_w, WD, a["l0f_wd"])
    load(g, g.d_w, rank, a["rank"])
    tw = load(g, g.d_w, wtb, a["l0f_wtb"].partition_broadcast(P))
    sq, tmp = view(w, 0, 2, NT), view(w, 2 * K, NT)
    t1 = layernorm(g, g.X, g.Hn, g.resid, sq, tmp)
    g.W(g.pe, tw)
    for c in range(DC):
        i, ps = slot(g)
        for e in range(E_):
            o = (e * L_) if e < 5 else S
            mm = g.pe.matmul(ps[:, o:o + L_], Bm[0:R_, e, c * P:(c + 1) * P], AT[0:R_, e * L_:(e + 1) * L_],
                             start=True, stop=True)
        t = g.E(mm)
        g.W(g.dve, t)
        g.V(g.dve.tensor_copy(tokg[:, c, 0:500], ps[:, 0:500]))
        tt = g.ring[i] = g.V(g.dve.tensor_copy(tokg[:, c, 500:600], ps[:, S:S + L_]))
    g.W(g.pe, tt)
    g.W(g.dve, tw)
    for e in range(E_):
        i, ps = slot(g)
        for c in range(DC):
            mm = g.pe.matmul(ps[0:L_, 0:D], tokg[:, c, e * L_:(e + 1) * L_], WT[:, c, :], start=c == 0, stop=c == 1)
        t = g.E(mm)
        g.W(g.dve, t)
        tvl = g.ring[i] = g.V(g.dve.tensor_tensor(val[0:L_, e, :], ps[0:L_, 0:D], wtb[0:L_, :], OP.add))
    g.W(g.dve, tvl)
    tvl = g.V(g.dve.memset(val[0:1], 0.0))
    PT = view(w, 3 * K, E_, NT)
    prob = [view(w, 9 * K + 1024 * j, n) for j in range(2)]
    sm = [view(g.small, 64 * j, 64) for j in range(2)]
    tfree = [None, None]
    sfree = [None, None]
    tlast = []
    for it in range(NT // P):
        j = it % 2
        i, ps = slot(g)
        g.W(g.pe, t1[it // 4], tt)
        for o, lo, hi in ((0, 0, 500), (S, 500, n + E_)):
            for c in range(DC):
                mm = g.pe.matmul(ps[:, o:o + hi - lo], g.Hn[:, c, it * P:(it + 1) * P], tokg[:, c, lo:hi],
                                 start=c == 0, stop=c == 1)
        t = g.E(mm)
        s = sm[j]
        mx, ng, su, gr = s[:, 0:7], s[:, 8:14], s[:, 16:22], s[:, 24:30]
        eq, m2, rs = s[:, 32:38], s[:, 40:41], s[:, 48:54]
        gl = ps[:, S + L_:S + L_ + E_]
        g.W(g.dve, t, sfree[j])
        g.V(g.dve.tensor_reduce(mx[:, 0:5], ps[:, 0:500].rearrange("p (e l) -> p e l", e=5), AX.X, OP.max))
        g.V(g.dve.tensor_reduce(mx[:, 5:6], ps[:, S:S + L_], AX.X, OP.max))
        t = g.V(g.dve.tensor_reduce(mx[:, 6:7], gl, AX.X, OP.max))
        g.W(g.dve, t)
        tn = g.V(g.dve.tensor_scalar(ng, mx[:, 0:6], -1.0 / 16, None, OP.mult))
        t = g.V(g.dve.tensor_scalar(eq, gl, mx[:, 6:7], None, OP.is_equal))
        g.W(g.dve, t)
        t = g.V(g.dve.tensor_tensor(eq, eq, rank, OP.mult))
        g.W(g.dve, t)
        t = g.V(g.dve.tensor_reduce(m2, eq, AX.X, OP.max))
        g.W(g.dve, t)
        tgt = g.V(g.dve.tensor_scalar(eq, eq, m2, None, OP.is_equal))
        g.W(g.act, tn, tgt, tfree[j])
        for e in range(E_):
            o = e * L_ if e < 5 else S
            te = g.A(g.act.activation(prob[j][:, e * L_:(e + 1) * L_], ps[:, o:o + L_], ACT.Exp, scale=1.0 / 16,
                                      bias=ng[:, e:e + 1], accum_out=su[:, e:e + 1]))
        g.ring[i] = te
        g.W(g.dve, te, tgt)
        t = g.V(g.dve.reciprocal(rs, su))
        g.W(g.dve, t)
        t = g.V(g.dve.tensor_tensor(gr, rs, eq, OP.mult))
        g.W(g.dve, t)
        pr = prob[j].rearrange("p (e l) -> p e l", e=E_)
        tp = sfree[j] = g.V(g.dve.tensor_tensor(pr, pr, gr.unsqueeze(2).broadcast_to([P, E_, L_]), OP.mult))
        i2, ps2 = slot(g)
        g.W(g.pe, tp)
        for e in range(E_):
            mm = g.pe.transpose(ps2[0:L_, e * P:(e + 1) * P], pr[:, e, :], g.iden[:, :])
        t = tfree[j] = g.E(mm)
        g.W(g.act, t)
        t = g.ring[i2] = g.A(g.act.activation(PT[0:L_, :, it * P:(it + 1) * P],
                                              ps2[0:L_, 0:E_ * P].rearrange("p (e t) -> p e t", e=E_), ACT.Copy))
        tlast.append(t)
    zb = view(w, 12 * K, 2, NT)
    g.W(g.pe, tvl)
    tz = []
    for n_ in range(B):
        i, ps = slot(g)
        g.W(g.pe, tlast[4 * n_ + 3])
        for m in range(DC):
            for e in range(E_):
                mm = g.pe.matmul(ps[:, half(m)], val[0:L_, e, m * P:(m + 1) * P], PT[0:L_, e, half(n_)],
                                 start=e == 0, stop=e == E_ - 1)
        t = g.E(mm)
        g.W(g.dve, t)
        t = g.ring[i] = g.V(g.dve.tensor_tensor(zb[:, :, half(n_)], ps.rearrange("p (c s) -> p c s", c=2),
                                                g.Hn[:, :, half(n_)], OP.add))
        tz.append(t)
    sb_ = view(g.small, 192, 2)
    t = g.V(g.dve.tensor_scalar(sb_, g.vec[:, VCOL["L0_ffn_wd_b"]:VCOL["L0_ffn_wd_b"] + 2], vcol(g, "L0_ffn_scale"),
                                None, OP.mult))
    ex, gd = view(w, 14 * K, 2, NT), view(w, 16 * K, 2, NT)

    def ev(m, ps, t2):
        g.W(g.act, t2, t)
        te = g.A(g.act.activation(ex[:, m, :], ps, ACT.Exp, scale=vcol(g, "L0_ffn_scale"), bias=sb_[:, m:m + 1]))
        g.W(g.dve, te)
        u = g.V(g.dve.tensor_scalar(gd[:, m, :], ex[:, m, :], 0.0, float(np.finfo(np.float32).eps),
                                    OP.is_equal, OP.mult))
        g.W(g.dve, u)
        u = g.V(g.dve.tensor_tensor(ex[:, m, :], ex[:, m, :], gd[:, m, :], OP.add))
        g.W(g.act, u)
        u = g.A(g.act.activation(ex[:, m, :], ex[:, m, :], ACT.Ln))
        v_ = g.V(g.dve.tensor_tensor(g.X[:, m, :], g.X[:, m, :], g.Hn[:, m, :], OP.add))
        g.W(g.dve, u, v_)
        u = g.V(g.dve.tensor_tensor(g.X[:, m, :], g.X[:, m, :], ex[:, m, :], OP.add))
        g.resid = [u, u]
        return te
    project(g, WD, zb, DC, DC, ev, tuple(tz))



def l1_attn(g):
    a, w, K = g.a, g.work, 1024
    A, Bt = g.WA, g.WB
    tw = load(g, g.d_w, Bt[:, 0:2048], a["w_l1_attn"])
    W = {n: view(Bt, i * 512, 2, 256) for i, n in enumerate(("k", "v", "r", "o"))}
    hp = view(Bt, 2048, 2, B, S + 1)
    sq, tmp = view(w, 0, 2, NT), view(w, 2 * K, NT)
    z = g.G(g.pool.memset(hp[:, :, :, 0:1], 0.0))
    t1 = layernorm(g, g.X, g.Hn, g.resid, sq, tmp, put=lambda c, n: hp[:, c, n, 1:])
    om = view(g.small, 0, 8)
    mixed = {"k": view(w, 0, 2, B, S), "v": view(w, 3 * K, 2, B, S), "r": view(w, 5 * K, 2, B, S)}
    g.W(g.dve, z, t1)
    tm = {}
    for q, n in enumerate("kvr"):
        col = VCOL["L1_attn_time_mix_" + n]
        t = g.V(g.dve.tensor_scalar(om[:, 2 * q:2 * q + 2], g.vec[:, col:col + 2], -1.0, 1.0, OP.mult, OP.add))
        for c in range(DC):
            t2 = g.V(g.dve.tensor_scalar(mixed[n][:, c], hp[:, c, :, 1:], vcol(g, "L1_attn_time_mix_" + n, c), None,
                                         OP.mult))
            g.W(g.dve, t, t2)
            tm[n] = g.V(g.dve.scalar_tensor_tensor(out=mixed[n][:, c], in0=hp[:, c, :, 0:S],
                                                   scalar=om[:, 2 * q + c:2 * q + c + 1], in1=mixed[n][:, c],
                                                   op0=OP.mult, op1=OP.add))
    k, v, r = (view(w, o * K, 2, NT) for o in (7, 9, 11))
    flat = {n: x.rearrange("p c b s -> p c (b s)") for n, x in mixed.items()}
    g.W(g.pe, tw)

    def copy_to(dst, func=ACT.Copy):
        def ev(m, ps, t):
            g.W(g.act, t)
            return g.A(g.act.activation(dst[:, m, :], ps, func))
        return ev
    tk = project(g, W["k"], flat["k"], DC, DC, copy_to(k), tm["k"])
    tv = project(g, W["v"], flat["v"], DC, DC, copy_to(v), tm["v"])
    tr = project(g, W["r"], flat["r"], DC, DC, copy_to(r, ACT.Sigmoid), tm["r"])
    pb = view(A, 0, 2, B, S + 1)
    qb = view(A, 2100, 2, B, S + 1)
    wb = view(w, 13 * K, S)
    ones = view(w, 13 * K + S, S)
    t = g.V(g.dve.memset(ones, 1.0))
    t0 = g.V(g.dve.memset(pb[:, :, :, 0:1], -BIG))
    t0 = g.V(g.dve.memset(qb[:, :, :, 0:1], 0.0))
    g.W(g.dve, t, t0, tk)
    for c in range(DC):
        t = g.V(g.dve.tensor_scalar(wb, ones, vcol(g, "L1_attn_time_decay", c), None, OP.mult))
        g.W(g.dve, t)
        for b in range(B):
            t = g.V(g.dve.tensor_tensor_scan(pb[:, c, b, 1:], wb, k[:, c, half(b)], -BIG, OP.add, OP.max))
        g.W(g.dve, t)
    tp = t
    uk, mx, so, sc = (view(w, o * K, 2, B, S) for o in (0, 3, 5, 14))
    sp, sn = view(A, 4200, 2, B, S), view(g.WB, 4200 - 100, 2, B, S)
    kb = k.rearrange("p c (b s) -> p c b s", b=B)
    vb = v.rearrange("p c (b s) -> p c b s", b=B)
    g.W(g.dve, g.now("pe"))

    def clamp_exp(dst, t):
        g.W(g.dve, t)
        t = g.V(g.dve.tensor_scalar(dst, dst, -30.0, None, OP.max))
        g.W(g.act, t)
        return g.A(g.act.activation(dst, dst, ACT.Exp))
    te = []
    for c in range(DC):
        p0, p1 = pb[:, c, :, 0:S], pb[:, c, :, 1:]
        t = g.V(g.dve.scalar_tensor_tensor(out=sp[:, c], in0=p0, scalar=vcol(g, "L1_attn_time_decay", c),
                                           in1=p1, op0=OP.add, op1=OP.subtract))
        t1_ = g.V(g.dve.tensor_tensor(sn[:, c], kb[:, c], p1, OP.subtract))
        te.append(clamp_exp(sp[:, c], t))
        te.append(clamp_exp(sn[:, c], t1_))
        t = g.V(g.dve.tensor_scalar(uk[:, c], kb[:, c], vcol(g, "L1_attn_time_first", c), None, OP.add))
        g.W(g.dve, t)
        t = g.V(g.dve.tensor_tensor(mx[:, c], p0, uk[:, c], OP.max))
        g.W(g.dve, t)
        t = g.V(g.dve.tensor_tensor(so[:, c], p0, mx[:, c], OP.subtract))
        t1_ = g.V(g.dve.tensor_tensor(sc[:, c], uk[:, c], mx[:, c], OP.subtract))
        te.append(clamp_exp(so[:, c], t))
        te.append(clamp_exp(sc[:, c], t1_))
    g.W(g.dve, te, tv)
    for c in range(DC):
        t = g.V(g.dve.tensor_tensor(sn[:, c], sn[:, c], vb[:, c], OP.mult))
        g.W(g.dve, t)
        for b in range(B):
            tq = g.V(g.dve.tensor_tensor_scan(qb[:, c, b, 1:], sp[:, c, b], sn[:, c, b], 0.0, OP.mult, OP.add))
        t = g.V(g.dve.tensor_tensor(mx[:, c], so[:, c], sc[:, c], OP.add))
        g.W(g.act, t)
        t = g.A(g.act.activation(uk[:, c], mx[:, c], ACT.Ln, bias=g.e9))
        g.W(g.act, t)
        t5 = g.A(g.act.activation(uk[:, c], uk[:, c], ACT.Exp, scale=-1.0))
        g.W(g.dve, tq)
        t = g.V(g.dve.tensor_tensor(so[:, c], so[:, c], qb[:, c, :, 0:S], OP.mult))
        t2 = g.V(g.dve.tensor_tensor(sc[:, c], sc[:, c], vb[:, c], OP.mult))
        g.W(g.dve, t2)
        t = g.V(g.dve.tensor_tensor(so[:, c], so[:, c], sc[:, c], OP.add))
        g.W(g.dve, t, t5)
        t = g.V(g.dve.tensor_tensor(so[:, c], so[:, c], uk[:, c], OP.mult))
        g.W(g.dve, t, tr)
        t = g.V(g.dve.tensor_tensor(so[:, c], so[:, c], r[:, c].rearrange("p (b s) -> p b s", b=B), OP.mult))
    project(g, W["o"], so.rearrange("p c b s -> p c (b s)"), DC, DC, add_resid(g), t)


def l1_xattn(g):
    a, w, K = g.a, g.work, 1024
    A, Bt = g.WA, g.WB
    tw = load(g, g.d_w, Bt[:, 0:1024], a["w_l1_xattn"])
    W = [view(Bt, 0, 2, D), view(Bt, 512, 2, D)]
    mraw, madd = view(Bt, 1024, B, S2).bitcast(I32), view(Bt, 1024 + 2 * K, B, S2)
    tmk = load(g, g.d_w2, mraw, a["mask1"].partition_broadcast(P))
    sq, tmp = view(w, 0, 2, NT), view(w, 2 * K, NT)
    u = view(w, 3 * K, 2, NT)
    tu = list(layernorm(g, g.X, u, g.resid, sq, tmp))
    g.W(g.dve, tmk)
    tmk = g.V(g.dve.tensor_scalar(madd, mraw, 0.0, FMIN, OP.is_equal, OP.mult))
    key = view(w, 5 * K, 2, NT)
    prob = [view(w, (7 + j) * K, S2) for j in range(4)]
    PT = [view(w, 11 * K, 8, S), view(w, 15 * K, 8, S)]
    sm = view(g.small, 0, 64)
    g.W(g.dve, tmk)
    g.W(g.pe, tw)
    pfree, ptfree, n_u = [None] * 4, [None] * 2, 0
    for hop in range(2):
        def ev(m, ps, t):
            g.W(g.act, t)
            return g.A(g.act.activation(key[:, m, :], ps, ACT.Copy))
        tk = project(g, W[hop], u, DC, DC, ev, tuple(tu))
        g.W(g.pe, tk)
        for b in range(B):
            for qt in range(4):
                j = n_u % 4
                i, ps = slot(g)
                q0 = b * S + qt * P
                for hf in range(2):
                    for c in range(DC):
                        mm = g.pe.matmul(ps[:, half(hf)], key[:, c, q0:q0 + P],
                                         g.ctxT[:, c, b * S2 + hf * S:b * S2 + (hf + 1) * S], start=c == 0, stop=c == 1)
                t = g.E(mm)
                nm, su, rs = (sm[:, o + j:o + j + 1] for o in (0, 8, 16))
                g.W(g.dve, t, pfree[j])
                t = g.ring[i] = g.V(g.dve.tensor_tensor_reduce(prob[j], ps, madd[:, b, :], -1.0, BIG * 3e8, OP.add,
                                                               OP.min, nm))
                g.W(g.act, t)
                t = g.A(g.act.activation(prob[j], prob[j], ACT.Exp, scale=-1.0, bias=nm, accum_out=su))
                g.W(g.dve, t)
                t = g.V(g.dve.reciprocal(rs, su))
                g.W(g.dve, t)
                t = g.V(g.dve.tensor_scalar(prob[j], prob[j], rs, None, OP.mult))
                i, ps = slot(g)
                g.W(g.pe, t)
                for kt in range(8):
                    mm = g.pe.transpose(ps[:, kt * P:(kt + 1) * P], prob[j][:, kt * P:(kt + 1) * P], g.iden[:, :])
                pfree[j] = t = g.E(mm)
                g.W(g.act, t, ptfree[b])
                tpt = g.ring[i] = g.A(g.act.activation(PT[b][:, :, qt * P:(qt + 1) * P],
                                                       ps.rearrange("p (k t) -> p k t", k=8), ACT.Copy))
                n_u += 1
            i, ps = slot(g)
            g.W(g.pe, tpt)
            for m in range(DC):
                for kt in range(8):
                    mm = g.pe.matmul(ps[:, half(m)], g.ctxK[:, b * 8 + kt, m * P:(m + 1) * P], PT[b][:, kt, :],
                                     start=kt == 0, stop=kt == 7)
            t = ptfree[b] = g.E(mm)
            g.W(g.dve, t)
            t = g.ring[i] = g.V(g.dve.tensor_tensor(u[:, :, half(b)], ps.rearrange("p (c s) -> p c s", c=2),
                                                    u[:, :, half(b)], OP.add))
            tu[b] = t
    g.W(g.dve, tu)
    t = g.V(g.dve.tensor_tensor(g.X, g.X, u, OP.add))
    g.resid = [t, t]


def quantize(g, src, dst, tmp, sc, ready, engine=None):
    am, s, inv, al = (sc[:, i:i + 1] for i in range(4))
    g.W(g.dve, ready)
    t = g.V(g.dve.tensor_reduce(am, src, AX.X, OP.max, apply_absolute_value=True))
    g.W(g.pool, t)
    t = g.G(g.pool.partition_all_reduce(al, am, P, bass.bass_isa.ReduceOp.max))
    g.W(g.dve, t)
    t = g.V(g.dve.tensor_scalar(s, al, 1e-6, 1.0 / 127, OP.max, OP.mult))
    g.W(g.dve, t)
    t = g.V(g.dve.reciprocal(inv, s))
    g.W(g.dve, t)
    t = g.V(g.dve.tensor_scalar(tmp, src, inv, ROUND, OP.mult, OP.add))
    g.W(g.dve, t)
    return g.V(g.dve.tensor_scalar(dst, tmp, ROUND, None, OP.subtract))


def l1_ffn(g):
    a, w, K = g.a, g.work, 1024
    A, Bt = g.WA, g.WB
    tw = load(g, g.d_w, A[:, 0:4096], a["w_l1_ffn"])
    W1, W2 = A[:, 0:2048], A[:, 2048:4096]
    W1q = view(A, 4096, K).bitcast(BF16)
    W2q = view(A, 4096 + K, K).bitcast(BF16)
    tb = Bt[:, 0:8192]
    sc = [view(g.small, 4 * i, 4) for i in range(4)]
    tw1 = quantize(g, W1, W1q, tb[:, 0:2048], sc[0], tw)
    tw2 = quantize(g, W2, W2q, tb[:, 2048:4096], sc[1], tw)
    sq, tmp = view(w, 0, 2, NT), view(w, 2 * K, NT)
    t1 = layernorm(g, g.X, g.Hn, g.resid, sq, tmp)
    hq = view(w, 3 * K, K).bitcast(BF16)
    tx = quantize(g, g.Hn.rearrange("p c t -> p (c t)"), hq, tb[:, 4096:6144], sc[2], t1)
    ss = view(g.small, 32, 2)
    b1s, b2s = view(g.small, 40, 8), view(g.small, 50, 2)
    g.W(g.dve, tx, tw2)
    t = g.V(g.dve.tensor_tensor(ss[:, 0:1], sc[0][:, 1:2], sc[2][:, 1:2], OP.mult))
    g.W(g.dve, t)
    col = VCOL["L1_ffn_b1"]
    tb1 = g.V(g.dve.tensor_scalar(b1s, g.vec[:, col:col + 8], ss[:, 0:1], None, OP.mult))
    hid = view(w, 4 * K, FC, NT)

    def ev1(m, ps, t):
        g.W(g.act, t, tb1)
        return g.A(g.act.activation(hid[:, m, :], ps, ACT.Gelu, scale=ss[:, 0:1], bias=b1s[:, m:m + 1]))
    th = project(g, W1q.rearrange("p (c f) -> p c f", c=2), hq.rearrange("p (c t) -> p c t", c=2), DC, FC, ev1,
                 [tx, tw1])
    hf = hid.rearrange("p c t -> p (c t)")
    hidq = view(w, 12 * K, 4 * K).bitcast(BF16)
    tq = quantize(g, hf, hidq, tb, sc[3], th)
    t = g.V(g.dve.tensor_tensor(ss[:, 1:2], sc[1][:, 1:2], sc[3][:, 1:2], OP.mult))
    g.W(g.dve, t)
    col = VCOL["L1_ffn_b2"]
    t = g.V(g.dve.tensor_scalar(b2s, g.vec[:, col:col + 2], ss[:, 1:2], None, OP.mult))
    g.W(g.dve, t)
    o = view(w, 0, 2, NT)

    def ev2(m, ps, t):
        g.W(g.dve, t)
        t = g.V(g.dve.tensor_scalar(o[:, m, :], ps, ss[:, 1:2], b2s[:, m:m + 1], OP.mult, OP.add))
        g.W(g.dve, t)
        t2 = g.V(g.dve.tensor_tensor(g.X[:, m, :], g.X[:, m, :], o[:, m, :], OP.add))
        g.resid = [t2, t2]
        return t
    project(g, W2q.rearrange("p (c f) -> p c f", c=FC), hidq.rearrange("p (c t) -> p c t", c=FC), FC, DC, ev2,
            [tq, tw2])



def mha(g, name):
    a, w, K = g.a, g.work, 1024
    cf = MHA[name]
    kind, nh, rows, keys = cf["kind"], cf["heads"], cf["rows"], cf["keys"]
    cross = name.endswith("xattn")
    nk = keys // P
    src = g.ctxT if cross else g.Hn
    kstride = S2 if cross else S
    q = [view(w, h * K, NT) for h in range(nh)]
    kT = view(w, 4 * K, B, keys)
    v = view(w, 6 * K, B, nk, P)
    NP = 3
    prob = [view(w, (8 + j) * K, keys) for j in range(NP)]
    PT = [view(w, (11 + 4 * j) * K, nh, nk, P) for j in range(2)]
    ws = [view(g.wst, 256 * i, 2, P) for i in range(3)]
    bv = g.wst[:, 768:768 + P]
    bqk = g.wst[:, 768 + P:768 + P + 2]
    sm = view(g.small, 0, 64)
    fixed = kind == "fixed"
    A, Bt = g.WA, g.WB
    fx = [view(A, o, K) for o in (0, K, 2 * K, 3 * K, 6 * K, 7 * K)] if fixed else None
    oT = view(A, 0, 8, NT) if not fixed and kind != "grouped" else None
    if fixed:
        oT = view(Bt, 0, 8, NT)
        sgn = [view(A, 4096 + j * 512, 512) for j in range(2)]
        nint = [view(A, 5120 + j * 512, 512).bitcast(I32) for j in range(2)]
    if kind == "grouped":
        G = view(A, 0, B, 4, S2)
        NEG = view(Bt, 0, B, 4, S2)
        tG = load(g, g.d_w, G, a["group"].rearrange("b (q p) k -> p b q k", p=P))
        tN = load(g, g.d_w2, NEG.bitcast(I32), a["mask2"].rearrange("b (q p) k -> p b q k", p=P))
        g.W(g.dve, tN, tG)
        nf = NEG.rearrange("p b q k -> p (b q k)")
        t = g.V(g.dve.tensor_scalar(nf, nf.bitcast(I32), -1.0, 1.0, OP.mult, OP.add))
        g.W(g.dve, t)
        t = g.V(g.dve.tensor_scalar(nf, nf, -1e9, None, OP.mult))
        g.W(g.dve, t)
        oT = None
    if kind in ("alibi", "causal"):
        rel = view(Bt, 0, S)
        tr = load(g, g.d_w, rel, a["rel" if kind == "alibi" else "causal"])
        g.W(g.dve, tr)
        g.W(g.pool, tr)
        if kind == "alibi":
            slopes = g.wst[:, 768 + P + 2:768 + P + 2 + nh]
            bias = [view(Bt, (1 + h) * S, S) for h in range(nh)]
    zero = []
    g.meet()
    for h in range(nh):
        zero.append(g.G(g.pool.memset(q[h], 0.0)))
    if kind == "grouped":
        oT = None
    scale = {"fixed": 1.0, "grouped": 0.25, "alibi": 0.25, "causal": 0.125}[kind]
    if kind == "alibi":
        rt = view(g.small, 100, 1)
        t = g.V(g.dve.reciprocal(rt, vcol(g, "L3_attn_temperature")))
        g.W(g.dve, t)
        t = g.V(g.dve.tensor_scalar(rt, rt, 0.25, None, OP.mult))
        g.W(g.dve, t)
        scale = rt
    wsrc = a["w_" + name]
    if kind == "grouped":
        oT = g.ctxK.rearrange("p k d -> p (k d)").rearrange("p (g t) -> p g t", t=NT)
    with g.fori(cf["groups"]) as gi:
        g.ring = [None] * 4
        g.ring_i = 0
        tw = g.dma(g.d_st, g.wst[:, 0:768], wsrc[gi])
        tw = g.dma(g.d_st, bqk, a["bqk_" + name][gi])
        tw = g.dma(g.d_st, bv, a["bv_" + name][gi].partition_broadcast(P))
        if kind == "alibi":
            tw = g.dma(g.d_st, slopes, a["slopes"][gi].partition_broadcast(P))
        for e in (g.pe, g.dve, g.act, g.pool):
            g.W(e, tw)
        if kind == "alibi":
            for h in range(nh):
                tb = g.G(g.pool.tensor_scalar(bias[h], rel, slopes[:, h:h + 1], 1.0, OP.mult, OP.mult))

        def fixed_point(src_ps, t, dst, sc_out, parts, st):
            y, s_ = st
            g.W(g.act, t)
            t = g.A(g.act.activation(y, src_ps, ACT.Copy, scale=FX))
            g.W(g.act, t)
            tf = t
            t1 = g.A(g.act.activation(s_, y, ACT.Sign))
            g.W(g.dve, t1)
            t = g.V(g.dve.tensor_scalar(y, y, FXMAX, -FXMAX, OP.min, OP.max))
            g.W(g.dve, t)
            n_ = s_.bitcast(I32)
            t = g.V(g.dve.scalar_tensor_tensor(out=n_, in0=s_, scalar=-HALF, in1=y, op0=OP.mult, op1=OP.add))
            g.W(g.dve, t)
            for d_, p0, p1 in parts:
                t = g.V(g.dve.tensor_scalar(d_, n_[p0:p1] if p1 - p0 < P else n_, sc_out, None, OP.mult))
            return tf, t

        i, ps = slot(g)
        for n in range(B):
            for c in range(DC):
                mm = g.pe.matmul(ps[:, half(n)], ws[0][:, c, :], g.Hn[:, c, half(n)], start=c == 0, stop=c == 1)
        t = g.E(mm)
        if fixed:
            parts = [(q[h][h * rows:(h + 1) * rows, :], h * rows, (h + 1) * rows) for h in range(nh)]
            g.ring[i], tq = fixed_point(ps, t, None, 0.125, parts, (fx[0], fx[1]))
        else:
            g.W(g.dve, t)
            for h in range(nh):
                r0 = h * rows
                tq = g.V(g.dve.tensor_scalar(q[h][r0:r0 + rows, :], ps[r0:r0 + rows, :], bqk[r0:r0 + rows, 0:1],
                                             scale if isinstance(scale, float) else scale[r0:r0 + rows, :],
                                             OP.add, OP.mult))
            g.ring[i] = tq
        kf = kT.rearrange("p b k -> p (b k)")
        for b2 in range(max(1, keys * B // NT)):
            i, ps = slot(g)
            for n in range(2):
                k0 = b2 * NT + n * S if keys == S2 else n * kstride
                for c in range(DC):
                    mm = g.pe.matmul(ps[:, half(n)], ws[1][:, c, :], src[:, c, k0:k0 + S], start=c == 0, stop=c == 1)
            t = g.E(mm)
            if fixed:
                g.ring[i], tk = fixed_point(ps, t, None, 1.0 / FX, [(kf, 0, P)], (fx[2], fx[3]))
            else:
                g.W(g.act, t)
                tk = g.ring[i] = g.A(g.act.activation(kf[:, b2 * NT:b2 * NT + NT], ps, ACT.Identity, bias=bqk[:, 1:2]))
        for b2 in range(B * nk // 8):
            i, ps = slot(g)
            for j in range(8):
                kt = b2 * 8 + j
                k0 = (kt // nk) * kstride + (kt % nk) * P
                for c in range(DC):
                    mm = g.pe.matmul(ps[:, j * P:(j + 1) * P], src[:, c, k0:k0 + P], ws[2][:, c, :],
                                     start=c == 0, stop=c == 1)
            t = g.E(mm)
            vf = v.rearrange("p b k d -> p (b k) d")
            if fixed:
                g.ring[i], tv = fixed_point(ps, t, None, 1.0 / FX, [(vf.rearrange("p k d -> p (k d)"), 0, P)],
                                            (fx[4], fx[5]))
            else:
                g.W(g.dve, t)
                tv = g.ring[i] = g.V(g.dve.tensor_tensor(vf[:, b2 * 8:b2 * 8 + 8, :],
                                                         ps.rearrange("p (k d) -> p k d", k=8),
                                                         bv.unsqueeze(1).broadcast_to([P, 8, P]), OP.add))
        g.W(g.pe, tq, tk, tv)
        if kind == "alibi":
            g.W(g.dve, tb)

        g.W(g.pe, g.ring)
        units = [(b, qt, h) for b in range(B) for qt in range(4) for h in range(nh)]
        s_free, t_free, o_free = [None] * 2, [None] * 2, [None] * 2
        p_free, pt_free = [None] * NP, [None] * 2
        st = {}
        n_t = 0

        def nkeys(qt):
            return (qt + 1) * P if cf["causal"] else keys

        def front(u):
            b, qt, h = units[u]
            n = nkeys(qt)
            sps = g.ps[:, (u % 2) * 1024:(u % 2) * 1024 + n]
            g.W(g.pe, s_free[u % 2])
            q0 = b * S + qt * P
            for o in range(0, n, S):
                e_ = min(n, o + S)
                mm = g.pe.matmul(sps[:, o:e_], q[h][:, q0:q0 + P], kT[:, b, o:e_], start=True, stop=True)
            t = g.E(mm)
            j = u % NP
            p = prob[j][:, 0:n]
            nm, su = sm[:, j:j + 1], sm[:, 8 + j:9 + j]
            if fixed:
                g.W(g.act, t)
                z = u % 2
                t1 = g.A(g.act.activation(sgn[z][:, 0:n], sps, ACT.Sign))
                g.W(g.dve, t, t1, st.get(("n", z)))
                t = g.V(g.dve.scalar_tensor_tensor(out=nint[z][:, 0:n], in0=sgn[z][:, 0:n], scalar=-HALF, in1=sps,
                                                   op0=OP.mult, op1=OP.add))
                s_free[u % 2] = t
                g.W(g.pool, t, p_free[j])
                t = g.G(g.pool.tensor_scalar(p, nint[z][:, 0:n], FXMAX, -FXMAX, OP.min, OP.max))
                st["n", z] = t
                g.W(g.act, t)
                st[u] = g.A(g.act.activation(p, p, ACT.Exp, scale=1.0 / FX, accum_out=su))
            else:
                g.W(g.dve, t, p_free[j])
                if kind == "grouped":
                    add = NEG[:, b, qt, :]
                elif kind == "alibi":
                    add = bias[h][:, S - n:S]
                else:
                    add = rel[:, S - n:S]
                t = s_free[u % 2] = g.V(g.dve.tensor_tensor_reduce(p, sps, add, -1.0, BIG * 3e8, OP.add, OP.min, nm))
                g.W(g.act, t)
                st[u] = g.A(g.act.activation(p, p, ACT.Exp, scale=-1.0, bias=nm, accum_out=su))

        def mid(u):
            b, qt, h = units[u]
            n = nkeys(qt)
            j = u % NP
            p = prob[j][:, 0:n]
            su, rs = sm[:, 8 + j:9 + j], sm[:, 16 + j:17 + j]
            g.W(g.dve, st[u])
            t = g.V(g.dve.reciprocal(rs, su))
            g.W(g.dve, t)
            if fixed:
                t = g.V(g.dve.tensor_scalar(rs, rs, FX, None, OP.mult))
                g.W(g.dve, t)
                st["m", u] = g.V(g.dve.tensor_scalar(p, p, rs, 8388607.5, OP.mult, OP.add))
            elif kind == "grouped":
                st["m", u] = g.V(g.dve.scalar_tensor_tensor(out=p, in0=p, scalar=rs, in1=G[:, b, qt, :], op0=OP.mult,
                                                            op1=OP.mult))
            else:
                g.W(g.pool, t)
                st["m", u] = g.G(g.pool.tensor_scalar(p, p, rs, 1.0, OP.mult, OP.mult))

        def back(u):
            nonlocal n_t
            b, qt, h = units[u]
            n = nkeys(qt)
            j = u % NP
            p = prob[j][:, 0:n]
            r = (u // nh) % 2
            g.W(g.pe, st["m", u])
            for o in range(0, n, S):
                z = n_t % 2
                n_t += 1
                nt = (min(n, o + S) - o) // P
                tps = g.ps[:, 2048 + z * S:2048 + z * S + nt * P]
                g.W(g.pe, t_free[z])
                for kt in range(nt):
                    mm = g.pe.transpose(tps[:, kt * P:(kt + 1) * P], p[:, o + kt * P:o + (kt + 1) * P], g.iden[:, :])
                t = p_free[j] = g.E(mm)
                dst = PT[r][:, h, o // P:o // P + nt, :].rearrange("p k t -> p (k t)")
                if fixed:
                    g.W(g.dve, t, pt_free[r])
                    t = g.V(g.dve.tensor_scalar(dst, tps, -8388608.0, 0.0, OP.add, OP.max))
                else:
                    g.W(g.act, t, pt_free[r])
                    t = g.A(g.act.activation(dst, tps, ACT.Copy))
                t_free[z] = t
            st["b", u] = t
            if h == nh - 1:
                ops = g.ps[:, 3072 + r * S:3072 + r * S + P]
                g.W(g.pe, [st["b", u - x] for x in range(nh)], o_free[r])
                nt = n // P
                for kt in range(nt):
                    for h2 in range(nh):
                        mm = g.pe.matmul(ops[h2 * rows:(h2 + 1) * rows, :], v[:, b, kt, h2 * rows:(h2 + 1) * rows],
                                         PT[r][:, h2, kt, :], start=kt == 0, stop=kt == nt - 1)
                t = pt_free[r] = g.E(mm)
                g.W(g.act, t)
                q0 = b * S + qt * P
                o_free[r] = g.A(g.act.activation(oT[:, gi, q0:q0 + P], ops, ACT.Copy))

        n_u = len(units)
        for u in range(n_u + 2):
            if u < n_u:
                front(u)
            if 1 <= u <= n_u:
                mid(u - 1)
            if u >= 2:
                back(u - 2)
    return oT


def out_project(g, name, oT, wo_at, bias, ready):
    n = MHA[name]["groups"]
    wo = view(wo_at, 0, n, D)
    tw = load(g, g.d_w, wo, g.a["wo_" + name])
    g.W(g.pe, tw)
    project(g, wo, oT, n, DC, add_resid(g, bias), ready)


def norm_for(g):
    w, K = g.work, 1024
    return layernorm(g, g.X, g.Hn, g.resid, view(w, 0, 2, NT), view(w, 2 * K, NT))


def fixed_in_place(g, x, tmp, n_cols, t, pre):
    g.W(g.dve, t)
    t = g.V(g.dve.tensor_scalar(x, x, pre, FXMAX, OP.mult, OP.min))
    g.W(g.dve, t)
    t = g.V(g.dve.tensor_scalar(x, x, -FXMAX, None, OP.max))
    g.W(g.act, t)
    t = g.A(g.act.activation(tmp, x, ACT.Sign))
    g.W(g.dve, t)
    ti = tmp.bitcast(I32)
    t = g.V(g.dve.scalar_tensor_tensor(out=ti, in0=tmp, scalar=-HALF, in1=x, op0=OP.mult, op1=OP.add))
    g.W(g.dve, t)
    return g.V(g.dve.tensor_scalar(x, ti, 1.0 / FX, None, OP.mult))


def fixed_attention(g, oT):
    a, w, K, A = g.a, g.work, 1024, g.WA
    nh, rows, nk, G = 2, 64, S // P, MHA["L2_attn"]["groups"]
    q = [[view(w, (4 * s + h) * K, NT) for h in range(nh)] for s in range(2)]
    kT = [view(w, (4 * s + 2) * K, NT) for s in range(2)]
    v = [view(w, (4 * s + 3) * K, B, nk, P) for s in range(2)]
    NE, NA, NS = 16, 8, 4
    ex = [view(w, 8 * K + j * S, S) for j in range(NE)]
    total = [view(w, 16 * K + j * S, S) for j in range(2)]
    diag = [view(w, 17 * K + j * S, S) for j in range(2)]
    sign = [view(w, 18 * K + j * S, S) for j in range(2)]
    attn = [view(A, j * S, S) for j in range(NA)]
    score = [view(A, (8 + j) * S, S).bitcast(I32) for j in range(NS)]
    whole = [view(A, (12 + j) * S, S).bitcast(I32) for j in range(2)]
    oy, osign = view(A, 14 * S, S), view(A, 15 * S, S)
    py, psign = ([view(g.extra, (2 * x + j) * S, S) for j in range(2)] for x in range(2))
    weights = [g.wst[:, 0:768], g.wst2[:, 0:768]]
    step_col, minus_half = g.small[:, 0:1], g.small[:, 1:2]
    recip = [g.small[:, 8 + 8 * j:12 + 8 * j] for j in range(2)]
    bank = [g.ps[:, i * S:(i + 1) * S] for i in range(8)]
    s_bank, r_bank, o_bank, p_bank = bank[0:3], bank[3:5], bank[5], bank[6:8]
    tiles = [(s, b, h, kt) for s in range(2) for b in range(B) for h in range(nh) for kt in range(nk)]
    n_t, per = len(tiles), B * nh * nk
    AGE = dict(scores=0, trunc=1, clip=2, exp=3, add=4, sum=5, diag=6, R=7, norm=11, int=12, conv=13, pv=15,
               out=17, osign=18, oint=19, oput=20)

    def chunk(s, what, n, z, ready):
        W = [view(weights[s], 256 * i, 2, P) for i in range(3)]
        ps = p_bank[z]
        g.W(g.pe, chunk.psum_free[z])
        if what == "v":
            for j in range(4):
                for c in range(DC):
                    k0 = n * S + j * P
                    mm = g.pe.matmul(ps[:, j * P:(j + 1) * P], g.Hn[:, c, k0:k0 + P], W[2][:, c, :],
                                     start=c == 0, stop=c == 1)
        else:
            for c in range(DC):
                mm = g.pe.matmul(ps, W[what == "k"][:, c, :], g.Hn[:, c, half(n)], start=c == 0, stop=c == 1)
        t = g.E(mm)
        yield
        g.W(g.act, t, chunk.free[z])
        g.A(g.act.activation(py[z], ps, ACT.Copy, scale=FX))
        t = chunk.psum_free[z] = g.A(g.act.activation(psign[z], ps, ACT.Sign))
        yield
        g.W(g.dve, t)
        t = g.V(g.dve.tensor_scalar(py[z], py[z], FXMAX, -FXMAX, OP.min, OP.max))
        g.W(g.dve, t)
        ni = psign[z].bitcast(I32)
        t = g.V(g.dve.scalar_tensor_tensor(out=ni, in0=psign[z], scalar=-HALF, in1=py[z], op0=OP.mult, op1=OP.add))
        g.W(g.dve, t, ready())
        if what == "q":
            for h in range(nh):
                r = slice(h * rows, (h + 1) * rows)
                t = g.V(g.dve.tensor_scalar(q[s][h][r, half(n)], ni[r], 0.125, None, OP.mult))
        else:
            dst = kT[s][:, half(n)] if what == "k" else v[s][:, n].rearrange("p k d -> p (k d)")
            t = g.V(g.dve.tensor_scalar(dst, ni, 1.0 / FX, None, OP.mult))
        chunk.free[z] = t
        yield t

    QK, V_ = [("q", 0), ("k", 0), ("q", 1), ("k", 1)], [("v", 0), ("v", 1)]

    def chunks(s, which, ready):
        running, toks = [], []
        todo = list(enumerate(which))
        while todo or running:
            running = [r for r in running if not isinstance(chunks_step(r, toks), Tok)]
            if todo and len(running) < 2:
                z, (what, n) = todo.pop(0)
                r = chunk(s, what, n, z % 2, ready)
                next(r)
                running.append(r)
            if running:
                yield
                chunks_step(running[-1], toks)
                yield
        g.projected = toks

    def chunks_step(r, toks):
        t = next(r)
        if isinstance(t, Tok):
            toks.append(t)
        return t

    def body(first, old, new, fetch_even=None, fetch_odd=None):
        chunk.psum_free, chunk.free = [None] * 2, [None] * 2
        T, running = {}, {}
        done = lambda name, i: T.get((name, i))
        plan = {0: ("v0", 0, V_, None),
                4: ("qk1", 1, QK, None),
                16: ("v1", 1, V_, lambda: done("pv", -1)),
                20: ("qk0", 0, QK, lambda: done("qk", per - 1))} if new else {}

        def due(stage):
            i = step - AGE[stage]
            return i, (new if i >= 0 else old) and i < n_t

        def head_due(stage):
            i, on = due(stage)
            return i // nk, on and i % nk == nk - 1
        for step in range(n_t if new else AGE["oput"] + 1):
            if step in plan:
                key, s, which, ready = plan[step]
                if key == "qk0":
                    g.W(g.pe, t_even)
                running[key] = chunks(s, which, ready or (lambda: None))
            for key in list(running):
                if next(running[key], "end") == "end":
                    T["projected", key] = g.projected
                    del running[key]
                    if key == "v0" and fetch_even:
                        t_even = fetch_even(g.now("pe"))
                    if key == "v1" and fetch_odd:
                        t_odd = fetch_odd(g.now("pe"))
            for stage in ("out", "osign", "oint", "oput"):
                i, on = due(stage)
                s, b, h, kt = tiles[i % n_t]
                if not (on and (h, kt) == (1, nk - 1)):
                    continue
                on_ = osign.bitcast(I32)
                if stage == "out":
                    g.W(g.dve, done("pv", i), done("oput", i - per // 2))
                    T[stage, i] = g.V(g.dve.tensor_scalar(oy, o_bank, FXMAX, -FXMAX, OP.min, OP.max))
                elif stage == "osign":
                    g.W(g.act, done("out", i))
                    T[stage, i] = g.A(g.act.activation(osign, oy, ACT.Sign))
                elif stage == "oint":
                    g.W(g.dve, done("osign", i))
                    T[stage, i] = g.V(g.dve.scalar_tensor_tensor(out=on_, in0=osign, scalar=-HALF, in1=oy,
                                                                 op0=OP.mult, op1=OP.add))
                else:
                    g.W(g.act, done("oint", i))
                    group = (first if i >= 0 else first - 2) + s
                    T[stage, i] = g.A(g.act.activation(oT[:, group, half(b)], on_, ACT.Copy, scale=1.0 / FX))
            i, on = due("exp")
            if on:
                g.W(g.act, done("clip", i))
                T["exp", i] = g.A(g.act.activation(ex[i % NE], ex[i % NE], ACT.Exp, scale=1.0 / FX))
            i, on = due("int")
            if on:
                g.W(g.act, done("norm", i), done("conv", i - 2))
                T["int", i] = g.A(g.act.activation(whole[i % 2], ex[i % NE], ACT.Identity, bias=minus_half))
            i, on = due("add")
            if on and i % nk > 0:
                u = i // nk
                g.W(g.pool, done("exp", i), done("exp", i - 1), done("sum", u - 2), done("add", i - 1))
                in0 = ex[(i - 1) % NE] if i % nk == 1 else total[u % 2]
                T["add", i] = g.G(g.pool.tensor_tensor(total[u % 2], in0, ex[i % NE], OP.add))
            i, on = due("conv")
            if on:
                g.W(g.pool, done("int", i), done("pv", i - NA))
                T["conv", i] = g.G(g.pool.tensor_scalar(attn[i % NA], whole[i % 2], 1.0, 0.0, OP.mult, OP.add))
            i, on = due("clip")
            if on:
                g.W(g.dve, done("trunc", i), done("int", i - NE))
                T["clip", i] = g.V(g.dve.tensor_scalar(ex[i % NE], score[i % NS], FXMAX, -FXMAX, OP.min, OP.max))
            i, on = due("norm")
            if on:
                g.W(g.dve, done("R", i // nk))
                T["norm", i] = g.V(g.dve.tensor_tensor(ex[i % NE], ex[i % NE], r_bank[i // nk % 2], OP.mult))
            u, on = head_due("diag")
            if on:
                g.W(g.dve, done("sum", u), done("diag", u - 2))
                t = g.V(g.dve.reciprocal(recip[u % 2], r_bank[u % 2][:, 0:4]))
                g.W(g.pool, t, done("R", u - 2))
                for j in range(4):
                    T["diag", u] = g.G(g.pool.tensor_scalar(diag[u % 2][:, j * P:(j + 1) * P], g.iden[:, :],
                                                            recip[u % 2][:, j:j + 1], 1.0, OP.mult, OP.mult))
            i, on = due("trunc")
            if on:
                ps = s_bank[i % n_t % 3]
                g.W(g.act, done("qk", i), done("trunc", i - 2))
                t = g.A(g.act.activation(sign[i % 2], ps, ACT.Sign))
                g.W(g.dve, t, done("clip", i - NS))
                T["trunc", i] = g.V(g.dve.scalar_tensor_tensor(out=score[i % NS], in0=sign[i % 2], scalar=-HALF,
                                                               in1=ps, op0=OP.mult, op1=OP.add))
            i = step
            if new:
                s, b, h, kt = tiles[i]
                if i == per:
                    g.W(g.pe, T["projected", "qk1"])
                g.W(g.pe, done("trunc", i - 3 if i >= 3 else (-2, -1, -3)[i]))
                T["qk", i] = g.E(g.pe.matmul(s_bank[i % 3], kT[s][:, b * S + kt * P:b * S + (kt + 1) * P],
                                             q[s][h][:, half(b)], start=True, stop=True))
            u, on = head_due("sum")
            if on:
                g.W(g.pe, done("add", u * nk + nk - 1), done("norm", (u - 2) * nk + nk - 1))
                for j in range(4):
                    mm = g.pe.matmul(r_bank[u % 2][:, j:j + 1], total[u % 2][:, j * P:(j + 1) * P], step_col,
                                     start=True, stop=True)
                T["sum", u] = g.E(mm)
            u, on = head_due("R")
            if on:
                g.W(g.pe, done("diag", u))
                T["R", u] = g.E(g.pe.matmul(r_bank[u % 2], g.ones[:, :], diag[u % 2], start=True, stop=True))
            i, on = due("pv")
            if on and tiles[i % n_t][2] == 1 and i % 2 == 1:
                s, b, h, kt = tiles[i % n_t]
                if i == nk + 1:
                    g.W(g.pe, T["projected", "v0"])
                if i == per + nk + 1:
                    g.W(g.pe, T["projected", "v1"])
                g.W(g.pe, done("conv", i), done("out", i - kt - nk - 1))
                for k2 in (kt - 1, kt):
                    for h2 in range(nh):
                        j = i - kt + k2 - nk * (1 - h2)
                        mm = g.pe.matmul(o_bank[h2 * rows:(h2 + 1) * rows, :],
                                         v[s][:, b, k2, h2 * rows:(h2 + 1) * rows], attn[j % NA],
                                         start=k2 == 0, stop=k2 == nk - 1)
                t = g.E(mm)
                for j in (i, i - 1, i - nk, i - nk - 1):
                    T["pv", j] = t
        for key in list(running):
            for _ in running[key]:
                pass
        if new and fetch_odd:
            g.W(g.pe, t_odd)

    wsrc = a["w_L2_attn"]

    def fetch(ch, s, group):
        def go(after=None):
            g.W(g.sp, after)
            return g.dma(ch, weights[s], wsrc[group])
        return go
    t = [fetch(g.d_w, 0, 0)(), fetch(g.d_w2, 1, 1)()]
    g.V(g.dve.memset(step_col, 1.0 / FX))
    g.V(g.dve.memset(minus_half, -HALF))
    for s in range(2):
        for h in range(nh):
            z = g.G(g.pool.memset(q[s][h], 0.0))
    g.W(g.dve, z)
    g.W(g.pe, t, g.now("dve"))
    chunk.psum_free, chunk.free = [None] * 2, [None] * 2
    for _ in chunks(0, QK, lambda: None):
        pass
    g.W(g.pe, g.projected)
    body(0, False, True, fetch(g.d_w, 0, 2), fetch(g.d_w2, 1, 3))
    with g.fori(G // 2 - 1) as i:
        body(2 * i + 2, True, True, fetch(g.d_st, 0, 2 * i + 4), fetch(g.d_st2, 1, 2 * i + 5))
    wo = view(w, 0, G, D)
    tw = load(g, g.d_w, wo, a["wo_L2_attn"])
    body(G, True, False)
    return wo, tw


def l2_attn(g):
    norm_for(g)
    g.meet()
    oT = view(g.WB, 0, 8, NT)
    wo, tw = fixed_attention(g, oT)
    g.W(g.pe, tw, g.now("act"))
    y, z = view(g.work, 8 * 1024, 2, NT), view(g.work, 10 * 1024, 2, NT)
    g.meet()
    g.ring = [None] * 4

    def ev(m, ps, t):
        g.W(g.act, t)
        t = t0 = g.A(g.act.activation(y[:, m, :], ps, ACT.Identity, bias=vcol(g, "L2_attn_b_proj", m)))
        t = fixed_in_place(g, y[:, m, :], z[:, m, :], NT, t, FX)
        g.W(g.dve, t)
        t = g.V(g.dve.tensor_tensor(g.X[:, m, :], g.X[:, m, :], y[:, m, :], OP.add))
        g.resid = [t, t]
        return t0
    project(g, wo, oT, 8, DC, ev, None)


def l2_xattn(g):
    norm_for(g)
    oT = mha(g, "L2_xattn")
    out_project(g, "L2_xattn", oT, g.WA, "L2_xattn_wo_b", None)


def l2_ffn(g):
    a, w, K = g.a, g.work, 1024
    M = 64
    Bt = g.WB
    win, w1, w2, wo = view(Bt, 0, 2, M), view(Bt, 128, FF), view(Bt, 1200, FC, M), view(Bt, 1800, D)
    load(g, g.d_w, win, a["l2f_win"])
    load(g, g.d_w, w1[0:M], a["l2f_w1"])
    load(g, g.d_w, w2, a["l2f_w2"])
    tw = load(g, g.d_w, wo[0:M], a["l2f_wout"])
    t1 = norm_for(g)
    s = view(w, 3 * K, NT)
    hid = view(w, 4 * K, FC, NT)
    g2 = view(w, 12 * K, NT)
    g.W(g.pe, tw)

    def thin(wT, rhs, kts, dst, bias, ready):
        i, ps = slot(g)
        for n in range(B):
            g.W(g.pe, ready)
            for k in range(kts):
                mm = g.pe.matmul(ps[0:M, half(n)], wT[:, k, :], rhs[:, k, half(n)], start=k == 0, stop=k == kts - 1)
        t = g.E(mm)
        g.W(g.act, t)
        t = g.ring[i] = g.A(g.act.activation(dst[0:M], ps[0:M], ACT.Identity, bias=vcol(g, bias)[0:M]))
        return t
    t = thin(win, g.Hn, DC, s, "L2_ffn_bin_", t1)
    for m in range(FC):
        i, ps = slot(g)
        g.W(g.pe, t)
        for n in range(B):
            mm = g.pe.matmul(ps[:, half(n)], w1[0:M, m * P:(m + 1) * P], s[0:M, half(n)], start=True, stop=True)
        tp = g.E(mm)
        g.W(g.act, tp)
        th = g.ring[i] = g.A(g.act.activation(hid[:, m, :], ps, ACT.Relu, bias=vcol(g, "L2_ffn_b1", m)))
    t = thin(w2, hid, FC, g2, "L2_ffn_b2", th)
    ev = add_resid(g, "L2_ffn_bout")
    for m in range(DC):
        i, ps = slot(g)
        g.W(g.pe, t)
        for n in range(B):
            mm = g.pe.matmul(ps[:, half(n)], wo[0:M, m * P:(m + 1) * P], g2[0:M, half(n)], start=True, stop=True)
        g.ring[i] = ev(m, ps, g.E(mm))


def l3_attn(g):
    norm_for(g)
    oT = mha(g, "L3_attn")
    out_project(g, "L3_attn", oT, g.WB, "L3_attn_b_proj", None)


def l3_xattn(g):
    norm_for(g)
    oT = mha(g, "L3_xattn")
    out_project(g, "L3_xattn", oT, g.WB, "L3_xattn_bo", None)


def ternary(g, src, dst, tmp, sc, ready):
    n = P * 2048
    am, s, inv, al = (sc[:, i:i + 1] for i in range(4))
    g.W(g.dve, ready)
    t = g.V(g.dve.tensor_reduce(am, src, AX.X, OP.add, apply_absolute_value=True))
    g.W(g.pool, t)
    t = g.G(g.pool.partition_all_reduce(al, am, P, bass.bass_isa.ReduceOp.add))
    g.W(g.dve, t)
    t = g.V(g.dve.tensor_scalar(s, al, 1.0 / n, 1e-8, OP.mult, OP.max))
    g.W(g.dve, t)
    t = g.V(g.dve.reciprocal(inv, s))
    g.W(g.dve, t)
    t = g.V(g.dve.tensor_scalar(tmp, src, inv, ROUND, OP.mult, OP.add))
    g.W(g.dve, t)
    t = g.V(g.dve.tensor_scalar(tmp, tmp, ROUND, 1.0, OP.subtract, OP.min))
    g.W(g.dve, t)
    return g.V(g.dve.tensor_scalar(dst, tmp, -1.0, None, OP.max))


def l3_ffn(g):
    a, w, K = g.a, g.work, 1024
    A = g.WA
    tw = load(g, g.d_w, A[:, 0:4096], a["w_l3_ffn"])
    W1, W2 = A[:, 0:2048], A[:, 2048:4096]
    sc = [view(g.small, 4 * i, 4) for i in range(2)]
    tw1 = ternary(g, W1, W1, A[:, 4096:6144], sc[0], tw)
    tw2 = ternary(g, W2, W2, A[:, 6144:8192], sc[1], tw)
    t1 = norm_for(g)
    hid = view(w, 4 * K, FC, NT)

    def ev1(m, ps, t):
        g.W(g.act, t)
        return g.A(g.act.activation(hid[:, m, :], ps, ACT.Gelu, bias=vcol(g, "L3_ffn_b1", m)))
    g.W(g.pe, tw1)
    th = project(g, W1.rearrange("p (c f) -> p c f", c=2), g.Hn, DC, FC, ev1, t1)
    g.W(g.pe, tw2)
    project(g, W2.rearrange("p (c f) -> p c f", c=FC), hid, FC, DC, add_resid(g, "L3_ffn_b2"), th[-1])


STAGES = [l0_attn, l0_xattn, l0_ffn, l1_attn, l1_xattn, l1_ffn, l2_attn, l2_xattn, l2_ffn, l3_attn, l3_xattn, l3_ffn]



def kxm(w):
    k, m = w.shape
    return np.ascontiguousarray(w.reshape(k // P, P, m).transpose(1, 0, 2))


def head_pack(w, rows, dh):
    k = w.shape[0]
    out = np.zeros((k, H, rows), w.dtype)
    out[:, :, :dh] = w.reshape(k, H, dh)
    return out.reshape(k, H * rows)


def lay_out(i):
    f = np.float32
    o = {}
    o["xT"] = np.ascontiguousarray(i["x"].reshape(NT, D).T)
    o["ctx_keys"] = np.ascontiguousarray(i["ctx_1024"].reshape(B * S2, D))
    o["ctxT"] = np.ascontiguousarray(o["ctx_keys"].T)
    o["ident"] = np.eye(P, dtype=f)
    o["blockdiag"] = np.kron(np.eye(P // 16, dtype=f), np.ones((16, 16), f))
    vec = dict(i)
    for j in range(4):
        vec[f"cw{j}"] = i["L0_attn_conv_w"][:, 0, j]
    vec["gamma"] = np.repeat(i["L0_attn_gamma_attn"].reshape(H), D // H)
    vec["L2_ffn_b1"] = i["L2_ffn_b1"].reshape(FF)
    V = np.zeros((P, NVEC), f)
    for n in VEC256:
        V[:, VCOL[n]:VCOL[n] + 2] = vec[n].reshape(2, P).T
    for n in VEC1024:
        V[:, VCOL[n]:VCOL[n] + 8] = vec[n].reshape(8, P).T
    for n in ("L2_ffn_bin_", "L2_ffn_b2"):
        V[:64, VCOL[n]] = vec[n]
    for n in ("L0_ffn_scale", "L3_attn_temperature"):
        V[:, VCOL[n]] = vec[n][0]
    o["vecs"] = V

    def packs(*ws):
        return np.concatenate([kxm(np.ascontiguousarray(w)).reshape(P, -1) for w in ws], axis=1)
    o["w_l0_attn"] = packs(*(i["L0_attn_" + n].T for n in ("qk_w", "v_w", "g_w", "o_w", "gate_w", "up_w", "down_w")))
    idx = np.linspace(0.0, 1.0, D // H, dtype=f)
    freqs = (f(10.0) ** idx)[None, :] * np.arange(H, dtype=f)[:, None]
    ang = np.arange(S, dtype=f)[:, None] * freqs.reshape(1, D)
    o["cos"] = np.ascontiguousarray(np.cos(ang.astype(np.float64)).astype(f).T)
    o["l0f_AT"] = np.ascontiguousarray(i["L0_ffn_A"].transpose(2, 0, 1).reshape(R_, E_ * L_))
    o["l0f_B"] = np.ascontiguousarray(i["L0_ffn_B"].transpose(1, 0, 2))
    o["l0f_gate"] = kxm(i["L0_ffn_w_gate"])
    o["l0f_wt"] = kxm(np.ascontiguousarray(i["L0_ffn_wt_w"].T))
    o["l0f_wd"] = kxm(np.ascontiguousarray(i["L0_ffn_wd_w"].T))
    o["l0f_wtb"] = i["L0_ffn_wt_b"]
    o["rank"] = np.tile(np.arange(E_, 0, -1, dtype=f), (P, 1))
    o["w_l1_attn"] = packs(*(i["L1_attn_W_" + n].T for n in "kvro"))
    o["w_l1_xattn"] = packs(i["L1_xattn_W0"].T, i["L1_xattn_W1"].T)
    o["mask1"] = np.ascontiguousarray(i["mask_BxS2_if1"])
    o["w_l1_ffn"] = packs(i["L1_ffn_w1"].T, i["L1_ffn_w2"].T)
    o["w_l3_ffn"] = packs(i["L3_ffn_W1"].T, i["L3_ffn_W2"].T)
    o["group"] = np.ascontiguousarray(i["fside_BxSxS2_0"])
    o["mask2"] = np.ascontiguousarray(i["mask_BxSxS2_ik1"])
    z1024 = np.zeros(1024, f)
    M = 64
    o["l2f_win"] = kxm(i["L2_ffn_Win"])
    w1, w2 = np.zeros((M, M, 16), f), np.zeros((M, 16, M), f)
    for m in range(M):
        w1[m, m], w2[m, :, m] = i["L2_ffn_W1"][m], i["L2_ffn_W2"][m]
    o["l2f_w1"] = w1.reshape(M, FF)
    o["l2f_w2"] = kxm(w2.reshape(FF, M))
    o["l2f_wout"] = np.ascontiguousarray(i["L2_ffn_Wout"])
    wqkv = i["L2_attn_w_qkv"].reshape(3, 1024, D)
    wa, ba = i["L3_attn_W_attn"].reshape(D, 3, D), i["L3_attn_b_attn"].reshape(3, D)
    heads = {
        "L2_attn": ([wqkv[j].T for j in range(3)], [z1024] * 3, i["L2_attn_w_proj"].T),
        "L2_xattn": ([i[f"L2_xattn_w{n}_k"] for n in "qkv"], [i[f"L2_xattn_w{n}_b"] for n in "qkv"], i["L2_xattn_wo_k"]),
        "L3_attn": ([wa[:, j] for j in range(3)], [ba[j] for j in range(3)], i["L3_attn_W_proj"]),
        "L3_xattn": ([i["L3_xattn_W" + n].T for n in "qkv"], [i["L3_xattn_b" + n] for n in "qkv"], i["L3_xattn_Wo"].T),
    }
    for n, (ws, bs, wo) in heads.items():
        G, rows, dh = MHA[n]["groups"], MHA[n]["rows"], MHA[n]["dh"]
        wp = [kxm(head_pack(w, rows, dh)).reshape(P, DC, G, P) for w in ws]
        ahead = 2 if n == "L2_attn" else 0
        o["w_" + n] = np.zeros((G + ahead, P, 3 * DC * P), f)
        o["w_" + n][:G] = np.stack(wp).transpose(3, 1, 0, 2, 4).reshape(G, P, 3 * DC * P)
        bp = [head_pack(b[None], rows, dh).reshape(G, P) for b in bs]
        o["bqk_" + n] = np.ascontiguousarray(np.stack(bp[:2], axis=2))
        o["bv_" + n] = np.ascontiguousarray(bp[2])
        o["wo_" + n] = kxm(np.ascontiguousarray(head_pack(np.ascontiguousarray(wo.T), rows, dh).T))
    j = np.arange(S)[None, :] - (S - P) - np.arange(P)[:, None]
    o["rel"] = np.where(j <= 0, j, -1e30).astype(f)
    o["causal"] = np.where(j <= 0, 0, -1e30).astype(f)
    start = 2.0 ** (-2.0 ** (-(np.log2(H) - 3)))
    o["slopes"] = np.array([start * start ** h for h in range(H)], f).reshape(4, 4)
    return o


def kernel(**inputs):
    import concourse.bacc as bacc
    from concourse.bass_utils import run_bass_kernel_spmd

    arrays = lay_out({k: np.asarray(v) for k, v in inputs.items()})
    nc = bacc.Bacc("TRN2", target_bir_lowering=False, num_devices=1)
    a = {n: nc.dram_tensor("in_" + n, x.shape, mybir.dt.from_np(x.dtype), kind="ExternalInput").ap()
         for n, x in arrays.items()}
    a["out"] = nc.dram_tensor("out_x", (D, NT), F32, kind="ExternalOutput").ap()
    decoder(nc, a, range(len(STAGES)))
    r = run_bass_kernel_spmd(nc, [{"in_" + k: v for k, v in arrays.items()}], core_ids=[0])
    return np.ascontiguousarray(r.results[0]["out_x"].T).reshape(B, S, D)
```

```python
from contextlib import ExitStack, contextmanager

import concourse.bass as bass
import concourse.mybir as mybir
import numpy as np
from concourse.alu_op_type import AluOpType as OP

ACT = mybir.ActivationFunctionType
AX = mybir.AxisListType
F32 = mybir.dt.float32
BF16 = mybir.dt.bfloat16
I32 = mybir.dt.int32

B, S, D, S2 = 2, 512, 256, 1024
NT = B * S
P = 128
DC = D // P
FF = 1024
FC = FF // P
H = 16
E_, L_, R_ = 6, 100, 16
LN_EPS = 1e-5
BIG = 1e30
FMIN = float(np.finfo(np.float32).min)
ROUND = 12582912.0
FX = 4096.0
FXMAX = 8 * FX - 1
HALF = 0.49998

VEC256 = ["L0_attn_ln1_w", "L0_attn_ln1_b", "L0_attn_conv_b", "L0_attn_g_b", "L0_attn_onorm_w",
          "L0_attn_onorm_b", "L0_attn_ln2_w", "L0_attn_ln2_b", "L0_attn_gamma1", "L0_attn_gamma2",
          "cw0", "cw1", "cw2", "cw3", "gamma", "L0_ffn_wd_b",
          "L1_attn_time_mix_k", "L1_attn_time_mix_v", "L1_attn_time_mix_r", "L1_attn_time_decay",
          "L1_attn_time_first", "L1_ffn_b2", "L2_attn_b_proj", "L2_xattn_wo_b", "L2_ffn_bout",
          "L3_attn_b_proj", "L3_xattn_bo", "L3_ffn_b2"]
VEC1024 = ["L1_ffn_b1", "L2_ffn_b1", "L3_ffn_b1"]
VCOL, _n = {}, 0
for _v in VEC256:
    VCOL[_v] = _n
    _n += 2
for _v in VEC1024:
    VCOL[_v] = _n
    _n += 8
for _v in ("L2_ffn_bin_", "L2_ffn_b2", "L0_ffn_scale", "L3_attn_temperature"):
    VCOL[_v] = _n
    _n += 1
NVEC = _n

MHA = {
    "L2_attn": dict(groups=8, heads=2, rows=64, dh=64, keys=S, causal=False, kind="fixed"),
    "L2_xattn": dict(groups=4, heads=4, rows=32, dh=16, keys=S2, causal=False, kind="grouped"),
    "L3_attn": dict(groups=4, heads=4, rows=32, dh=16, keys=S, causal=True, kind="alibi"),
    "L3_xattn": dict(groups=8, heads=2, rows=64, dh=64, keys=S, causal=True, kind="causal"),
}


class Tok:

    def __init__(self, ch, n):
        self.ch, self.n = ch, n


class Chan:

    def __init__(self, nc, ctx, name, step=1):
        self.sem, self.step, self.n, self.name = ctx.enter_context(nc.semaphore(name)), step, 0, name


class Prog:

    def __init__(self, nc, ctx, aps):
        self.nc, self.ctx, self.a = nc, ctx, aps
        self.pe, self.dve, self.act, self.pool, self.sp = nc.tensor, nc.vector, nc.scalar, nc.gpsimd, nc.sync
        self.c = {n: Chan(nc, ctx, "s_" + n) for n in ("pe", "dve", "act", "pool")}
        self.inner = {n: Chan(nc, ctx, "l_" + n) for n in ("pe", "dve", "act", "pool")}
        self.d_st = Chan(nc, ctx, "l_dma", 16)
        self.d_st2 = Chan(nc, ctx, "l_dma_2", 16)
        self.waited = {}

    def mark(self, eng, ins):
        ch = self.c[eng]
        ins.then_inc(ch.sem, 1)
        ch.n += 1
        return Tok(ch, ch.n)

    def E(self, ins):
        return self.mark("pe", ins)

    def V(self, ins):
        return self.mark("dve", ins)

    def A(self, ins):
        return self.mark("act", ins)

    def G(self, ins):
        return self.mark("pool", ins)

    def dma_chan(self, name):
        return Chan(self.nc, self.ctx, "d_" + name, 16)

    def dma(self, ch, out, in_, eng=None):
        (eng or self.sp).dma_start(out, in_).then_inc(ch.sem, 16)
        ch.n += 16
        return Tok(ch, ch.n)

    def W(self, eng, *toks):
        todo = list(toks)
        last = {}
        while todo:
            t = todo.pop()
            if isinstance(t, (list, tuple)):
                todo += t
            elif t is not None and t.n > last.get(t.ch.name, (0,))[0]:
                last[t.ch.name] = t.n, t.ch
        for name, (n, ch) in last.items():
            if n > self.waited.get((id(eng), name), 0):
                self.waited[id(eng), name] = n
                eng.wait_ge(ch.sem, n)

    def now(self, *names):
        return [Tok(self.c[n], self.c[n].n) for n in names if self.c[n].n]

    def meet(self, *dma):
        toks = self.now("pe", "dve", "act", "pool")
        for eng in (self.pe, self.dve, self.act, self.pool, self.sp):
            self.W(eng, toks, *dma)

    @contextmanager
    def fori(self, trips):
        self.meet()
        outer, outer_waited, self.c = self.c, self.waited, self.inner
        with self.nc.Fori(0, trips) as i:
            self.waited = {}
            every = list(self.inner.values()) + [self.d_st, self.d_st2]
            for ch in every:
                ch.n = 0
            yield i
            self.meet()
            self.nc.all_engine_barrier(sems_to_clear=range(every[0].sem.num, every[-1].sem.num + 1))
        self.c, self.waited = outer, outer_waited
        self.ring = [None] * 4


def view(t, off, *dims):
    n = int(np.prod(dims))
    ap = t[:, off:off + n]
    if len(dims) == 1:
        return ap
    names = "abcd"[:len(dims)]
    pat = "p (" + " ".join(names) + ") -> p " + " ".join(names)
    return ap.rearrange(pat, **{k: v for k, v in zip(names[1:], dims[1:])})


def decoder(nc, a, stages):
    ctx = ExitStack()
    with ctx:
        def sb(name, cols, dt=F32):
            return ctx.enter_context(nc.sbuf_tensor(name, [P, cols], dt))

        g = Prog(nc, ctx, a)
        g.X = view(sb("resid", DC * NT), 0, DC, NT)
        g.Hn = view(sb("normed", DC * NT), 0, DC, NT)
        g.ctxK = view(sb("ctx_keys", 16 * D), 0, 16, D)
        g.ctxT = view(sb("ctx_feat", DC * B * S2), 0, DC, B * S2)
        g.WA = sb("arena_a", 8192)
        g.WB = sb("arena_b", 8192)
        g.work = sb("work", 19 * 1024)
        g.wst = sb("head_weights", 3 * DC * P + P + 8)
        g.wst2 = sb("head_weights_2", 3 * DC * P + P + 8)
        g.extra = sb("extra", 2048)
        g.vec = sb("vecs", NVEC)
        g.one = sb("mean_matrix", P)
        g.ones = sb("ones_matrix", P)
        g.iden = sb("identity", P)
        g.small = sb("small", 256)
        g.ps = ctx.enter_context(nc.psum_tensor("ps", [P, 4096], F32))
        g.ring = [None] * 4
        g.ring_i = 0

        g.d_in = g.dma_chan("in")
        g.d_ctx = g.dma_chan("ctx")
        g.d_w = g.dma_chan("w")
        g.d_w2 = g.dma_chan("w2")
        g.d_out = g.dma_chan("out")
        g.d_scr = g.dma_chan("scratch")

        g.dma(g.d_in, g.vec[:, :], a["vecs"])
        g.dma(g.d_in, g.iden[:, :], a["ident"])
        t_in = g.dma(g.d_in, g.X, a["xT"].rearrange("(c p) t -> p c t", p=P))
        g.dma(g.d_ctx, g.ctxK, a["ctx_keys"].rearrange("(k p) d -> p k d", p=P), nc.scalar)
        g.t_ctx = g.dma(g.d_ctx, g.ctxT, a["ctxT"].rearrange("(c p) t -> p c t", p=P), nc.scalar)
        g.V(nc.vector.memset(g.one[:, :], 1.0 / D))
        g.V(nc.vector.memset(g.ones[:, :], 1.0))
        const = sb("constants", 3)
        g.eps, g.ln15, g.e9 = (const[:, j:j + 1] for j in range(3))
        for ap, value in ((g.eps, LN_EPS), (g.ln15, 15 * float(np.log(2.0))), (g.e9, 1e-9)):
            g.V(nc.vector.memset(ap, value))
        g.meet(t_in, g.t_ctx)
        g.resid = [t_in, t_in]

        for s in stages:
            STAGES[s](g)
            g.meet()
            g.ring = [None] * 4

        t_out = g.dma(g.d_out, a["out"].rearrange("(c p) t -> p c t", p=P), g.X)
        g.W(nc.sync, t_out)



def vcol(g, name, c=0):
    return g.vec[:, VCOL[name] + c:VCOL[name] + c + 1]


def slot(g):
    i = g.ring_i
    g.ring_i = (i + 1) % 4
    g.W(g.pe, g.ring[i])
    return i, g.ps[:, i * 1024:(i + 1) * 1024]


def half(n):
    return slice(n * S, (n + 1) * S)


def layernorm(g, src, dst, ready, sq, tmp, w=None, b=None, put=None):
    one = g.one[:, :]
    im, mean = slot(g)
    iv, var = slot(g)
    t1 = []
    for n in range(B):
        g.W(g.pe, ready[n])
        for c in range(DC):
            mm = g.pe.matmul(mean[:, half(n)], one, src[:, c, half(n)], start=c == 0, stop=c == DC - 1)
        t1.append(g.E(mm))
    t2 = []
    for n in range(B):
        g.W(g.dve, t1[n], ready[n])
        for c in range(DC):
            t = g.V(g.dve.tensor_tensor(dst[:, c, half(n)], src[:, c, half(n)], mean[:, half(n)], OP.subtract))
        t2.append(t)
    g.ring[im] = t2[-1]
    t3 = []
    for n in range(B):
        g.W(g.act, t2[n])
        t3.append(g.A(g.act.activation(sq[:, :, half(n)], dst[:, :, half(n)], ACT.Square)))
    t4 = []
    for n in range(B):
        g.W(g.pe, t3[n])
        for c in range(DC):
            mm = g.pe.matmul(var[:, half(n)], one, sq[:, c, half(n)], start=c == 0, stop=c == DC - 1)
        t4.append(g.E(mm))
    t6 = []
    for n in range(B):
        g.W(g.act, t4[n])
        t5 = g.A(g.act.activation(tmp[:, half(n)], var[:, half(n)], ACT.Ln, bias=g.eps))
        g.W(g.act, t5)
        t6.append(g.A(g.act.activation(tmp[:, half(n)], tmp[:, half(n)], ACT.Exp, scale=-0.5)))
    g.ring[iv] = t6[-1]
    out = []
    for n in range(B):
        g.W(g.dve, t6[n])
        for c in range(DC):
            last = w is None
            o = put(c, n) if last and put is not None else dst[:, c, half(n)]
            t = g.V(g.dve.tensor_tensor(o, dst[:, c, half(n)], tmp[:, half(n)], OP.mult))
            if not last:
                g.W(g.dve, t)
                o = put(c, n) if put is not None else dst[:, c, half(n)]
                t = g.V(g.dve.tensor_scalar(o, dst[:, c, half(n)], vcol(g, w, c), vcol(g, b, c), OP.mult, OP.add))
        out.append(t)
    return tuple(out)


def project(g, wT, src, kts, mts, evac, ready, src_ap=None):
    out = []
    for m in range(mts):
        i, ps = slot(g)
        for n in range(B):
            g.W(g.pe, ready[n] if isinstance(ready, tuple) else ready)
            for k in range(kts):
                rhs = src_ap(k, n) if src_ap else src[:, k, half(n)]
                mm = g.pe.matmul(ps[:, half(n)], wT[:, k, m * P:(m + 1) * P], rhs, start=k == 0, stop=k == kts - 1)
        t = g.E(mm)
        g.ring[i] = evac(m, ps, t)
        out.append(g.ring[i])
    return out


def add_resid(g, bias=None, scale=None):
    toks = []

    def evac(m, ps, t):
        g.W(g.dve, t)
        if bias is None:
            t = g.V(g.dve.tensor_tensor(g.X[:, m, :], ps, g.X[:, m, :], OP.add))
        else:
            t = g.V(g.dve.scalar_tensor_tensor(out=g.X[:, m, :], in0=ps, scalar=vcol(g, bias, m),
                                               in1=g.X[:, m, :], op0=OP.add, op1=OP.add))
        g.resid = [t, t]
        return t
    return evac


def load(g, ch, dst, src, *after):
    g.W(g.sp, *after)
    return g.dma(ch, dst, src)



def l0_attn(g):
    a = g.a
    A, Bt, w = g.WA, g.WB, g.work
    tw = load(g, g.d_w, A[:, :], a["w_l0_attn"])
    W = {n: view(A, i * 512, 2, 256) for i, n in enumerate(("qk", "v", "g", "o"))}
    Wg, Wu, Wd = view(A, 2048, 2, FF), view(A, 4096, 2, FF), view(A, 6144, FC, D)
    cosT = view(Bt, 0, 2, S)
    tcos = load(g, g.d_w2, cosT, a["cos"].rearrange("(c p) t -> p c t", p=P))
    blk = view(Bt, 1024, P)
    tcos = load(g, g.d_w2, blk, a["blockdiag"])
    K = 1024
    tmp, sq = view(w, 0, NT), view(w, K, 2, NT)
    hin = view(w, 3 * K, 2, NT)
    hpad = view(Bt, 2048, 2, B, S + 3)
    xc = view(w, 5 * K, 2, B, S)
    kk, v, gate = view(w, 7 * K, 2, NT), view(w, 9 * K, 2, NT), view(w, 11 * K, 2, NT)
    dec, rdec = view(w, 13 * K, 2, S), view(w, 14 * K, 2, S)
    ones, gam = view(w, 15 * K, S), view(w, 15 * K + S, S)
    cs = view(w, 16 * K, 2, B, S)

    t1 = layernorm(g, g.X, hin, g.resid, sq, tmp)
    z = g.G(g.pool.memset(hpad[:, :, :, 0:3], 0.0))
    t2 = layernorm(g, hin, g.Hn, t1, sq, tmp, "L0_attn_ln1_w", "L0_attn_ln1_b",
                   put=lambda c, n: hpad[:, c, n, 3:])
    g.W(g.dve, z)
    tx = []
    for c in range(DC):
        g.W(g.dve, t2)
        t = g.V(g.dve.tensor_scalar(xc[:, c], hpad[:, c, :, 0:S], vcol(g, "cw0", c), vcol(g, "L0_attn_conv_b", c),
                                    OP.mult, OP.add))
        for j in range(1, 4):
            g.W(g.dve, t)
            t = g.V(g.dve.scalar_tensor_tensor(out=xc[:, c], in0=hpad[:, c, :, j:j + S], scalar=vcol(g, f"cw{j}", c),
                                               in1=xc[:, c], op0=OP.mult, op1=OP.add))
        tx.append(t)
    t = g.V(g.dve.memset(ones, 1.0))
    g.W(g.dve, t)
    td = []
    for c in range(DC):
        t = g.V(g.dve.tensor_scalar(gam, ones, vcol(g, "gamma", c), None, OP.mult))
        m = g.V(g.dve.memset(dec[:, c, 0:1], 1.0))
        g.W(g.dve, t, m)
        t = g.V(g.dve.tensor_tensor_scan(dec[:, c, 1:S], gam[:, 1:S], ones[:, 1:S], 1.0, OP.mult, OP.mult))
        g.W(g.dve, t)
        td.append(t)
    t = g.V(g.dve.tensor_scalar(rdec, dec, 1e-6, None, OP.add))
    g.W(g.dve, t)
    trd = g.V(g.dve.reciprocal(rdec, rdec))
    xcf = xc.rearrange("p c b s -> p c (b s)")
    g.W(g.pe, tw, tcos)

    def ev_qk(m, ps, t):
        g.W(g.act, t)
        g.A(g.act.activation(kk[:, m, :], ps, ACT.Copy))
        return g.A(g.act.activation(sq[:, m, :], ps, ACT.Square))
    tq = project(g, W["qk"], xcf, DC, DC, ev_qk, tx[-1])

    def ev_v(m, ps, t):
        g.W(g.act, t)
        return g.A(g.act.activation(v[:, m, :], ps, ACT.Copy))
    tv = project(g, W["v"], xcf, DC, DC, ev_v, tx[-1])
    for m in range(DC):
        i, ps = slot(g)
        g.W(g.pe, tq[m])
        for n in range(B):
            mm = g.pe.matmul(ps[:, half(n)], blk, sq[:, m, half(n)], start=True, stop=True)
        t = g.E(mm)
        g.W(g.dve, t)
        t = g.V(g.dve.tensor_scalar(tmp, ps, 1e-24, None, OP.max))
        g.ring[i] = t
        g.W(g.act, t)
        t = g.A(g.act.activation(tmp, tmp, ACT.Ln, scale=2.0 ** 30))
        g.W(g.act, t)
        t = g.A(g.act.activation(tmp, tmp, ACT.Exp, scale=-0.5, bias=g.ln15))
        g.W(g.dve, t)
        tk = g.V(g.dve.tensor_tensor(kk[:, m, :], kk[:, m, :], tmp, OP.mult))
        g.W(g.dve, tk)

    def ev_g(m, ps, t):
        g.W(g.act, t)
        return g.A(g.act.activation(gate[:, m, :], ps, ACT.Sigmoid, bias=vcol(g, "L0_attn_g_b", m)))
    tg = project(g, W["g"], xcf, DC, DC, ev_g, tx[-1])
    g.W(g.dve, tcos, tv, tk)
    kb = kk.rearrange("p c (b s) -> p c b s", b=B)
    for c in range(DC):
        for b in range(B):
            g.V(g.dve.tensor_tensor(cs[:, c, b, 1:S], cosT[:, c, 1:S], kb[:, c, b, 0:S - 1], OP.add))
            t = g.V(g.dve.tensor_copy(cs[:, c, b, 0:1], cosT[:, c, 0:1]))
    g.W(g.dve, t)
    csf = cs.rearrange("p c b s -> p c (b s)")
    t = g.V(g.dve.tensor_tensor(csf, csf, v, OP.mult))
    g.W(g.dve, t, tg)
    t = g.V(g.dve.tensor_tensor(csf, csf, gate, OP.mult))
    g.W(g.dve, t)
    for c in range(DC):
        for b in range(B):
            t = g.V(g.dve.tensor_tensor(cs[:, c, b], cs[:, c, b], dec[:, c], OP.mult))
            g.W(g.dve, t)
            t = g.V(g.dve.tensor_tensor_scan(gate[:, c, half(b)], ones, cs[:, c, b], 0.0, OP.mult, OP.add))
            g.W(g.dve, t, trd)
            t = g.V(g.dve.tensor_tensor(gate[:, c, half(b)], gate[:, c, half(b)], rdec[:, c], OP.mult))
            g.W(g.dve, t)
            t = g.V(g.dve.tensor_tensor(gate[:, c, half(b)], gate[:, c, half(b)], kk[:, c, half(b)], OP.mult))
    ao = v

    def ev_o(m, ps, t):
        g.W(g.act, t)
        return g.A(g.act.activation(ao[:, m, :], ps, ACT.Copy))
    to = project(g, W["o"], gate, DC, DC, ev_o, t)
    tn = layernorm(g, ao, g.Hn, [to[-1]] * 2, sq, tmp, "L0_attn_onorm_w", "L0_attn_onorm_b")
    x2 = hin
    g.W(g.dve, tn)
    for c in range(DC):
        t = g.V(g.dve.scalar_tensor_tensor(out=x2[:, c, :], in0=g.Hn[:, c, :], scalar=vcol(g, "L0_attn_gamma1", c),
                                           in1=x2[:, c, :], op0=OP.mult, op1=OP.add))
    h2 = view(w, 5 * K, 2, NT)
    tn = layernorm(g, x2, h2, [t, t], sq, tmp, "L0_attn_ln2_w", "L0_attn_ln2_b")
    hid = view(w, 7 * K, FC, NT)
    sil = [view(w, 15 * K, NT), view(w, 16 * K, NT)]
    ts = [None, None]
    th = None
    for m in range(FC):
        def ev_gate(_, ps, t):
            g.W(g.act, t, ts[m % 2])
            g.tsil = g.A(g.act.activation(sil[m % 2], ps, ACT.Silu))
            return g.tsil

        def ev_up(_, ps, t):
            g.W(g.dve, t, g.tsil)
            ts[m % 2] = g.V(g.dve.tensor_tensor(hid[:, m, :], ps, sil[m % 2], OP.mult))
            return ts[m % 2]
        project(g, Wg[:, :, m * P:(m + 1) * P], h2, DC, 1, ev_gate, tn)
        th = project(g, Wu[:, :, m * P:(m + 1) * P], h2, DC, 1, ev_up, tn)[0]

    def ev_d(m, ps, t):
        g.W(g.dve, t)
        t = g.V(g.dve.scalar_tensor_tensor(out=x2[:, m, :], in0=ps, scalar=vcol(g, "L0_attn_gamma2", m),
                                           in1=x2[:, m, :], op0=OP.mult, op1=OP.add))
        g.W(g.dve, t)
        t2 = g.V(g.dve.tensor_tensor(g.X[:, m, :], g.X[:, m, :], x2[:, m, :], OP.add))
        g.resid = [t2, t2]
        return t
    project(g, Wd, hid, FC, DC, ev_d, th)


def l0_xattn(g):
    w, K = g.work, 1024
    sq, tmp = view(w, 0, 2, NT), view(w, 2 * K, NT)
    hid = [view(w, (3 + 4 * b) * K, 8, S) for b in range(B)]
    t1 = layernorm(g, g.X, g.Hn, g.resid, sq, tmp)
    for b in range(B):
        for k2 in range(4):
            i, ps = slot(g)
            g.W(g.pe, t1[b])
            for j in range(2):
                kt = 2 * k2 + j
                for c in range(DC):
                    mm = g.pe.matmul(ps[:, half(j)], g.ctxT[:, c, b * S2 + kt * P:b * S2 + (kt + 1) * P],
                                     g.Hn[:, c, half(b)], start=c == 0, stop=c == DC - 1)
            t = g.E(mm)
            g.W(g.act, t)
            g.ring[i] = g.A(g.act.activation(hid[b][:, 2 * k2:2 * k2 + 2, :],
                                             ps.rearrange("p (a s) -> p a s", a=2), ACT.Gelu_apprx_tanh))
    for b in range(B):
        i, ps = slot(g)
        g.W(g.pe, g.now("act"))
        for m in range(DC):
            for kt in range(8):
                mm = g.pe.matmul(ps[:, half(m)], g.ctxK[:, b * 8 + kt, m * P:(m + 1) * P], hid[b][:, kt, :],
                                 start=kt == 0, stop=kt == 7)
        t = g.E(mm)
        g.W(g.dve, t)
        t = g.V(g.dve.tensor_tensor(g.X[:, :, half(b)], ps.rearrange("p (c s) -> p c s", c=2),
                                    g.X[:, :, half(b)], OP.add))
        g.ring[i] = t
        g.resid[b] = t


def l0_ffn(g):
    a, w, K = g.a, g.work, 1024
    Bt = g.WB
    n = E_ * L_
    AT, Bm = view(Bt, 0, n), view(Bt, 600, E_, D)
    tokg = view(Bt, 2200, 2, n + E_)
    WT, WD = view(Bt, 3500, 2, D), view(Bt, 4100, 2, D)
    wtb = view(Bt, 4700, D)
    rank = view(Bt, 5000, E_)
    val = view(Bt, 5100, E_, D)
    tw = load(g, g.d_w, AT[0:R_, :], a["l0f_AT"])
    load(g, g.d_w, Bm[0:R_], a["l0f_B"])
    load(g, g.d_w, tokg[:, :, n:n + E_], a["l0f_gate"])
    load(g, g.d_w, WT, a["l0f_wt"])
    load(g, g.d_w, WD, a["l0f_wd"])
    load(g, g.d_w, rank, a["rank"])
    tw = load(g, g.d_w, wtb, a["l0f_wtb"].partition_broadcast(P))
    sq, tmp = view(w, 0, 2, NT), view(w, 2 * K, NT)
    t1 = layernorm(g, g.X, g.Hn, g.resid, sq, tmp)
    g.W(g.pe, tw)
    for c in range(DC):
        i, ps = slot(g)
        for e in range(E_):
            o = (e * L_) if e < 5 else S
            mm = g.pe.matmul(ps[:, o:o + L_], Bm[0:R_, e, c * P:(c + 1) * P], AT[0:R_, e * L_:(e + 1) * L_],
                             start=True, stop=True)
        t = g.E(mm)
        g.W(g.dve, t)
        g.V(g.dve.tensor_copy(tokg[:, c, 0:500], ps[:, 0:500]))
        tt = g.ring[i] = g.V(g.dve.tensor_copy(tokg[:, c, 500:600], ps[:, S:S + L_]))
    g.W(g.pe, tt)
    g.W(g.dve, tw)
    for e in range(E_):
        i, ps = slot(g)
        for c in range(DC):
            mm = g.pe.matmul(ps[0:L_, 0:D], tokg[:, c, e * L_:(e + 1) * L_], WT[:, c, :], start=c == 0, stop=c == 1)
        t = g.E(mm)
        g.W(g.dve, t)
        tvl = g.ring[i] = g.V(g.dve.tensor_tensor(val[0:L_, e, :], ps[0:L_, 0:D], wtb[0:L_, :], OP.add))
    g.W(g.dve, tvl)
    tvl = g.V(g.dve.memset(val[0:1], 0.0))
    PT = view(w, 3 * K, E_, NT)
    prob = [view(w, 9 * K + 1024 * j, n) for j in range(2)]
    sm = [view(g.small, 64 * j, 64) for j in range(2)]
    tfree = [None, None]
    sfree = [None, None]
    tlast = []
    for it in range(NT // P):
        j = it % 2
        i, ps = slot(g)
        g.W(g.pe, t1[it // 4], tt)
        for o, lo, hi in ((0, 0, 500), (S, 500, n + E_)):
            for c in range(DC):
                mm = g.pe.matmul(ps[:, o:o + hi - lo], g.Hn[:, c, it * P:(it + 1) * P], tokg[:, c, lo:hi],
                                 start=c == 0, stop=c == 1)
        t = g.E(mm)
        s = sm[j]
        mx, ng, su, gr = s[:, 0:7], s[:, 8:14], s[:, 16:22], s[:, 24:30]
        eq, m2, rs = s[:, 32:38], s[:, 40:41], s[:, 48:54]
        gl = ps[:, S + L_:S + L_ + E_]
        g.W(g.dve, t, sfree[j])
        g.V(g.dve.tensor_reduce(mx[:, 0:5], ps[:, 0:500].rearrange("p (e l) -> p e l", e=5), AX.X, OP.max))
        g.V(g.dve.tensor_reduce(mx[:, 5:6], ps[:, S:S + L_], AX.X, OP.max))
        t = g.V(g.dve.tensor_reduce(mx[:, 6:7], gl, AX.X, OP.max))
        g.W(g.dve, t)
        tn = g.V(g.dve.tensor_scalar(ng, mx[:, 0:6], -1.0 / 16, None, OP.mult))
        t = g.V(g.dve.tensor_scalar(eq, gl, mx[:, 6:7], None, OP.is_equal))
        g.W(g.dve, t)
        t = g.V(g.dve.tensor_tensor(eq, eq, rank, OP.mult))
        g.W(g.dve, t)
        t = g.V(g.dve.tensor_reduce(m2, eq, AX.X, OP.max))
        g.W(g.dve, t)
        tgt = g.V(g.dve.tensor_scalar(eq, eq, m2, None, OP.is_equal))
        g.W(g.act, tn, tgt, tfree[j])
        for e in range(E_):
            o = e * L_ if e < 5 else S
            te = g.A(g.act.activation(prob[j][:, e * L_:(e + 1) * L_], ps[:, o:o + L_], ACT.Exp, scale=1.0 / 16,
                                      bias=ng[:, e:e + 1], accum_out=su[:, e:e + 1]))
        g.ring[i] = te
        g.W(g.dve, te, tgt)
        t = g.V(g.dve.reciprocal(rs, su))
        g.W(g.dve, t)
        t = g.V(g.dve.tensor_tensor(gr, rs, eq, OP.mult))
        g.W(g.dve, t)
        pr = prob[j].rearrange("p (e l) -> p e l", e=E_)
        tp = sfree[j] = g.V(g.dve.tensor_tensor(pr, pr, gr.unsqueeze(2).broadcast_to([P, E_, L_]), OP.mult))
        i2, ps2 = slot(g)
        g.W(g.pe, tp)
        for e in range(E_):
            mm = g.pe.transpose(ps2[0:L_, e * P:(e + 1) * P], pr[:, e, :], g.iden[:, :])
        t = tfree[j] = g.E(mm)
        g.W(g.act, t)
        t = g.ring[i2] = g.A(g.act.activation(PT[0:L_, :, it * P:(it + 1) * P],
                                              ps2[0:L_, 0:E_ * P].rearrange("p (e t) -> p e t", e=E_), ACT.Copy))
        tlast.append(t)
    zb = view(w, 12 * K, 2, NT)
    g.W(g.pe, tvl)
    tz = []
    for n_ in range(B):
        i, ps = slot(g)
        g.W(g.pe, tlast[4 * n_ + 3])
        for m in range(DC):
            for e in range(E_):
                mm = g.pe.matmul(ps[:, half(m)], val[0:L_, e, m * P:(m + 1) * P], PT[0:L_, e, half(n_)],
                                 start=e == 0, stop=e == E_ - 1)
        t = g.E(mm)
        g.W(g.dve, t)
        t = g.ring[i] = g.V(g.dve.tensor_tensor(zb[:, :, half(n_)], ps.rearrange("p (c s) -> p c s", c=2),
                                                g.Hn[:, :, half(n_)], OP.add))
        tz.append(t)
    sb_ = view(g.small, 192, 2)
    t = g.V(g.dve.tensor_scalar(sb_, g.vec[:, VCOL["L0_ffn_wd_b"]:VCOL["L0_ffn_wd_b"] + 2], vcol(g, "L0_ffn_scale"),
                                None, OP.mult))
    ex, gd = view(w, 14 * K, 2, NT), view(w, 16 * K, 2, NT)

    def ev(m, ps, t2):
        g.W(g.act, t2, t)
        te = g.A(g.act.activation(ex[:, m, :], ps, ACT.Exp, scale=vcol(g, "L0_ffn_scale"), bias=sb_[:, m:m + 1]))
        g.W(g.dve, te)
        u = g.V(g.dve.tensor_scalar(gd[:, m, :], ex[:, m, :], 0.0, float(np.finfo(np.float32).eps),
                                    OP.is_equal, OP.mult))
        g.W(g.dve, u)
        u = g.V(g.dve.tensor_tensor(ex[:, m, :], ex[:, m, :], gd[:, m, :], OP.add))
        g.W(g.act, u)
        u = g.A(g.act.activation(ex[:, m, :], ex[:, m, :], ACT.Ln))
        v_ = g.V(g.dve.tensor_tensor(g.X[:, m, :], g.X[:, m, :], g.Hn[:, m, :], OP.add))
        g.W(g.dve, u, v_)
        u = g.V(g.dve.tensor_tensor(g.X[:, m, :], g.X[:, m, :], ex[:, m, :], OP.add))
        g.resid = [u, u]
        return te
    project(g, WD, zb, DC, DC, ev, tuple(tz))



def l1_attn(g):
    a, w, K = g.a, g.work, 1024
    A, Bt = g.WA, g.WB
    tw = load(g, g.d_w, Bt[:, 0:2048], a["w_l1_attn"])
    W = {n: view(Bt, i * 512, 2, 256) for i, n in enumerate(("k", "v", "r", "o"))}
    hp = view(Bt, 2048, 2, B, S + 1)
    sq, tmp = view(w, 0, 2, NT), view(w, 2 * K, NT)
    z = g.G(g.pool.memset(hp[:, :, :, 0:1], 0.0))
    t1 = layernorm(g, g.X, g.Hn, g.resid, sq, tmp, put=lambda c, n: hp[:, c, n, 1:])
    om = view(g.small, 0, 8)
    mixed = {"k": view(w, 0, 2, B, S), "v": view(w, 3 * K, 2, B, S), "r": view(w, 5 * K, 2, B, S)}
    g.W(g.dve, z, t1)
    tm = {}
    for q, n in enumerate("kvr"):
        col = VCOL["L1_attn_time_mix_" + n]
        t = g.V(g.dve.tensor_scalar(om[:, 2 * q:2 * q + 2], g.vec[:, col:col + 2], -1.0, 1.0, OP.mult, OP.add))
        for c in range(DC):
            t2 = g.V(g.dve.tensor_scalar(mixed[n][:, c], hp[:, c, :, 1:], vcol(g, "L1_attn_time_mix_" + n, c), None,
                                         OP.mult))
            g.W(g.dve, t, t2)
            tm[n] = g.V(g.dve.scalar_tensor_tensor(out=mixed[n][:, c], in0=hp[:, c, :, 0:S],
                                                   scalar=om[:, 2 * q + c:2 * q + c + 1], in1=mixed[n][:, c],
                                                   op0=OP.mult, op1=OP.add))
    k, v, r = (view(w, o * K, 2, NT) for o in (7, 9, 11))
    flat = {n: x.rearrange("p c b s -> p c (b s)") for n, x in mixed.items()}
    g.W(g.pe, tw)

    def copy_to(dst, func=ACT.Copy):
        def ev(m, ps, t):
            g.W(g.act, t)
            return g.A(g.act.activation(dst[:, m, :], ps, func))
        return ev
    tk = project(g, W["k"], flat["k"], DC, DC, copy_to(k), tm["k"])
    tv = project(g, W["v"], flat["v"], DC, DC, copy_to(v), tm["v"])
    tr = project(g, W["r"], flat["r"], DC, DC, copy_to(r, ACT.Sigmoid), tm["r"])
    pb = view(A, 0, 2, B, S + 1)
    qb = view(A, 2100, 2, B, S + 1)
    wb = view(w, 13 * K, S)
    ones = view(w, 13 * K + S, S)
    t = g.V(g.dve.memset(ones, 1.0))
    t0 = g.V(g.dve.memset(pb[:, :, :, 0:1], -BIG))
    t0 = g.V(g.dve.memset(qb[:, :, :, 0:1], 0.0))
    g.W(g.dve, t, t0, tk)
    for c in range(DC):
        t = g.V(g.dve.tensor_scalar(wb, ones, vcol(g, "L1_attn_time_decay", c), None, OP.mult))
        g.W(g.dve, t)
        for b in range(B):
            t = g.V(g.dve.tensor_tensor_scan(pb[:, c, b, 1:], wb, k[:, c, half(b)], -BIG, OP.add, OP.max))
        g.W(g.dve, t)
    tp = t
    uk, mx, so, sc = (view(w, o * K, 2, B, S) for o in (0, 3, 5, 14))
    sp, sn = view(A, 4200, 2, B, S), view(g.WB, 4200 - 100, 2, B, S)
    kb = k.rearrange("p c (b s) -> p c b s", b=B)
    vb = v.rearrange("p c (b s) -> p c b s", b=B)
    g.W(g.dve, g.now("pe"))

    def clamp_exp(dst, t):
        g.W(g.dve, t)
        t = g.V(g.dve.tensor_scalar(dst, dst, -30.0, None, OP.max))
        g.W(g.act, t)
        return g.A(g.act.activation(dst, dst, ACT.Exp))
    te = []
    for c in range(DC):
        p0, p1 = pb[:, c, :, 0:S], pb[:, c, :, 1:]
        t = g.V(g.dve.scalar_tensor_tensor(out=sp[:, c], in0=p0, scalar=vcol(g, "L1_attn_time_decay", c),
                                           in1=p1, op0=OP.add, op1=OP.subtract))
        t1_ = g.V(g.dve.tensor_tensor(sn[:, c], kb[:, c], p1, OP.subtract))
        te.append(clamp_exp(sp[:, c], t))
        te.append(clamp_exp(sn[:, c], t1_))
        t = g.V(g.dve.tensor_scalar(uk[:, c], kb[:, c], vcol(g, "L1_attn_time_first", c), None, OP.add))
        g.W(g.dve, t)
        t = g.V(g.dve.tensor_tensor(mx[:, c], p0, uk[:, c], OP.max))
        g.W(g.dve, t)
        t = g.V(g.dve.tensor_tensor(so[:, c], p0, mx[:, c], OP.subtract))
        t1_ = g.V(g.dve.tensor_tensor(sc[:, c], uk[:, c], mx[:, c], OP.subtract))
        te.append(clamp_exp(so[:, c], t))
        te.append(clamp_exp(sc[:, c], t1_))
    g.W(g.dve, te, tv)
    for c in range(DC):
        t = g.V(g.dve.tensor_tensor(sn[:, c], sn[:, c], vb[:, c], OP.mult))
        g.W(g.dve, t)
        for b in range(B):
            tq = g.V(g.dve.tensor_tensor_scan(qb[:, c, b, 1:], sp[:, c, b], sn[:, c, b], 0.0, OP.mult, OP.add))
        t = g.V(g.dve.tensor_tensor(mx[:, c], so[:, c], sc[:, c], OP.add))
        g.W(g.act, t)
        t = g.A(g.act.activation(uk[:, c], mx[:, c], ACT.Ln, bias=g.e9))
        g.W(g.act, t)
        t5 = g.A(g.act.activation(uk[:, c], uk[:, c], ACT.Exp, scale=-1.0))
        g.W(g.dve, tq)
        t = g.V(g.dve.tensor_tensor(so[:, c], so[:, c], qb[:, c, :, 0:S], OP.mult))
        t2 = g.V(g.dve.tensor_tensor(sc[:, c], sc[:, c], vb[:, c], OP.mult))
        g.W(g.dve, t2)
        t = g.V(g.dve.tensor_tensor(so[:, c], so[:, c], sc[:, c], OP.add))
        g.W(g.dve, t, t5)
        t = g.V(g.dve.tensor_tensor(so[:, c], so[:, c], uk[:, c], OP.mult))
        g.W(g.dve, t, tr)
        t = g.V(g.dve.tensor_tensor(so[:, c], so[:, c], r[:, c].rearrange("p (b s) -> p b s", b=B), OP.mult))
    project(g, W["o"], so.rearrange("p c b s -> p c (b s)"), DC, DC, add_resid(g), t)


def l1_xattn(g):
    a, w, K = g.a, g.work, 1024
    A, Bt = g.WA, g.WB
    tw = load(g, g.d_w, Bt[:, 0:1024], a["w_l1_xattn"])
    W = [view(Bt, 0, 2, D), view(Bt, 512, 2, D)]
    mraw, madd = view(Bt, 1024, B, S2).bitcast(I32), view(Bt, 1024 + 2 * K, B, S2)
    tmk = load(g, g.d_w2, mraw, a["mask1"].partition_broadcast(P))
    sq, tmp = view(w, 0, 2, NT), view(w, 2 * K, NT)
    u = view(w, 3 * K, 2, NT)
    tu = list(layernorm(g, g.X, u, g.resid, sq, tmp))
    g.W(g.dve, tmk)
    tmk = g.V(g.dve.tensor_scalar(madd, mraw, 0.0, FMIN, OP.is_equal, OP.mult))
    key = view(w, 5 * K, 2, NT)
    prob = [view(w, (7 + j) * K, S2) for j in range(4)]
    PT = [view(w, 11 * K, 8, S), view(w, 15 * K, 8, S)]
    sm = view(g.small, 0, 64)
    g.W(g.dve, tmk)
    g.W(g.pe, tw)
    pfree, ptfree, n_u = [None] * 4, [None] * 2, 0
    for hop in range(2):
        def ev(m, ps, t):
            g.W(g.act, t)
            return g.A(g.act.activation(key[:, m, :], ps, ACT.Copy))
        tk = project(g, W[hop], u, DC, DC, ev, tuple(tu))
        g.W(g.pe, tk)
        for b in range(B):
            for qt in range(4):
                j = n_u % 4
                i, ps = slot(g)
                q0 = b * S + qt * P
                for hf in range(2):
                    for c in range(DC):
                        mm = g.pe.matmul(ps[:, half(hf)], key[:, c, q0:q0 + P],
                                         g.ctxT[:, c, b * S2 + hf * S:b * S2 + (hf + 1) * S], start=c == 0, stop=c == 1)
                t = g.E(mm)
                nm, su, rs = (sm[:, o + j:o + j + 1] for o in (0, 8, 16))
                g.W(g.dve, t, pfree[j])
                t = g.ring[i] = g.V(g.dve.tensor_tensor_reduce(prob[j], ps, madd[:, b, :], -1.0, BIG * 3e8, OP.add,
                                                               OP.min, nm))
                g.W(g.act, t)
                t = g.A(g.act.activation(prob[j], prob[j], ACT.Exp, scale=-1.0, bias=nm, accum_out=su))
                g.W(g.dve, t)
                t = g.V(g.dve.reciprocal(rs, su))
                g.W(g.dve, t)
                t = g.V(g.dve.tensor_scalar(prob[j], prob[j], rs, None, OP.mult))
                i, ps = slot(g)
                g.W(g.pe, t)
                for kt in range(8):
                    mm = g.pe.transpose(ps[:, kt * P:(kt + 1) * P], prob[j][:, kt * P:(kt + 1) * P], g.iden[:, :])
                pfree[j] = t = g.E(mm)
                g.W(g.act, t, ptfree[b])
                tpt = g.ring[i] = g.A(g.act.activation(PT[b][:, :, qt * P:(qt + 1) * P],
                                                       ps.rearrange("p (k t) -> p k t", k=8), ACT.Copy))
                n_u += 1
            i, ps = slot(g)
            g.W(g.pe, tpt)
            for m in range(DC):
                for kt in range(8):
                    mm = g.pe.matmul(ps[:, half(m)], g.ctxK[:, b * 8 + kt, m * P:(m + 1) * P], PT[b][:, kt, :],
                                     start=kt == 0, stop=kt == 7)
            t = ptfree[b] = g.E(mm)
            g.W(g.dve, t)
            t = g.ring[i] = g.V(g.dve.tensor_tensor(u[:, :, half(b)], ps.rearrange("p (c s) -> p c s", c=2),
                                                    u[:, :, half(b)], OP.add))
            tu[b] = t
    g.W(g.dve, tu)
    t = g.V(g.dve.tensor_tensor(g.X, g.X, u, OP.add))
    g.resid = [t, t]


def quantize(g, src, dst, tmp, sc, ready, engine=None):
    am, s, inv, al = (sc[:, i:i + 1] for i in range(4))
    g.W(g.dve, ready)
    t = g.V(g.dve.tensor_reduce(am, src, AX.X, OP.max, apply_absolute_value=True))
    g.W(g.pool, t)
    t = g.G(g.pool.partition_all_reduce(al, am, P, bass.bass_isa.ReduceOp.max))
    g.W(g.dve, t)
    t = g.V(g.dve.tensor_scalar(s, al, 1e-6, 1.0 / 127, OP.max, OP.mult))
    g.W(g.dve, t)
    t = g.V(g.dve.reciprocal(inv, s))
    g.W(g.dve, t)
    t = g.V(g.dve.tensor_scalar(tmp, src, inv, ROUND, OP.mult, OP.add))
    g.W(g.dve, t)
    return g.V(g.dve.tensor_scalar(dst, tmp, ROUND, None, OP.subtract))


def l1_ffn(g):
    a, w, K = g.a, g.work, 1024
    A, Bt = g.WA, g.WB
    tw = load(g, g.d_w, A[:, 0:4096], a["w_l1_ffn"])
    W1, W2 = A[:, 0:2048], A[:, 2048:4096]
    W1q = view(A, 4096, K).bitcast(BF16)
    W2q = view(A, 4096 + K, K).bitcast(BF16)
    tb = Bt[:, 0:8192]
    sc = [view(g.small, 4 * i, 4) for i in range(4)]
    tw1 = quantize(g, W1, W1q, tb[:, 0:2048], sc[0], tw)
    tw2 = quantize(g, W2, W2q, tb[:, 2048:4096], sc[1], tw)
    sq, tmp = view(w, 0, 2, NT), view(w, 2 * K, NT)
    t1 = layernorm(g, g.X, g.Hn, g.resid, sq, tmp)
    hq = view(w, 3 * K, K).bitcast(BF16)
    tx = quantize(g, g.Hn.rearrange("p c t -> p (c t)"), hq, tb[:, 4096:6144], sc[2], t1)
    ss = view(g.small, 32, 2)
    b1s, b2s = view(g.small, 40, 8), view(g.small, 50, 2)
    g.W(g.dve, tx, tw2)
    t = g.V(g.dve.tensor_tensor(ss[:, 0:1], sc[0][:, 1:2], sc[2][:, 1:2], OP.mult))
    g.W(g.dve, t)
    col = VCOL["L1_ffn_b1"]
    tb1 = g.V(g.dve.tensor_scalar(b1s, g.vec[:, col:col + 8], ss[:, 0:1], None, OP.mult))
    hid = view(w, 4 * K, FC, NT)

    def ev1(m, ps, t):
        g.W(g.act, t, tb1)
        return g.A(g.act.activation(hid[:, m, :], ps, ACT.Gelu, scale=ss[:, 0:1], bias=b1s[:, m:m + 1]))
    th = project(g, W1q.rearrange("p (c f) -> p c f", c=2), hq.rearrange("p (c t) -> p c t", c=2), DC, FC, ev1,
                 [tx, tw1])
    hf = hid.rearrange("p c t -> p (c t)")
    hidq = view(w, 12 * K, 4 * K).bitcast(BF16)
    tq = quantize(g, hf, hidq, tb, sc[3], th)
    t = g.V(g.dve.tensor_tensor(ss[:, 1:2], sc[1][:, 1:2], sc[3][:, 1:2], OP.mult))
    g.W(g.dve, t)
    col = VCOL["L1_ffn_b2"]
    t = g.V(g.dve.tensor_scalar(b2s, g.vec[:, col:col + 2], ss[:, 1:2], None, OP.mult))
    g.W(g.dve, t)
    o = view(w, 0, 2, NT)

    def ev2(m, ps, t):
        g.W(g.dve, t)
        t = g.V(g.dve.tensor_scalar(o[:, m, :], ps, ss[:, 1:2], b2s[:, m:m + 1], OP.mult, OP.add))
        g.W(g.dve, t)
        t2 = g.V(g.dve.tensor_tensor(g.X[:, m, :], g.X[:, m, :], o[:, m, :], OP.add))
        g.resid = [t2, t2]
        return t
    project(g, W2q.rearrange("p (c f) -> p c f", c=FC), hidq.rearrange("p (c t) -> p c t", c=FC), FC, DC, ev2,
            [tq, tw2])



def norm_for(g):
    w, K = g.work, 1024
    return layernorm(g, g.X, g.Hn, g.resid, view(w, 0, 2, NT), view(w, 2 * K, NT))


def fixed_in_place(g, x, tmp, n_cols, t, pre):
    g.W(g.dve, t)
    t = g.V(g.dve.tensor_scalar(x, x, pre, FXMAX, OP.mult, OP.min))
    g.W(g.dve, t)
    t = g.V(g.dve.tensor_scalar(x, x, -FXMAX, None, OP.max))
    g.W(g.act, t)
    t = g.A(g.act.activation(tmp, x, ACT.Sign))
    g.W(g.dve, t)
    ti = tmp.bitcast(I32)
    t = g.V(g.dve.scalar_tensor_tensor(out=ti, in0=tmp, scalar=-HALF, in1=x, op0=OP.mult, op1=OP.add))
    g.W(g.dve, t)
    return g.V(g.dve.tensor_scalar(x, ti, 1.0 / FX, None, OP.mult))


class Stages:
    pass


ATTEND_AGE = dict(scores=0, max=1, exp=2, mult=3, turn=4, pv=5, put=6, finish=7)


def attend(g, c, old, new, hook=None):
    T, n_u = {}, c.units
    done = lambda name, i: T.get((name, i))

    def due(stage):
        i = step - ATTEND_AGE[stage]
        return i, (new if i >= 0 else old) and i < n_u
    n_turn = [0]
    for step in range(n_u if new else ATTEND_AGE["finish"]):
        if hook:
            hook(step, T, done)
        i, on = due("exp")
        if on:
            p = c.prob[i % c.NP][:, 0:c.keys(i)]
            g.W(g.act, done("max", i))
            T["exp", i] = g.A(g.act.activation(p, p, ACT.Exp, scale=-1.0, bias=c.minmax[:, i % 8:i % 8 + 1],
                                               accum_out=c.sums[:, i % 8:i % 8 + 1]))
        i, on = due("put")
        if on:
            g.W(g.act, done("pv", i), done("mult", i))
            T["put", i] = g.A(g.act.activation(c.out(i), c.o_psum[i % 2][:, 0:c.dh], ACT.Copy,
                                               scale=c.recip[:, i % 8:i % 8 + 1]))
        i, on = due("mult")
        if on:
            g.W(g.dve, done("exp", i), done("put", i - 8))
            T["mult", i] = g.V(g.dve.reciprocal(c.recip[:, i % 8:i % 8 + 1], c.sums[:, i % 8:i % 8 + 1]))
            if c.mult is not None:
                p = c.prob[i % c.NP][:, 0:c.keys(i)]
                T["mult", i] = g.V(g.dve.tensor_tensor(p, p, c.mult(i), OP.mult))
        i, on = due("max")
        if on:
            n = c.keys(i)
            g.W(g.dve, done("scores", i), done("turn", i - c.NP), done("exp", i - 8))
            T["max", i] = g.V(g.dve.tensor_tensor_reduce(c.prob[i % c.NP][:, 0:n], c.s_psum[i % c.NS][:, 0:n], c.add(i),
                                                         -1.0, BIG * 3e8, OP.add, OP.min,
                                                         c.minmax[:, i % 8:i % 8 + 1]))
        i, on = due("scores")
        if on:
            g.W(g.pe, done("max", i - c.NS))
            T["scores", i] = g.E(c.scores(i, c.s_psum[i % c.NS], T))
        i, on = due("turn")
        if on:
            n = c.keys(i)
            g.W(g.pe, done("mult", i) or done("exp", i))
            for o in range(0, n, S):
                z = n_turn[0] % 2
                n_turn[0] += 1
                nt = (min(n, o + S) - o) // P
                g.W(g.pe, T.get(("turn_free", z)))
                for kt in range(nt):
                    mm = g.pe.transpose(c.t_psum[z][:, kt * P:(kt + 1) * P],
                                        c.prob[i % c.NP][:, o + kt * P:o + (kt + 1) * P], g.iden[:, :])
                t = T["turn", i] = g.E(mm)
                dst = c.PT[i % 2][:, o // P:o // P + nt, :].rearrange("p k t -> p (k t)")
                g.W(g.act, t, done("pv", i - 2))
                T["turn_free", z] = T["turned", i] = g.A(g.act.activation(dst, c.t_psum[z][:, 0:nt * P], ACT.Copy))
        i, on = due("finish")
        if on and c.finish and c.finish(i):
            tile, dst = c.finish(i)
            z = n_turn[0] % 2
            n_turn[0] += 1
            g.W(g.pe, done("put", i), T.get(("turn_free", z)))
            for qt in range(4):
                mm = g.pe.transpose(c.t_psum[z][:, qt * P:(qt + 1) * P], tile[:, qt, :], g.iden[:, :])
            g.W(g.act, g.E(mm))
            T["turn_free", z] = g.A(g.act.activation(dst, c.t_psum[z], ACT.Copy))
        i, on = due("pv")
        if on:
            nt = c.keys(i) // P
            g.W(g.pe, done("turned", i), done("put", i - 2))
            if c.before_v:
                c.before_v(i, T)
            for kt in range(nt):
                mm = g.pe.matmul(c.o_psum[i % 2][:, 0:c.dh], c.PT[i % 2][:, kt, :], c.v(i, kt),
                                 start=kt == 0, stop=kt == nt - 1)
            T["pv", i] = g.E(mm)
    return T


def thin_heads(g, name):
    a, w, K = g.a, g.work, 1024
    grouped = name == "L2_xattn"
    keys, causal = (S2, False) if grouped else (S, True)
    nk, NK, dh = keys // P, B * keys, D // H
    src = g.ctxT if grouped else g.Hn
    ROWS = 6 * dh
    scr_q = g.nc.dram_tensor("parts_q_" + name, (3, D + dh, NT), BF16, kind="Internal").ap()
    scr_k = g.nc.dram_tensor("parts_k_" + name, (3, D + dh, NK), BF16, kind="Internal").ap()
    W = [view(g.extra, 512 * j, 2, D) for j in range(4)]
    bv, bqk = g.wst[:, 0:D], g.wst[:, D:D + 4]
    load(g, g.d_w, g.extra[:, 0:2048], a["w_" + name])
    load(g, g.d_w, bqk, a["bqk_" + name])
    tw = load(g, g.d_w, bv, a["bv_" + name].partition_broadcast(P))
    if grouped:
        G, NEG = view(g.WA, 0, B, 4, S2), view(g.WB, 0, B, 4, S2)
        tG = load(g, g.d_w2, G, a["group"].rearrange("b (q p) k -> p b q k", p=P))
        tG = load(g, g.d_w2, NEG.bitcast(I32), a["mask2"].rearrange("b (q p) k -> p b q k", p=P))
        scale = 0.25
    else:
        rel = view(g.WB, 0, S)
        bias = [view(g.WB, (1 + z) * S, S) for z in range(2)]
        slope = [g.small[:, 64 + z:65 + z] for z in range(2)]
        tG = load(g, g.d_w2, rel, a["rel"])
        rt = view(g.small, 100, 1)
        t = g.V(g.dve.reciprocal(rt, vcol(g, "L3_attn_temperature")))
        g.W(g.dve, t)
        scale = rt
        g.W(g.dve, g.V(g.dve.tensor_scalar(rt, rt, 0.25, None, OP.mult)))
    v = view(w, 0, B * nk, D)
    t_ln = norm_for_at(g, 4 * K)
    g.W(g.pe, tw)
    g.W(g.dve, tw)

    QP = view(w, 7 * K, 3, DC, NT // 2).bitcast(BF16)
    KP = view(w, 10 * K, 3, DC, NK // 2).bitcast(BF16)
    g.ring = [None] * 4
    rest = [view(w, 4 * K + j * S, S) for j in range(6)]
    rest_free = [None] * 3
    n_c = 0
    t_parts = {}
    for part, wj, x, n_tok, dst in (("q", 0, g.Hn, NT, QP), ("k", 1, src, NK, KP)):
        for m in range(DC):
            for t0 in range(0, n_tok, S):
                z = n_c % 3
                n_c += 1
                i, ps = slot(g)
                if x is g.Hn:
                    g.W(g.pe, t_ln[t0 // S])
                for c in range(DC):
                    mm = g.pe.matmul(ps[:, 0:S], W[wj][:, c, m * P:(m + 1) * P], x[:, c, t0:t0 + S], start=c == 0,
                                     stop=c == 1)
                g.W(g.act, g.E(mm))
                g.W(g.act, rest_free[z])
                y, r = rest[2 * z], rest[2 * z + 1]
                hi, mid, lo = (dst[:, j, m, t0:t0 + S] for j in range(3))
                col = bqk[:, 2 * wj + m:2 * wj + m + 1]
                if part == "q":
                    g.W(g.dve, g.now("pe"), rest_free[z])
                    t = g.V(g.dve.tensor_scalar(y, ps[:, 0:S], col, scale, OP.add, OP.mult))
                else:
                    t = g.A(g.act.activation(y, ps[:, 0:S], ACT.Identity, bias=col))
                g.ring[i] = t
                g.W(g.act, t)
                t = g.A(g.act.activation(hi, y, ACT.Copy))
                g.W(g.dve, t)
                t = g.V(g.dve.tensor_tensor(r, y, hi, OP.subtract))
                g.W(g.pool, t)
                t = g.G(g.pool.tensor_scalar(mid, r, 1.0, 0.0, OP.mult, OP.add))
                g.W(g.dve, t)
                t = rest_free[z] = g.V(g.dve.tensor_tensor(lo, r, mid, OP.subtract))
                t_parts[part] = t
        scr = scr_q if part == "q" else scr_k
        g.W(g.sp, t_parts[part])
        for j in range(3):
            g.dma(g.d_scr, scr[j, 0:D].rearrange("(c p) t -> p c t", p=P), dst[:, j])
            t_scr = g.dma(g.d_scr, scr[j, D:D + dh], dst[0:dh, j, 0])
    if grouped:
        g.W(g.dve, tG)
        nf = NEG.rearrange("p b q k -> p (b q k)")
        t = g.V(g.dve.tensor_scalar(nf, nf.bitcast(I32), -1.0, 1.0, OP.mult, OP.add))
        g.W(g.dve, t)
        t = g.V(g.dve.tensor_scalar(nf, nf, -1e9, None, OP.mult))
        g.W(g.dve, t)
    for k0 in range(0, B * nk, 4):
        i, ps = slot(g)
        for j in range(4):
            for c in range(DC):
                mm = g.pe.matmul(ps[:, j * D:(j + 1) * D], src[:, c, (k0 + j) * P:(k0 + j + 1) * P], W[2][:, c, :],
                                 start=c == 0, stop=c == 1)
        g.W(g.dve, g.E(mm))
        tv = g.ring[i] = g.V(g.dve.tensor_tensor(v[:, k0:k0 + 4, :], ps.rearrange("p (k d) -> p k d", k=4),
                                                 bv.unsqueeze(1).broadcast_to([P, 4, D]), OP.add))
    g.meet(t_scr, tG)

    qs = [view(w, 4 * K + z * S, S).bitcast(BF16) for z in range(2)]
    ks = [view(w, (5 + z) * K, K).bitcast(BF16) for z in range(2)]
    vh = [view(g.wst2, 256 * z, B * nk, dh) for z in range(2)]
    O = view(w, 7 * K, 8, D)
    c = Stages()
    c.units, c.NP, c.NS, c.dh, c.finish = 2 * B * 4, 8, 2048 // keys, dh, None
    c.prob = [view(w, (9 + j) * K, keys) for j in range(8)]
    c.PT = [view(w, (17 + j) * K, nk, P) for j in range(2)]
    c.s_psum = [g.ps[:, z * keys:(z + 1) * keys] for z in range(c.NS)]
    c.t_psum = [g.ps[:, (4 + z) * S:(5 + z) * S] for z in range(2)]
    c.o_psum = [g.ps[:, (6 + z) * S:(7 + z) * S] for z in range(2)]
    c.minmax, c.sums, c.recip = (g.small[:, 8 * j:8 * j + 8] for j in range(3))
    where = lambda i: (i % 16 // 8, i % 8 // 4, i % 4)
    c.keys = lambda i: (i % 4 + 1) * P if causal else keys

    def fetch(ch, z, head):
        f0 = head * dh
        for blk, jq, jk in ((0, 0, 0), (1, 1, 0), (2, 2, 0), (3, 0, 1), (4, 1, 1), (5, 0, 2)):
            r = slice(blk * dh, (blk + 1) * dh)
            g.dma(ch, qs[z][r, 0:NT], scr_q[jq, bass.ds(f0, dh), :])
            t = g.dma(ch, ks[z][r, 0:NK], scr_k[jk, bass.ds(f0, dh), :])
        if not grouped:
            t = g.dma(ch, slope[z], a["slopes"][bass.ds(head, 1)].partition_broadcast(P))
        return t

    def iteration(pair, old, new, ch0=None, ch1=None):
        if grouped:
            c.add = lambda i: NEG[:, where(i)[1], where(i)[2], :]
            c.mult = lambda i: G[:, where(i)[1], where(i)[2], :]
        else:
            c.add = lambda i: bias[where(i)[0]][:, S - c.keys(i):S]
            c.mult = None

        def scores(i, ps, T):
            h, b, qt = where(i)
            n = c.keys(i)
            q0 = b * S + qt * P
            if i == 8:
                g.W(g.pe, T["set1"])
            for o in range(0, n, S):
                e_ = min(n, o + S)
                mm = g.pe.matmul(ps[:, o:e_], qs[h][0:ROWS, q0:q0 + P], ks[h][0:ROWS, b * keys + o:b * keys + e_],
                                 start=True, stop=True)
            return mm
        c.scores = scores
        c.v = lambda i, kt: vh[where(i)[0]][:, where(i)[1] * nk + kt, :]

        def before_v(i, T):
            if i in (0, 8):
                g.W(g.pe, T["vh", where(i)[0]])
        c.before_v = before_v

        def out(i):
            h, b, qt = where(i)
            head = (2 * pair if i >= 0 else 2 * pair - 2) + h
            return O[:, b * 4 + qt, bass.ds(head * dh, dh)]
        c.out = out

        def hook(step, T, done):
            if not new:
                return
            if step == 0:
                T["set1"] = fetch(ch1, 1, 2 * pair + 1)
            if step == 2 and not grouped:
                g.W(g.pool, T["set1"], done("max", -1))
                T["bias1"] = g.G(g.pool.tensor_scalar(bias[1], rel, slope[1], 1.0, OP.mult, OP.mult))
            if step == 9 and not grouped:
                g.W(g.dve, T["bias1"])
            if step in (0, 6):
                z = int(step == 6)
                g.W(g.act, done("pv", -1))
                T["vh", z] = g.A(g.act.activation(vh[z], v[:, :, bass.ds((2 * pair + z) * dh, dh)], ACT.Copy))
            if step == 9:
                g.W(g.sp, done("scores", 7), T.get("bias1"), first_bias if not old else None)
                T["set0"] = fetch(ch0, 0, 2 * pair + 2)
            if step == 12 and not grouped:
                g.W(g.pool, T["set0"], done("max", 7))
                T["bias0"] = g.G(g.pool.tensor_scalar(bias[0], rel, slope[0], 1.0, OP.mult, OP.mult))
        T = attend(g, c, old, new, hook)
        if new:
            g.W(g.pe, T["set0"])
    g.W(g.sp, t_scr)
    t0 = fetch(g.d_w, 0, 0)
    g.W(g.pe, t0)
    first_bias = None
    if not grouped:
        g.W(g.pool, t0)
        first_bias = g.G(g.pool.tensor_scalar(bias[0], rel, slope[0], 1.0, OP.mult, OP.mult))
        g.W(g.dve, first_bias)
    iteration(0, False, True, g.d_w, g.d_w2)
    with g.fori(H // 2 - 1) as i:
        iteration(i + 1, True, True, g.d_st, g.d_st2)
    iteration(H // 2, True, False)

    g.meet()
    oT = view(w, 9 * K, DC, NT)
    for m in range(DC):
        i, ps = slot(g)
        for qt in range(8):
            mm = g.pe.transpose(ps[:, qt * P:(qt + 1) * P], O[:, qt, m * P:(m + 1) * P], g.iden[:, :])
        g.W(g.act, g.E(mm))
        t = g.ring[i] = g.A(g.act.activation(oT[:, m, :], ps, ACT.Copy))
    project(g, W[3], oT, DC, DC, add_resid(g, name + ("_wo_b" if grouped else "_b_proj")), t)


def wide_heads(g, name):
    a, w, K = g.a, g.work, 1024
    nh, rows, nk, G = 2, 64, S // P, MHA[name]["groups"]
    q = [[view(w, (4 * s + h) * K, NT) for h in range(nh)] for s in range(2)]
    kT = [view(w, (4 * s + 2) * K, NT) for s in range(2)]
    v = [view(w, (4 * s + 3) * K, B, nk, P) for s in range(2)]
    O = [[view(w, 8 * K + (2 * s + b) * S, 4, P) for b in range(B)] for s in range(2)]
    weights = [g.wst[:, 0:898], g.wst2[:, 0:898]]
    causal, wo, oT = view(g.WB, 0, S), view(g.WB, S, G, D), view(g.WA, 0, G, NT)
    c = Stages()
    c.units, c.NP, c.NS, c.dh, c.before_v, c.mult = 2 * B * nh * 4, 8, 2, 64, None, None
    c.prob = [view(w, 10 * K + j * S, S) for j in range(8)]
    c.PT = [view(w, 14 * K + j * S, nk, P) for j in range(2)]
    bank = [g.ps[:, z * S:(z + 1) * S] for z in range(8)]
    c.s_psum, c.t_psum, c.o_psum, p_bank = bank[0:2], bank[2:4], bank[4:6], bank[6:8]
    c.minmax, c.sums, c.recip = (g.small[:, 8 * j:8 * j + 8] for j in range(3))
    units = [(s, b, h, qt) for s in range(2) for b in range(B) for h in range(nh) for qt in range(4)]
    per = c.units // 2
    c.keys = lambda i: (i % 4 + 1) * P
    c.add = lambda i: causal[:, S - c.keys(i):S]

    def fetch(ch, s, group, *after):
        g.W(g.sp, *after)
        return g.dma(ch, weights[s], a["w_" + name][group])

    def project_group(s, T):
        W = [view(weights[s], 256 * j, 2, P) for j in range(3)]
        bv, bqk = weights[s][:, 768:896], weights[s][:, 896:898]
        free, out = [None] * 2, []
        for n_c, (what, n) in enumerate([("q", 0), ("k", 0), ("q", 1), ("k", 1), ("v", 0), ("v", 1)]):
            ps = p_bank[n_c % 2]
            g.W(g.pe, free[n_c % 2])
            if what == "v":
                for j in range(4):
                    for x in range(DC):
                        k0 = n * S2 + j * P
                        mm = g.pe.matmul(ps[:, j * P:(j + 1) * P], g.ctxT[:, x, k0:k0 + P], W[2][:, x, :],
                                         start=x == 0, stop=x == 1)
            else:
                src, t0 = (g.Hn, n * S) if what == "q" else (g.ctxT, n * S2)
                for x in range(DC):
                    mm = g.pe.matmul(ps, W[what == "k"][:, x, :], src[:, x, t0:t0 + S], start=x == 0, stop=x == 1)
            t = g.E(mm)
            yield
            if what == "q":
                g.W(g.dve, t)
                for h in range(nh):
                    r = slice(h * rows, (h + 1) * rows)
                    t = g.V(g.dve.tensor_scalar(q[s][h][r, half(n)], ps[r], bqk[r, 0:1], 0.125, OP.add, OP.mult))
            elif what == "k":
                g.W(g.act, t)
                t = g.A(g.act.activation(kT[s][:, half(n)], ps, ACT.Identity, bias=bqk[:, 1:2]))
            else:
                g.W(g.dve, t)
                t = g.V(g.dve.tensor_tensor(v[s][:, n], ps.rearrange("p (k d) -> p k d", k=4),
                                            bv.unsqueeze(1).broadcast_to([P, 4, P]), OP.add))
            free[n_c % 2] = t
            out.append(t)
            yield
        T["projected", s] = out

    def iteration(first, old, new, ch0=None, ch1=None):
        running = []

        def scores(i, ps, T):
            s, b, h, qt = units[i]
            n, q0 = c.keys(i), b * S + qt * P
            if i == per:
                g.W(g.pe, T["projected", 1])
            return g.pe.matmul(ps[:, 0:n], q[s][h][:, q0:q0 + P], kT[s][:, b * S:b * S + n], start=True, stop=True)
        c.scores = scores
        c.v = lambda i, kt: v[units[i % c.units][0]][:, units[i % c.units][1], kt,
                                                     units[i % c.units][2] * rows:(units[i % c.units][2] + 1) * rows]

        def out(i):
            s, b, h, qt = units[i % c.units]
            return O[s][b][:, qt, h * rows:(h + 1) * rows]
        c.out = out

        def finish(i):
            s, b, h, qt = units[i % c.units]
            if (h, qt) != (1, 3):
                return None
            return O[s][b], oT[:, (first if i >= 0 else first - 2) + s, half(b)]
        c.finish = finish

        def hook(step, T, done):
            if not new:
                return
            if step == 0:
                T["w0"] = fetch(ch0, 0, first + 2, g.now("pe", "dve", "act"))
                running.append(project_group(1, T))
            if step == per:
                T["w1"] = fetch(ch1, 1, first + 3, g.now("pe", "dve", "act"))
                g.W(g.pe, T["w0"])
                g.W(g.dve, T["w0"])
                g.W(g.act, T["w0"])
                running.append(project_group(0, T))
                g.W(g.dve, done("scores", per - 1))
                g.W(g.act, done("scores", per - 1))
            if step == 6:
                g.W(g.dve, done("pv", -1))
            if step == per + 6:
                g.W(g.dve, done("pv", per - 1))
            for r in list(running):
                if next(r, "end") == "end":
                    running.remove(r)
        T = attend(g, c, old, new, hook)
        if new:
            for e in (g.pe, g.dve, g.act):
                g.W(e, T["w1"])
        for r in running:
            for _ in r:
                pass

    tc = load(g, g.d_w2, causal, a["causal"])
    tw = load(g, g.d_w2, wo, a["wo_" + name])
    t0, t1 = fetch(g.d_w, 0, 0), fetch(g.d_scr, 1, 1)
    tn = layernorm(g, g.X, g.Hn, g.resid, view(w, 12 * K, 2, NT), view(w, 14 * K, NT))
    for s in range(2):
        for h in range(nh):
            z = g.G(g.pool.memset(q[s][h], 0.0))
    g.meet(tn, tw, t0, t1)
    first_group = {}
    for _ in project_group(0, first_group):
        pass
    g.W(g.pe, first_group["projected", 0])
    iteration(0, False, True, g.d_w, g.d_w2)
    with g.fori(G // 2 - 1) as i:
        iteration(2 * i + 2, True, True, g.d_st, g.d_st2)
    iteration(G, True, False)
    g.ring = [None] * 4
    g.W(g.pe, g.now("act", "dve"))
    project(g, wo, oT, G, DC, add_resid(g, name + "_bo"), None)


def norm_for_at(g, off):
    w, K = g.work, 1024
    return layernorm(g, g.X, g.Hn, g.resid, view(w, off, 2, NT), view(w, off + 2 * K, NT))


def fixed_attention(g, oT):
    a, w, K, A = g.a, g.work, 1024, g.WA
    nh, rows, nk, G = 2, 64, S // P, MHA["L2_attn"]["groups"]
    q = [[view(w, (4 * s + h) * K, NT) for h in range(nh)] for s in range(2)]
    kT = [view(w, (4 * s + 2) * K, NT) for s in range(2)]
    v = [view(w, (4 * s + 3) * K, B, nk, P) for s in range(2)]
    NE, NA, NS = 16, 8, 4
    ex = [view(w, 8 * K + j * S, S) for j in range(NE)]
    total = [view(w, 16 * K + j * S, S) for j in range(2)]
    diag = [view(w, 17 * K + j * S, S) for j in range(2)]
    sign = [view(w, 18 * K + j * S, S) for j in range(2)]
    attn = [view(A, j * S, S) for j in range(NA)]
    score = [view(A, (8 + j) * S, S).bitcast(I32) for j in range(NS)]
    whole = [view(A, (12 + j) * S, S).bitcast(I32) for j in range(2)]
    oy, osign = view(A, 14 * S, S), view(A, 15 * S, S)
    py, psign = ([view(g.extra, (2 * x + j) * S, S) for j in range(2)] for x in range(2))
    weights = [g.wst[:, 0:898], g.wst2[:, 0:898]]
    step_col, minus_half = g.small[:, 0:1], g.small[:, 1:2]
    recip = [g.small[:, 8 + 8 * j:12 + 8 * j] for j in range(2)]
    bank = [g.ps[:, i * S:(i + 1) * S] for i in range(8)]
    s_bank, r_bank, o_bank, p_bank = bank[0:3], bank[3:5], bank[5], bank[6:8]
    tiles = [(s, b, h, kt) for s in range(2) for b in range(B) for h in range(nh) for kt in range(nk)]
    n_t, per = len(tiles), B * nh * nk
    AGE = dict(scores=0, trunc=1, clip=2, exp=3, add=4, sum=5, diag=6, R=7, norm=11, int=12, conv=13, pv=15,
               out=17, osign=18, oint=19, oput=20)

    def chunk(s, what, n, z, ready):
        W = [view(weights[s], 256 * i, 2, P) for i in range(3)]
        ps = p_bank[z]
        g.W(g.pe, chunk.psum_free[z])
        if what == "v":
            for j in range(4):
                for c in range(DC):
                    k0 = n * S + j * P
                    mm = g.pe.matmul(ps[:, j * P:(j + 1) * P], g.Hn[:, c, k0:k0 + P], W[2][:, c, :],
                                     start=c == 0, stop=c == 1)
        else:
            for c in range(DC):
                mm = g.pe.matmul(ps, W[what == "k"][:, c, :], g.Hn[:, c, half(n)], start=c == 0, stop=c == 1)
        t = g.E(mm)
        yield
        g.W(g.act, t, chunk.free[z])
        g.A(g.act.activation(py[z], ps, ACT.Copy, scale=FX))
        t = chunk.psum_free[z] = g.A(g.act.activation(psign[z], ps, ACT.Sign))
        yield
        g.W(g.dve, t)
        t = g.V(g.dve.tensor_scalar(py[z], py[z], FXMAX, -FXMAX, OP.min, OP.max))
        g.W(g.dve, t)
        ni = psign[z].bitcast(I32)
        t = g.V(g.dve.scalar_tensor_tensor(out=ni, in0=psign[z], scalar=-HALF, in1=py[z], op0=OP.mult, op1=OP.add))
        g.W(g.dve, t, ready())
        if what == "q":
            for h in range(nh):
                r = slice(h * rows, (h + 1) * rows)
                t = g.V(g.dve.tensor_scalar(q[s][h][r, half(n)], ni[r], 0.125, None, OP.mult))
        else:
            dst = kT[s][:, half(n)] if what == "k" else v[s][:, n].rearrange("p k d -> p (k d)")
            t = g.V(g.dve.tensor_scalar(dst, ni, 1.0 / FX, None, OP.mult))
        chunk.free[z] = t
        yield t

    QK, V_ = [("q", 0), ("k", 0), ("q", 1), ("k", 1)], [("v", 0), ("v", 1)]

    def chunks(s, which, ready):
        running, toks = [], []
        todo = list(enumerate(which))
        while todo or running:
            running = [r for r in running if not isinstance(chunks_step(r, toks), Tok)]
            if todo and len(running) < 2:
                z, (what, n) = todo.pop(0)
                r = chunk(s, what, n, z % 2, ready)
                next(r)
                running.append(r)
            if running:
                yield
                chunks_step(running[-1], toks)
                yield
        g.projected = toks

    def chunks_step(r, toks):
        t = next(r)
        if isinstance(t, Tok):
            toks.append(t)
        return t

    def body(first, old, new, fetch_even=None, fetch_odd=None):
        chunk.psum_free, chunk.free = [None] * 2, [None] * 2
        T, running = {}, {}
        done = lambda name, i: T.get((name, i))
        plan = {0: ("v0", 0, V_, None),
                4: ("qk1", 1, QK, None),
                16: ("v1", 1, V_, lambda: done("pv", -1)),
                20: ("qk0", 0, QK, lambda: done("qk", per - 1))} if new else {}

        def due(stage):
            i = step - AGE[stage]
            return i, (new if i >= 0 else old) and i < n_t

        def head_due(stage):
            i, on = due(stage)
            return i // nk, on and i % nk == nk - 1
        for step in range(n_t if new else AGE["oput"] + 1):
            if step in plan:
                key, s, which, ready = plan[step]
                if key == "qk0":
                    g.W(g.pe, t_even)
                running[key] = chunks(s, which, ready or (lambda: None))
            for key in list(running):
                if next(running[key], "end") == "end":
                    T["projected", key] = g.projected
                    del running[key]
                    if key == "v0" and fetch_even:
                        t_even = fetch_even(g.now("pe"))
                    if key == "v1" and fetch_odd:
                        t_odd = fetch_odd(g.now("pe"))
            for stage in ("out", "osign", "oint", "oput"):
                i, on = due(stage)
                s, b, h, kt = tiles[i % n_t]
                if not (on and (h, kt) == (1, nk - 1)):
                    continue
                on_ = osign.bitcast(I32)
                if stage == "out":
                    g.W(g.dve, done("pv", i), done("oput", i - per // 2))
                    T[stage, i] = g.V(g.dve.tensor_scalar(oy, o_bank, FXMAX, -FXMAX, OP.min, OP.max))
                elif stage == "osign":
                    g.W(g.act, done("out", i))
                    T[stage, i] = g.A(g.act.activation(osign, oy, ACT.Sign))
                elif stage == "oint":
                    g.W(g.dve, done("osign", i))
                    T[stage, i] = g.V(g.dve.scalar_tensor_tensor(out=on_, in0=osign, scalar=-HALF, in1=oy,
                                                                 op0=OP.mult, op1=OP.add))
                else:
                    g.W(g.act, done("oint", i))
                    group = (first if i >= 0 else first - 2) + s
                    T[stage, i] = g.A(g.act.activation(oT[:, group, half(b)], on_, ACT.Copy, scale=1.0 / FX))
            i, on = due("exp")
            if on:
                g.W(g.act, done("clip", i))
                T["exp", i] = g.A(g.act.activation(ex[i % NE], ex[i % NE], ACT.Exp, scale=1.0 / FX))
            i, on = due("int")
            if on:
                g.W(g.act, done("norm", i), done("conv", i - 2))
                T["int", i] = g.A(g.act.activation(whole[i % 2], ex[i % NE], ACT.Identity, bias=minus_half))
            i, on = due("add")
            if on and i % nk > 0:
                u = i // nk
                g.W(g.pool, done("exp", i), done("exp", i - 1), done("sum", u - 2), done("add", i - 1))
                in0 = ex[(i - 1) % NE] if i % nk == 1 else total[u % 2]
                T["add", i] = g.G(g.pool.tensor_tensor(total[u % 2], in0, ex[i % NE], OP.add))
            i, on = due("conv")
            if on:
                g.W(g.pool, done("int", i), done("pv", i - NA))
                T["conv", i] = g.G(g.pool.tensor_scalar(attn[i % NA], whole[i % 2], 1.0, 0.0, OP.mult, OP.add))
            i, on = due("clip")
            if on:
                g.W(g.dve, done("trunc", i), done("int", i - NE))
                T["clip", i] = g.V(g.dve.tensor_scalar(ex[i % NE], score[i % NS], FXMAX, -FXMAX, OP.min, OP.max))
            i, on = due("norm")
            if on:
                g.W(g.dve, done("R", i // nk))
                T["norm", i] = g.V(g.dve.tensor_tensor(ex[i % NE], ex[i % NE], r_bank[i // nk % 2], OP.mult))
            u, on = head_due("diag")
            if on:
                g.W(g.dve, done("sum", u), done("diag", u - 2))
                t = g.V(g.dve.reciprocal(recip[u % 2], r_bank[u % 2][:, 0:4]))
                g.W(g.pool, t, done("R", u - 2))
                for j in range(4):
                    T["diag", u] = g.G(g.pool.tensor_scalar(diag[u % 2][:, j * P:(j + 1) * P], g.iden[:, :],
                                                            recip[u % 2][:, j:j + 1], 1.0, OP.mult, OP.mult))
            i, on = due("trunc")
            if on:
                ps = s_bank[i % n_t % 3]
                g.W(g.act, done("qk", i), done("trunc", i - 2))
                t = g.A(g.act.activation(sign[i % 2], ps, ACT.Sign))
                g.W(g.dve, t, done("clip", i - NS))
                T["trunc", i] = g.V(g.dve.scalar_tensor_tensor(out=score[i % NS], in0=sign[i % 2], scalar=-HALF,
                                                               in1=ps, op0=OP.mult, op1=OP.add))
            i = step
            if new:
                s, b, h, kt = tiles[i]
                if i == per:
                    g.W(g.pe, T["projected", "qk1"])
                g.W(g.pe, done("trunc", i - 3 if i >= 3 else (-2, -1, -3)[i]))
                T["qk", i] = g.E(g.pe.matmul(s_bank[i % 3], kT[s][:, b * S + kt * P:b * S + (kt + 1) * P],
                                             q[s][h][:, half(b)], start=True, stop=True))
            u, on = head_due("sum")
            if on:
                g.W(g.pe, done("add", u * nk + nk - 1), done("norm", (u - 2) * nk + nk - 1))
                for j in range(4):
                    mm = g.pe.matmul(r_bank[u % 2][:, j:j + 1], total[u % 2][:, j * P:(j + 1) * P], step_col,
                                     start=True, stop=True)
                T["sum", u] = g.E(mm)
            u, on = head_due("R")
            if on:
                g.W(g.pe, done("diag", u))
                T["R", u] = g.E(g.pe.matmul(r_bank[u % 2], g.ones[:, :], diag[u % 2], start=True, stop=True))
            i, on = due("pv")
            if on and tiles[i % n_t][2] == 1 and i % 2 == 1:
                s, b, h, kt = tiles[i % n_t]
                if i == nk + 1:
                    g.W(g.pe, T["projected", "v0"])
                if i == per + nk + 1:
                    g.W(g.pe, T["projected", "v1"])
                g.W(g.pe, done("conv", i), done("out", i - kt - nk - 1))
                for k2 in (kt - 1, kt):
                    for h2 in range(nh):
                        j = i - kt + k2 - nk * (1 - h2)
                        mm = g.pe.matmul(o_bank[h2 * rows:(h2 + 1) * rows, :],
                                         v[s][:, b, k2, h2 * rows:(h2 + 1) * rows], attn[j % NA],
                                         start=k2 == 0, stop=k2 == nk - 1)
                t = g.E(mm)
                for j in (i, i - 1, i - nk, i - nk - 1):
                    T["pv", j] = t
        for key in list(running):
            for _ in running[key]:
                pass
        if new and fetch_odd:
            g.W(g.pe, t_odd)

    wsrc = a["w_L2_attn"]

    def fetch(ch, s, group):
        def go(after=None):
            g.W(g.sp, after)
            return g.dma(ch, weights[s], wsrc[group])
        return go
    t = [fetch(g.d_w, 0, 0)(), fetch(g.d_w2, 1, 1)()]
    g.V(g.dve.memset(step_col, 1.0 / FX))
    g.V(g.dve.memset(minus_half, -HALF))
    for s in range(2):
        for h in range(nh):
            z = g.G(g.pool.memset(q[s][h], 0.0))
    g.W(g.dve, z)
    g.W(g.pe, t, g.now("dve"))
    chunk.psum_free, chunk.free = [None] * 2, [None] * 2
    for _ in chunks(0, QK, lambda: None):
        pass
    g.W(g.pe, g.projected)
    body(0, False, True, fetch(g.d_w, 0, 2), fetch(g.d_w2, 1, 3))
    with g.fori(G // 2 - 1) as i:
        body(2 * i + 2, True, True, fetch(g.d_st, 0, 2 * i + 4), fetch(g.d_st2, 1, 2 * i + 5))
    wo = view(w, 0, G, D)
    tw = load(g, g.d_w, wo, a["wo_L2_attn"])
    body(G, True, False)
    return wo, tw


def l2_attn(g):
    norm_for(g)
    g.meet()
    oT = view(g.WB, 0, 8, NT)
    wo, tw = fixed_attention(g, oT)
    g.W(g.pe, tw, g.now("act"))
    y, z = view(g.work, 8 * 1024, 2, NT), view(g.work, 10 * 1024, 2, NT)
    g.meet()
    g.ring = [None] * 4

    def ev(m, ps, t):
        g.W(g.act, t)
        t = t0 = g.A(g.act.activation(y[:, m, :], ps, ACT.Identity, bias=vcol(g, "L2_attn_b_proj", m)))
        t = fixed_in_place(g, y[:, m, :], z[:, m, :], NT, t, FX)
        g.W(g.dve, t)
        t = g.V(g.dve.tensor_tensor(g.X[:, m, :], g.X[:, m, :], y[:, m, :], OP.add))
        g.resid = [t, t]
        return t0
    project(g, wo, oT, 8, DC, ev, None)


def l2_xattn(g):
    thin_heads(g, "L2_xattn")


def l2_ffn(g):
    a, w, K = g.a, g.work, 1024
    M = 64
    Bt = g.WB
    win, w1, w2, wo = view(Bt, 0, 2, M), view(Bt, 128, FF), view(Bt, 1200, FC, M), view(Bt, 1800, D)
    load(g, g.d_w, win, a["l2f_win"])
    load(g, g.d_w, w1[0:M], a["l2f_w1"])
    load(g, g.d_w, w2, a["l2f_w2"])
    tw = load(g, g.d_w, wo[0:M], a["l2f_wout"])
    t1 = norm_for(g)
    s = view(w, 3 * K, NT)
    hid = view(w, 4 * K, FC, NT)
    g2 = view(w, 12 * K, NT)
    g.W(g.pe, tw)

    def thin(wT, rhs, kts, dst, bias, ready):
        i, ps = slot(g)
        for n in range(B):
            g.W(g.pe, ready)
            for k in range(kts):
                mm = g.pe.matmul(ps[0:M, half(n)], wT[:, k, :], rhs[:, k, half(n)], start=k == 0, stop=k == kts - 1)
        t = g.E(mm)
        g.W(g.act, t)
        t = g.ring[i] = g.A(g.act.activation(dst[0:M], ps[0:M], ACT.Identity, bias=vcol(g, bias)[0:M]))
        return t
    t = thin(win, g.Hn, DC, s, "L2_ffn_bin_", t1)
    for m in range(FC):
        i, ps = slot(g)
        g.W(g.pe, t)
        for n in range(B):
            mm = g.pe.matmul(ps[:, half(n)], w1[0:M, m * P:(m + 1) * P], s[0:M, half(n)], start=True, stop=True)
        tp = g.E(mm)
        g.W(g.act, tp)
        th = g.ring[i] = g.A(g.act.activation(hid[:, m, :], ps, ACT.Relu, bias=vcol(g, "L2_ffn_b1", m)))
    t = thin(w2, hid, FC, g2, "L2_ffn_b2", th)
    ev = add_resid(g, "L2_ffn_bout")
    for m in range(DC):
        i, ps = slot(g)
        g.W(g.pe, t)
        for n in range(B):
            mm = g.pe.matmul(ps[:, half(n)], wo[0:M, m * P:(m + 1) * P], g2[0:M, half(n)], start=True, stop=True)
        g.ring[i] = ev(m, ps, g.E(mm))


def l3_attn(g):
    thin_heads(g, "L3_attn")


def l3_xattn(g):
    wide_heads(g, "L3_xattn")


def ternary(g, src, dst, tmp, sc, ready):
    n = P * 2048
    am, s, inv, al = (sc[:, i:i + 1] for i in range(4))
    g.W(g.dve, ready)
    t = g.V(g.dve.tensor_reduce(am, src, AX.X, OP.add, apply_absolute_value=True))
    g.W(g.pool, t)
    t = g.G(g.pool.partition_all_reduce(al, am, P, bass.bass_isa.ReduceOp.add))
    g.W(g.dve, t)
    t = g.V(g.dve.tensor_scalar(s, al, 1.0 / n, 1e-8, OP.mult, OP.max))
    g.W(g.dve, t)
    t = g.V(g.dve.reciprocal(inv, s))
    g.W(g.dve, t)
    t = g.V(g.dve.tensor_scalar(tmp, src, inv, ROUND, OP.mult, OP.add))
    g.W(g.dve, t)
    t = g.V(g.dve.tensor_scalar(tmp, tmp, ROUND, 1.0, OP.subtract, OP.min))
    g.W(g.dve, t)
    return g.V(g.dve.tensor_scalar(dst, tmp, -1.0, None, OP.max))


def l3_ffn(g):
    a, w, K = g.a, g.work, 1024
    A = g.WA
    tw = load(g, g.d_w, A[:, 0:4096], a["w_l3_ffn"])
    W1, W2 = A[:, 0:2048], A[:, 2048:4096]
    sc = [view(g.small, 4 * i, 4) for i in range(2)]
    tw1 = ternary(g, W1, W1, A[:, 4096:6144], sc[0], tw)
    tw2 = ternary(g, W2, W2, A[:, 6144:8192], sc[1], tw)
    t1 = norm_for(g)
    hid = view(w, 4 * K, FC, NT)

    def ev1(m, ps, t):
        g.W(g.act, t)
        return g.A(g.act.activation(hid[:, m, :], ps, ACT.Gelu, bias=vcol(g, "L3_ffn_b1", m)))
    g.W(g.pe, tw1)
    th = project(g, W1.rearrange("p (c f) -> p c f", c=2), g.Hn, DC, FC, ev1, t1)
    g.W(g.pe, tw2)
    project(g, W2.rearrange("p (c f) -> p c f", c=FC), hid, FC, DC, add_resid(g, "L3_ffn_b2"), th[-1])


STAGES = [l0_attn, l0_xattn, l0_ffn, l1_attn, l1_xattn, l1_ffn, l2_attn, l2_xattn, l2_ffn, l3_attn, l3_xattn, l3_ffn]



def kxm(w):
    k, m = w.shape
    return np.ascontiguousarray(w.reshape(k // P, P, m).transpose(1, 0, 2))


def head_pack(w, rows, dh):
    k = w.shape[0]
    out = np.zeros((k, H, rows), w.dtype)
    out[:, :, :dh] = w.reshape(k, H, dh)
    return out.reshape(k, H * rows)


def lay_out(i):
    f = np.float32
    o = {}
    o["xT"] = np.ascontiguousarray(i["x"].reshape(NT, D).T)
    o["ctx_keys"] = np.ascontiguousarray(i["ctx_1024"].reshape(B * S2, D))
    o["ctxT"] = np.ascontiguousarray(o["ctx_keys"].T)
    o["ident"] = np.eye(P, dtype=f)
    o["blockdiag"] = np.kron(np.eye(P // 16, dtype=f), np.ones((16, 16), f))
    vec = dict(i)
    for j in range(4):
        vec[f"cw{j}"] = i["L0_attn_conv_w"][:, 0, j]
    vec["gamma"] = np.repeat(i["L0_attn_gamma_attn"].reshape(H), D // H)
    vec["L2_ffn_b1"] = i["L2_ffn_b1"].reshape(FF)
    V = np.zeros((P, NVEC), f)
    for n in VEC256:
        V[:, VCOL[n]:VCOL[n] + 2] = vec[n].reshape(2, P).T
    for n in VEC1024:
        V[:, VCOL[n]:VCOL[n] + 8] = vec[n].reshape(8, P).T
    for n in ("L2_ffn_bin_", "L2_ffn_b2"):
        V[:64, VCOL[n]] = vec[n]
    for n in ("L0_ffn_scale", "L3_attn_temperature"):
        V[:, VCOL[n]] = vec[n][0]
    o["vecs"] = V

    def packs(*ws):
        return np.concatenate([kxm(np.ascontiguousarray(w)).reshape(P, -1) for w in ws], axis=1)
    o["w_l0_attn"] = packs(*(i["L0_attn_" + n].T for n in ("qk_w", "v_w", "g_w", "o_w", "gate_w", "up_w", "down_w")))
    idx = np.linspace(0.0, 1.0, D // H, dtype=f)
    freqs = (f(10.0) ** idx)[None, :] * np.arange(H, dtype=f)[:, None]
    ang = np.arange(S, dtype=f)[:, None] * freqs.reshape(1, D)
    o["cos"] = np.ascontiguousarray(np.cos(ang.astype(np.float64)).astype(f).T)
    o["l0f_AT"] = np.ascontiguousarray(i["L0_ffn_A"].transpose(2, 0, 1).reshape(R_, E_ * L_))
    o["l0f_B"] = np.ascontiguousarray(i["L0_ffn_B"].transpose(1, 0, 2))
    o["l0f_gate"] = kxm(i["L0_ffn_w_gate"])
    o["l0f_wt"] = kxm(np.ascontiguousarray(i["L0_ffn_wt_w"].T))
    o["l0f_wd"] = kxm(np.ascontiguousarray(i["L0_ffn_wd_w"].T))
    o["l0f_wtb"] = i["L0_ffn_wt_b"]
    o["rank"] = np.tile(np.arange(E_, 0, -1, dtype=f), (P, 1))
    o["w_l1_attn"] = packs(*(i["L1_attn_W_" + n].T for n in "kvro"))
    o["w_l1_xattn"] = packs(i["L1_xattn_W0"].T, i["L1_xattn_W1"].T)
    o["mask1"] = np.ascontiguousarray(i["mask_BxS2_if1"])
    o["w_l1_ffn"] = packs(i["L1_ffn_w1"].T, i["L1_ffn_w2"].T)
    o["w_l3_ffn"] = packs(i["L3_ffn_W1"].T, i["L3_ffn_W2"].T)
    o["group"] = np.ascontiguousarray(i["fside_BxSxS2_0"])
    o["mask2"] = np.ascontiguousarray(i["mask_BxSxS2_ik1"])
    z1024 = np.zeros(1024, f)
    M = 64
    o["l2f_win"] = kxm(i["L2_ffn_Win"])
    w1, w2 = np.zeros((M, M, 16), f), np.zeros((M, 16, M), f)
    for m in range(M):
        w1[m, m], w2[m, :, m] = i["L2_ffn_W1"][m], i["L2_ffn_W2"][m]
    o["l2f_w1"] = w1.reshape(M, FF)
    o["l2f_w2"] = kxm(w2.reshape(FF, M))
    o["l2f_wout"] = np.ascontiguousarray(i["L2_ffn_Wout"])
    wqkv = i["L2_attn_w_qkv"].reshape(3, 1024, D)
    wa, ba = i["L3_attn_W_attn"].reshape(D, 3, D), i["L3_attn_b_attn"].reshape(3, D)
    heads = {
        "L2_attn": ([wqkv[j].T for j in range(3)], [z1024] * 3, i["L2_attn_w_proj"].T),
        "L2_xattn": ([i[f"L2_xattn_w{n}_k"] for n in "qkv"], [i[f"L2_xattn_w{n}_b"] for n in "qkv"], i["L2_xattn_wo_k"]),
        "L3_attn": ([wa[:, j] for j in range(3)], [ba[j] for j in range(3)], i["L3_attn_W_proj"]),
        "L3_xattn": ([i["L3_xattn_W" + n].T for n in "qkv"], [i["L3_xattn_b" + n] for n in "qkv"], i["L3_xattn_Wo"].T),
    }
    for n, (ws, bs, wo) in heads.items():
        if MHA[n]["dh"] == 16:
            o["w_" + n] = packs(*ws, wo)
            o["bqk_" + n] = np.concatenate([x.reshape(2, P).T for x in bs[:2]], axis=1)
            o["bv_" + n] = np.ascontiguousarray(bs[2])
            continue
        G, rows, dh = MHA[n]["groups"], MHA[n]["rows"], MHA[n]["dh"]
        wp = [kxm(head_pack(w, rows, dh)).reshape(P, DC, G, P) for w in ws]
        o["w_" + n] = np.zeros((G + 2, P, 3 * DC * P + P + 2), f)
        o["w_" + n][:G, :, :768] = np.stack(wp).transpose(3, 1, 0, 2, 4).reshape(G, P, 3 * DC * P)
        bp = [head_pack(b[None], rows, dh).reshape(G, P) for b in bs]
        o["w_" + n][:G, :, 768:896] = bp[2][:, None, :]
        o["w_" + n][:G, :, 896:898] = np.stack(bp[:2], axis=2)
        o["wo_" + n] = kxm(np.ascontiguousarray(head_pack(np.ascontiguousarray(wo.T), rows, dh).T))
    j = np.arange(S)[None, :] - (S - P) - np.arange(P)[:, None]
    o["rel"] = np.where(j <= 0, j, -1e30).astype(f)
    o["causal"] = np.where(j <= 0, 0, -1e30).astype(f)
    start = 2.0 ** (-2.0 ** (-(np.log2(H) - 3)))
    o["slopes"] = np.array([start * start ** h for h in range(H + 1)], f)
    return o


def kernel(**inputs):
    import concourse.bacc as bacc
    from concourse.bass_utils import run_bass_kernel_spmd

    arrays = lay_out({k: np.asarray(v) for k, v in inputs.items()})
    nc = bacc.Bacc("TRN2", target_bir_lowering=False, num_devices=1)
    a = {n: nc.dram_tensor("in_" + n, x.shape, mybir.dt.from_np(x.dtype), kind="ExternalInput").ap()
         for n, x in arrays.items()}
    a["out"] = nc.dram_tensor("out_x", (D, NT), F32, kind="ExternalOutput").ap()
    decoder(nc, a, range(len(STAGES)))
    r = run_bass_kernel_spmd(nc, [{"in_" + k: v for k, v in arrays.items()}], core_ids=[0])
    return np.ascontiguousarray(r.results[0]["out_x"].T).reshape(B, S, D)
```

```python
from contextlib import ExitStack, contextmanager

import concourse.bass as bass
import concourse.mybir as mybir
import numpy as np
from concourse.alu_op_type import AluOpType as OP

ACT = mybir.ActivationFunctionType
AX = mybir.AxisListType
F32 = mybir.dt.float32
BF16 = mybir.dt.bfloat16
I32 = mybir.dt.int32

B, S, D, S2 = 2, 512, 256, 1024
NT = B * S
P = 128
DC = D // P
FF = 1024
FC = FF // P
H = 16
E_, L_, R_ = 6, 100, 16
LN_EPS = 1e-5
BIG = 1e30
FMIN = float(np.finfo(np.float32).min)
ROUND = 12582912.0
FX = 4096.0
FXMAX = 8 * FX - 1
HALF = 0.49998

VEC256 = ["L0_attn_ln1_w", "L0_attn_ln1_b", "L0_attn_conv_b", "L0_attn_g_b", "L0_attn_onorm_w",
          "L0_attn_onorm_b", "L0_attn_ln2_w", "L0_attn_ln2_b", "L0_attn_gamma1", "L0_attn_gamma2",
          "cw0", "cw1", "cw2", "cw3", "gamma", "L0_ffn_wd_b",
          "L1_attn_time_mix_k", "L1_attn_time_mix_v", "L1_attn_time_mix_r", "L1_attn_time_decay",
          "L1_attn_time_first", "L1_ffn_b2", "L2_attn_b_proj", "L2_xattn_wo_b", "L2_ffn_bout",
          "L3_attn_b_proj", "L3_xattn_bo", "L3_ffn_b2"]
VEC1024 = ["L1_ffn_b1", "L2_ffn_b1", "L3_ffn_b1"]
VCOL, _n = {}, 0
for _v in VEC256:
    VCOL[_v] = _n
    _n += 2
for _v in VEC1024:
    VCOL[_v] = _n
    _n += 8
for _v in ("L2_ffn_bin_", "L2_ffn_b2", "L0_ffn_scale", "L3_attn_temperature"):
    VCOL[_v] = _n
    _n += 1
NVEC = _n

MHA = {
    "L2_attn": dict(groups=8, rows=64, dh=64),
    "L2_xattn": dict(dh=16),
    "L3_attn": dict(dh=16),
    "L3_xattn": dict(groups=8, rows=64, dh=64),
}


class Tok:

    def __init__(self, ch, n):
        self.ch, self.n = ch, n


class Chan:

    def __init__(self, nc, ctx, name, step=1):
        self.sem, self.step, self.n, self.name = ctx.enter_context(nc.semaphore(name)), step, 0, name


class Prog:

    def __init__(self, nc, ctx, aps):
        self.nc, self.ctx, self.a = nc, ctx, aps
        self.pe, self.dve, self.act, self.pool, self.sp = nc.tensor, nc.vector, nc.scalar, nc.gpsimd, nc.sync
        self.c = {n: Chan(nc, ctx, "s_" + n) for n in ("pe", "dve", "act", "pool")}
        self.inner = {n: Chan(nc, ctx, "l_" + n) for n in ("pe", "dve", "act", "pool")}
        self.d_st = Chan(nc, ctx, "l_dma", 16)
        self.d_st2 = Chan(nc, ctx, "l_dma_2", 16)
        self.waited = {}

    def mark(self, eng, ins):
        ch = self.c[eng]
        ins.then_inc(ch.sem, 1)
        ch.n += 1
        return Tok(ch, ch.n)

    def E(self, ins):
        return self.mark("pe", ins)

    def V(self, ins):
        return self.mark("dve", ins)

    def A(self, ins):
        return self.mark("act", ins)

    def G(self, ins):
        return self.mark("pool", ins)

    def dma_chan(self, name):
        return Chan(self.nc, self.ctx, "d_" + name, 16)

    def dma(self, ch, out, in_, eng=None):
        (eng or self.sp).dma_start(out, in_).then_inc(ch.sem, 16)
        ch.n += 16
        return Tok(ch, ch.n)

    def W(self, eng, *toks):
        todo = list(toks)
        last = {}
        while todo:
            t = todo.pop()
            if isinstance(t, (list, tuple)):
                todo += t
            elif t is not None and t.n > last.get(t.ch.name, (0,))[0]:
                last[t.ch.name] = t.n, t.ch
        for name, (n, ch) in last.items():
            if n > self.waited.get((id(eng), name), 0):
                self.waited[id(eng), name] = n
                eng.wait_ge(ch.sem, n)

    def now(self, *names):
        return [Tok(self.c[n], self.c[n].n) for n in names if self.c[n].n]

    def meet(self, *dma):
        toks = self.now("pe", "dve", "act", "pool")
        for eng in (self.pe, self.dve, self.act, self.pool, self.sp):
            self.W(eng, toks, *dma)

    @contextmanager
    def fori(self, trips):
        self.meet()
        outer, outer_waited, self.c = self.c, self.waited, self.inner
        with self.nc.Fori(0, trips) as i:
            self.waited = {}
            every = list(self.inner.values()) + [self.d_st, self.d_st2]
            for ch in every:
                ch.n = 0
            yield i
            self.meet()
            self.nc.all_engine_barrier(sems_to_clear=range(every[0].sem.num, every[-1].sem.num + 1))
        self.c, self.waited = outer, outer_waited
        self.ring = [None] * 4


def view(t, off, *dims):
    n = int(np.prod(dims))
    ap = t[:, off:off + n]
    if len(dims) == 1:
        return ap
    names = "abcd"[:len(dims)]
    pat = "p (" + " ".join(names) + ") -> p " + " ".join(names)
    return ap.rearrange(pat, **{k: v for k, v in zip(names[1:], dims[1:])})


def decoder(nc, a, stages):
    ctx = ExitStack()
    with ctx:
        def sb(name, cols, dt=F32):
            return ctx.enter_context(nc.sbuf_tensor(name, [P, cols], dt))

        g = Prog(nc, ctx, a)
        g.X = view(sb("resid", DC * NT), 0, DC, NT)
        g.Hn = view(sb("normed", DC * NT), 0, DC, NT)
        g.ctxK = view(sb("ctx_keys", 16 * D), 0, 16, D)
        g.ctxT = view(sb("ctx_feat", DC * B * S2), 0, DC, B * S2)
        g.WA = sb("arena_a", 8192)
        g.WB = sb("arena_b", 8192)
        g.work = sb("work", 19 * 1024)
        g.wst = sb("head_weights", 3 * DC * P + P + 8)
        g.wst2 = sb("head_weights_2", 3 * DC * P + P + 8)
        g.extra = sb("extra", 2048)
        g.vec = sb("vecs", NVEC)
        g.one = sb("mean_matrix", P)
        g.ones = sb("ones_matrix", P)
        g.iden = sb("identity", P)
        g.small = sb("small", 256)
        g.ps = ctx.enter_context(nc.psum_tensor("ps", [P, 4096], F32))
        g.ring = [None] * 4
        g.ring_i = 0

        g.d_in = g.dma_chan("in")
        g.d_ctx = g.dma_chan("ctx")
        g.d_w = g.dma_chan("w")
        g.d_w2 = g.dma_chan("w2")
        g.d_out = g.dma_chan("out")
        g.d_next = g.dma_chan("next")
        g.d_scr, g.d_scr2 = g.dma_chan("scratch"), g.dma_chan("scratch_2")

        g.dma(g.d_in, g.vec[:, :], a["vecs"])
        g.dma(g.d_in, g.iden[:, :], a["ident"])
        t_in = g.dma(g.d_in, g.X, a["xT"].rearrange("(c p) t -> p c t", p=P))
        g.dma(g.d_ctx, g.ctxT, a["ctxT"].rearrange("(c p) t -> p c t", p=P))
        g.t_ctx = g.dma(g.d_ctx, g.ctxK, a["ctx_keys"].rearrange("(k p) d -> p k d", p=P))
        g.V(nc.vector.memset(g.one[:, :], 1.0 / D))
        g.V(nc.vector.memset(g.ones[:, :], 1.0))
        const = sb("constants", 3)
        g.eps, g.ln15, g.e9 = (const[:, j:j + 1] for j in range(3))
        for ap, value in ((g.eps, LN_EPS), (g.ln15, 15 * float(np.log(2.0))), (g.e9, 1e-9)):
            g.V(nc.vector.memset(ap, value))
        g.meet(t_in)
        g.quantized, g.ternary = [None, None], [None, None]
        g.resid = [t_in, t_in]

        for s in stages:
            if s:
                for e in (g.pe, g.dve, g.act, g.pool):
                    g.W(e, g.t_ctx)
            STAGES[s](g)
            g.meet()
            g.ring = [None] * 4

        t_out = g.dma(g.d_out, a["out"].rearrange("(c p) t -> p c t", p=P), g.X)
        g.W(nc.sync, t_out)



def vcol(g, name, c=0):
    return g.vec[:, VCOL[name] + c:VCOL[name] + c + 1]


def slot(g):
    i = g.ring_i
    g.ring_i = (i + 1) % 4
    g.W(g.pe, g.ring[i])
    return i, g.ps[:, i * 1024:(i + 1) * 1024]


def half(n):
    return slice(n * S, (n + 1) * S)


def layernorm(g, src, dst, ready, sq, tmp, w=None, b=None, put=None):
    one = g.one[:, :]
    im, mean = slot(g)
    iv, var = slot(g)
    t1 = []
    for n in range(B):
        g.W(g.pe, ready[n])
        for c in range(DC):
            mm = g.pe.matmul(mean[:, half(n)], one, src[:, c, half(n)], start=c == 0, stop=c == DC - 1)
        t1.append(g.E(mm))
    t2 = []
    for n in range(B):
        g.W(g.dve, t1[n], ready[n])
        for c in range(DC):
            t = g.V(g.dve.tensor_tensor(dst[:, c, half(n)], src[:, c, half(n)], mean[:, half(n)], OP.subtract))
        t2.append(t)
    g.ring[im] = t2[-1]
    t3 = []
    for n in range(B):
        g.W(g.act, t2[n])
        t3.append(g.A(g.act.activation(sq[:, :, half(n)], dst[:, :, half(n)], ACT.Square)))
    t4 = []
    for n in range(B):
        g.W(g.pe, t3[n])
        for c in range(DC):
            mm = g.pe.matmul(var[:, half(n)], one, sq[:, c, half(n)], start=c == 0, stop=c == DC - 1)
        t4.append(g.E(mm))
    t5, t6 = [], []
    for n in range(B):
        g.W(g.act, t4[n])
        t5.append(g.A(g.act.activation(tmp[:, half(n)], var[:, half(n)], ACT.Ln, bias=g.eps)))
    for n in range(B):
        g.W(g.act, t5[n])
        t6.append(g.A(g.act.activation(tmp[:, half(n)], tmp[:, half(n)], ACT.Exp, scale=-0.5)))
    g.ring[iv] = t6[-1]
    out = []
    for n in range(B):
        g.W(g.dve, t6[n])
        for c in range(DC):
            last = w is None
            o = put(c, n) if last and put is not None else dst[:, c, half(n)]
            t = g.V(g.dve.tensor_tensor(o, dst[:, c, half(n)], tmp[:, half(n)], OP.mult))
            if not last:
                g.W(g.dve, t)
                o = put(c, n) if put is not None else dst[:, c, half(n)]
                t = g.V(g.dve.tensor_scalar(o, dst[:, c, half(n)], vcol(g, w, c), vcol(g, b, c), OP.mult, OP.add))
        out.append(t)
    return tuple(out)


def project(g, wT, src, kts, mts, evac, ready, src_ap=None):
    out = []
    for m in range(mts):
        i, ps = slot(g)
        for n in range(B):
            g.W(g.pe, ready[n] if isinstance(ready, tuple) else ready)
            for k in range(kts):
                rhs = src_ap(k, n) if src_ap else src[:, k, half(n)]
                mm = g.pe.matmul(ps[:, half(n)], wT[:, k, m * P:(m + 1) * P], rhs, start=k == 0, stop=k == kts - 1)
        t = g.E(mm)
        g.ring[i] = evac(m, ps, t)
        out.append(g.ring[i])
    return out


def add_resid(g, bias=None, scale=None):
    toks = []

    def evac(m, ps, t):
        g.W(g.dve, t)
        if bias is None:
            t = g.V(g.dve.tensor_tensor(g.X[:, m, :], ps, g.X[:, m, :], OP.add))
        else:
            t = g.V(g.dve.scalar_tensor_tensor(out=g.X[:, m, :], in0=ps, scalar=vcol(g, bias, m),
                                               in1=g.X[:, m, :], op0=OP.add, op1=OP.add))
        g.resid = [t, t]
        return t
    return evac


def load(g, ch, dst, src, *after):
    g.W(g.sp, *after)
    return g.dma(ch, dst, src)



def l0_attn(g):
    a = g.a
    A, Bt, w = g.WA, g.WB, g.work
    tw = load(g, g.d_w, A[:, :], a["w_l0_attn"])
    W = {n: view(A, i * 512, 2, 256) for i, n in enumerate(("qk", "v", "g", "o"))}
    Wg, Wu, Wd = view(A, 2048, 2, FF), view(A, 4096, 2, FF), view(A, 6144, FC, D)
    cosT = view(Bt, 0, 2, S)
    tcos = load(g, g.d_w2, cosT, a["cos"].rearrange("(c p) t -> p c t", p=P))
    blk = view(Bt, 1024, P)
    tcos = load(g, g.d_w2, blk, a["blockdiag"])
    K = 1024
    tmp, sq = view(w, 0, NT), view(w, K, 2, NT)
    hin = view(w, 3 * K, 2, NT)
    hpad = view(Bt, 2048, 2, B, S + 3)
    xc = view(w, 5 * K, 2, B, S)
    kk, v, gate = view(w, 7 * K, 2, NT), view(w, 9 * K, 2, NT), view(w, 11 * K, 2, NT)
    dec, rdec = view(w, 13 * K, 2, S), view(w, 14 * K, 2, S)
    ones, gam = view(w, 15 * K, S), view(w, 15 * K + S, S)
    cs = view(w, 16 * K, 2, B, S)

    t1 = layernorm(g, g.X, hin, g.resid, sq, tmp)
    z = g.G(g.pool.memset(hpad[:, :, :, 0:3], 0.0))
    t2 = layernorm(g, hin, g.Hn, t1, sq, tmp, "L0_attn_ln1_w", "L0_attn_ln1_b",
                   put=lambda c, n: hpad[:, c, n, 3:])
    tx = []
    g.W(g.dve, z, t2)
    for c in range(DC):
        t = g.V(g.dve.tensor_scalar(xc[:, c], hpad[:, c, :, 0:S], vcol(g, "cw0", c), vcol(g, "L0_attn_conv_b", c),
                                    OP.mult, OP.add))
        for j in range(1, 4):
            g.W(g.dve, t)
            t = g.V(g.dve.scalar_tensor_tensor(out=xc[:, c], in0=hpad[:, c, :, j:j + S], scalar=vcol(g, f"cw{j}", c),
                                               in1=xc[:, c], op0=OP.mult, op1=OP.add))
        tx.append(t)
    t = g.V(g.dve.memset(ones, 1.0))
    g.W(g.dve, t)
    td = []
    for c in range(DC):
        t = g.V(g.dve.tensor_scalar(gam, ones, vcol(g, "gamma", c), None, OP.mult))
        m = g.V(g.dve.memset(dec[:, c, 0:1], 1.0))
        g.W(g.dve, t, m)
        t = g.V(g.dve.tensor_tensor_scan(dec[:, c, 1:S], gam[:, 1:S], ones[:, 1:S], 1.0, OP.mult, OP.mult))
        g.W(g.dve, t)
        td.append(t)
    t = g.V(g.dve.tensor_scalar(rdec, dec, 1e-6, None, OP.add))
    g.W(g.dve, t)
    trd = g.V(g.dve.reciprocal(rdec, rdec))
    xcf = xc.rearrange("p c b s -> p c (b s)")
    g.W(g.pe, tw, tcos)

    def ev_qk(m, ps, t):
        g.W(g.act, t)
        g.A(g.act.activation(kk[:, m, :], ps, ACT.Copy))
        return g.A(g.act.activation(sq[:, m, :], ps, ACT.Square))
    tq = project(g, W["qk"], xcf, DC, DC, ev_qk, tx[-1])

    def ev_v(m, ps, t):
        g.W(g.act, t)
        return g.A(g.act.activation(v[:, m, :], ps, ACT.Copy))
    tv = project(g, W["v"], xcf, DC, 1, ev_v, tx[-1])
    norm = [tmp, view(w, 16 * K, NT)]
    tn = []
    for m in range(DC):
        i, ps = slot(g)
        g.W(g.pe, tq[m])
        for n in range(B):
            mm = g.pe.matmul(ps[:, half(n)], blk, sq[:, m, half(n)], start=True, stop=True)
        t = g.E(mm)
        g.W(g.dve, t)
        t = g.ring[i] = g.V(g.dve.tensor_scalar(norm[m], ps, 1e-24, None, OP.max))
        tn.append(t)
    for m in range(DC):
        g.W(g.act, tn[m])
        tn[m] = g.A(g.act.activation(norm[m], norm[m], ACT.Ln, scale=2.0 ** 30))
    for m in range(DC):
        g.W(g.act, tn[m])
        tn[m] = g.A(g.act.activation(norm[m], norm[m], ACT.Exp, scale=-0.5, bias=g.ln15))
    tv += project(g, W["v"][:, :, P:2 * P], xcf, DC, 1, lambda m, ps, t: ev_v(1, ps, t), tx[-1])
    for m in range(DC):
        g.W(g.dve, tn[m])
        tk = g.V(g.dve.tensor_tensor(kk[:, m, :], kk[:, m, :], norm[m], OP.mult))
    g.W(g.dve, tk)

    def ev_g(m, ps, t):
        g.W(g.act, t)
        return g.A(g.act.activation(gate[:, m, :], ps, ACT.Sigmoid, bias=vcol(g, "L0_attn_g_b", m)))
    tg = project(g, W["g"], xcf, DC, DC, ev_g, tx[-1])
    kr = xc
    g.W(g.pool, tk, tg, trd, g.now("pe"))
    tkr, tgd = {}, {}
    for c in range(DC):
        for b in range(B):
            tgd[c, b] = g.G(g.pool.tensor_tensor(gate[:, c, half(b)], gate[:, c, half(b)], dec[:, c], OP.mult))
    for c in range(DC):
        for b in range(B):
            tkr[c, b] = g.G(g.pool.tensor_tensor(kr[:, c, b], kk[:, c, half(b)], rdec[:, c], OP.mult))
    g.W(g.dve, tcos, tv, tk)
    kb = kk.rearrange("p c (b s) -> p c b s", b=B)
    for c in range(DC):
        for b in range(B):
            g.V(g.dve.tensor_tensor(cs[:, c, b, 1:S], cosT[:, c, 1:S], kb[:, c, b, 0:S - 1], OP.add))
            t = g.V(g.dve.tensor_copy(cs[:, c, b, 0:1], cosT[:, c, 0:1]))
    g.W(g.dve, t)
    csf = cs.rearrange("p c b s -> p c (b s)")
    t = g.V(g.dve.tensor_tensor(csf, csf, v, OP.mult))
    g.W(g.dve, t)
    out = v
    for c in range(DC):
        for b in range(B):
            g.W(g.dve, tgd[c, b])
            t = g.V(g.dve.tensor_tensor(cs[:, c, b], cs[:, c, b], gate[:, c, half(b)], OP.mult))
            g.W(g.dve, t)
            t = g.V(g.dve.tensor_tensor_scan(out[:, c, half(b)], ones, cs[:, c, b], 0.0, OP.mult, OP.add))
            g.W(g.dve, t, tkr[c, b])
            t = g.V(g.dve.tensor_tensor(out[:, c, half(b)], out[:, c, half(b)], kr[:, c, b], OP.mult))
    ao = gate

    def ev_o(m, ps, t):
        g.W(g.act, t)
        return g.A(g.act.activation(ao[:, m, :], ps, ACT.Copy))
    to = project(g, W["o"], out, DC, DC, ev_o, t)
    tn = layernorm(g, ao, g.Hn, [to[-1]] * 2, sq, tmp, "L0_attn_onorm_w", "L0_attn_onorm_b")
    x2 = hin
    g.W(g.dve, tn)
    for c in range(DC):
        t = g.V(g.dve.scalar_tensor_tensor(out=x2[:, c, :], in0=g.Hn[:, c, :], scalar=vcol(g, "L0_attn_gamma1", c),
                                           in1=x2[:, c, :], op0=OP.mult, op1=OP.add))
    h2 = view(w, 5 * K, 2, NT)
    tn = layernorm(g, x2, h2, [t, t], sq, tmp, "L0_attn_ln2_w", "L0_attn_ln2_b")
    hid = view(w, 7 * K, FC, NT)
    sil = [view(w, 15 * K, NT), view(w, 16 * K, NT)]
    ts = [None, None]
    th = None
    for m in range(FC):
        def ev_gate(_, ps, t):
            g.W(g.act, t, ts[m % 2])
            g.tsil = g.A(g.act.activation(sil[m % 2], ps, ACT.Silu))
            return g.tsil

        def ev_up(_, ps, t):
            g.W(g.dve, t, g.tsil)
            ts[m % 2] = g.V(g.dve.tensor_tensor(hid[:, m, :], ps, sil[m % 2], OP.mult))
            return ts[m % 2]
        project(g, Wg[:, :, m * P:(m + 1) * P], h2, DC, 1, ev_gate, tn)
        th = project(g, Wu[:, :, m * P:(m + 1) * P], h2, DC, 1, ev_up, tn)[0]

    def ev_d(m, ps, t):
        g.W(g.dve, t)
        t = g.V(g.dve.scalar_tensor_tensor(out=x2[:, m, :], in0=ps, scalar=vcol(g, "L0_attn_gamma2", m),
                                           in1=x2[:, m, :], op0=OP.mult, op1=OP.add))
        g.W(g.dve, t)
        t2 = g.V(g.dve.tensor_tensor(g.X[:, m, :], g.X[:, m, :], x2[:, m, :], OP.add))
        g.resid = [t2, t2]
        return t
    project(g, Wd, hid, FC, DC, ev_d, th)


def l0_xattn(g):
    w, K = g.work, 1024
    sq, tmp = view(w, 0, 2, NT), view(w, 2 * K, NT)
    hid = [view(w, (3 + 4 * b) * K, 8, S) for b in range(B)]
    t1 = layernorm(g, g.X, g.Hn, g.resid, sq, tmp)
    for b in range(B):
        for k2 in range(4):
            i, ps = slot(g)
            g.W(g.pe, t1[b])
            for j in range(2):
                kt = 2 * k2 + j
                for c in range(DC):
                    mm = g.pe.matmul(ps[:, half(j)], g.ctxT[:, c, b * S2 + kt * P:b * S2 + (kt + 1) * P],
                                     g.Hn[:, c, half(b)], start=c == 0, stop=c == DC - 1)
            t = g.E(mm)
            g.W(g.act, t)
            g.ring[i] = g.A(g.act.activation(hid[b][:, 2 * k2:2 * k2 + 2, :],
                                             ps.rearrange("p (a s) -> p a s", a=2), ACT.Gelu_apprx_tanh))
    for b in range(B):
        i, ps = slot(g)
        g.W(g.pe, g.now("act"))
        for m in range(DC):
            for kt in range(8):
                mm = g.pe.matmul(ps[:, half(m)], g.ctxK[:, b * 8 + kt, m * P:(m + 1) * P], hid[b][:, kt, :],
                                 start=kt == 0, stop=kt == 7)
        t = g.E(mm)
        g.W(g.dve, t)
        t = g.V(g.dve.tensor_tensor(g.X[:, :, half(b)], ps.rearrange("p (c s) -> p c s", c=2),
                                    g.X[:, :, half(b)], OP.add))
        g.ring[i] = t
        g.resid[b] = t


def l0_ffn(g):
    a, w, K = g.a, g.work, 1024
    Bt = g.WB
    n = E_ * L_
    AT, Bm = view(Bt, 0, n), view(Bt, 600, E_, D)
    tokg = view(Bt, 2200, 2, n + E_)
    WT, WD = view(Bt, 3500, 2, D), view(Bt, 4100, 2, D)
    wtb = view(Bt, 4700, D)
    rank = view(Bt, 5000, E_)
    val = view(Bt, 5100, E_, D)
    tw = load(g, g.d_w, AT[0:R_, :], a["l0f_AT"])
    load(g, g.d_w, Bm[0:R_], a["l0f_B"])
    load(g, g.d_w, tokg[:, :, n:n + E_], a["l0f_gate"])
    load(g, g.d_w, WT, a["l0f_wt"])
    load(g, g.d_w, WD, a["l0f_wd"])
    load(g, g.d_w, rank, a["rank"])
    tw = load(g, g.d_w, wtb, a["l0f_wtb"].partition_broadcast(P))
    sq, tmp = view(w, 0, 2, NT), view(w, 2 * K, NT)
    t1 = layernorm(g, g.X, g.Hn, g.resid, sq, tmp)
    g.W(g.pe, tw)
    for c in range(DC):
        i, ps = slot(g)
        for e in range(E_):
            o = (e * L_) if e < 5 else S
            mm = g.pe.matmul(ps[:, o:o + L_], Bm[0:R_, e, c * P:(c + 1) * P], AT[0:R_, e * L_:(e + 1) * L_],
                             start=True, stop=True)
        t = g.E(mm)
        g.W(g.dve, t)
        g.V(g.dve.tensor_copy(tokg[:, c, 0:500], ps[:, 0:500]))
        tt = g.ring[i] = g.V(g.dve.tensor_copy(tokg[:, c, 500:600], ps[:, S:S + L_]))
    g.W(g.pe, tt)
    g.W(g.dve, tw)
    for e in range(E_):
        i, ps = slot(g)
        for c in range(DC):
            mm = g.pe.matmul(ps[0:L_, 0:D], tokg[:, c, e * L_:(e + 1) * L_], WT[:, c, :], start=c == 0, stop=c == 1)
        t = g.E(mm)
        g.W(g.dve, t)
        tvl = g.ring[i] = g.V(g.dve.tensor_tensor(val[0:L_, e, :], ps[0:L_, 0:D], wtb[0:L_, :], OP.add))
    g.W(g.dve, tvl)
    tvl = g.V(g.dve.memset(val[0:1], 0.0))
    PT = view(w, 3 * K, E_, NT)
    prob = [view(w, 9 * K + 1024 * j, n) for j in range(2)]
    sm = [view(g.small, 64 * j, 64) for j in range(2)]
    tfree = [None, None]
    sfree = [None, None]
    tlast = []
    tprob = {}

    def turn(it):
        j = it % 2
        pr = prob[j].rearrange("p (e l) -> p e l", e=E_)
        i2, ps2 = slot(g)
        g.W(g.pe, tprob[it])
        for e in range(E_):
            mm = g.pe.transpose(ps2[0:L_, e * P:(e + 1) * P], pr[:, e, :], g.iden[:, :])
        t = tfree[j] = g.E(mm)
        g.W(g.act, t)
        t = g.ring[i2] = g.A(g.act.activation(PT[0:L_, :, it * P:(it + 1) * P],
                                              ps2[0:L_, 0:E_ * P].rearrange("p (e t) -> p e t", e=E_), ACT.Copy))
        tlast.append(t)

    for it in range(NT // P):
        j = it % 2
        i, ps = slot(g)
        g.W(g.pe, t1[it // 4], tt)
        for o, lo, hi in ((0, 0, 500), (S, 500, n + E_)):
            for c in range(DC):
                mm = g.pe.matmul(ps[:, o:o + hi - lo], g.Hn[:, c, it * P:(it + 1) * P], tokg[:, c, lo:hi],
                                 start=c == 0, stop=c == 1)
        t = g.E(mm)
        s = sm[j]
        mx, ng, su, gr = s[:, 0:7], s[:, 8:14], s[:, 16:22], s[:, 24:30]
        eq, m2, rs = s[:, 32:38], s[:, 40:41], s[:, 48:54]
        gl = ps[:, S + L_:S + L_ + E_]
        g.W(g.dve, t, sfree[j])
        g.V(g.dve.tensor_reduce(mx[:, 0:5], ps[:, 0:500].rearrange("p (e l) -> p e l", e=5), AX.X, OP.max))
        g.V(g.dve.tensor_reduce(mx[:, 5:6], ps[:, S:S + L_], AX.X, OP.max))
        t = g.V(g.dve.tensor_reduce(mx[:, 6:7], gl, AX.X, OP.max))
        g.W(g.dve, t)
        tn = g.V(g.dve.tensor_scalar(ng, mx[:, 0:6], -1.0 / 16, None, OP.mult))
        t = g.V(g.dve.tensor_scalar(eq, gl, mx[:, 6:7], None, OP.is_equal))
        g.W(g.dve, t)
        t = g.V(g.dve.tensor_tensor(eq, eq, rank, OP.mult))
        g.W(g.dve, t)
        t = g.V(g.dve.tensor_reduce(m2, eq, AX.X, OP.max))
        g.W(g.dve, t)
        tgt = g.V(g.dve.tensor_scalar(eq, eq, m2, None, OP.is_equal))
        g.W(g.act, tn, tgt, tfree[j])
        for e in range(E_):
            o = e * L_ if e < 5 else S
            te = g.A(g.act.activation(prob[j][:, e * L_:(e + 1) * L_], ps[:, o:o + L_], ACT.Exp, scale=1.0 / 16,
                                      bias=ng[:, e:e + 1], accum_out=su[:, e:e + 1]))
        g.ring[i] = te
        g.W(g.dve, te, tgt)
        t = g.V(g.dve.reciprocal(rs, su))
        g.W(g.dve, t)
        t = g.V(g.dve.tensor_tensor(gr, rs, eq, OP.mult))
        g.W(g.dve, t)
        pr = prob[j].rearrange("p (e l) -> p e l", e=E_)
        tprob[it] = sfree[j] = g.V(g.dve.tensor_tensor(pr, pr, gr.unsqueeze(2).broadcast_to([P, E_, L_]), OP.mult))
        if it:
            turn(it - 1)
    turn(NT // P - 1)
    zb = view(w, 12 * K, 2, NT)
    g.W(g.pe, tvl)
    tz = []
    for n_ in range(B):
        i, ps = slot(g)
        g.W(g.pe, tlast[4 * n_ + 3])
        for m in range(DC):
            for e in range(E_):
                mm = g.pe.matmul(ps[:, half(m)], val[0:L_, e, m * P:(m + 1) * P], PT[0:L_, e, half(n_)],
                                 start=e == 0, stop=e == E_ - 1)
        t = g.E(mm)
        g.W(g.dve, t)
        t = g.ring[i] = g.V(g.dve.tensor_tensor(zb[:, :, half(n_)], ps.rearrange("p (c s) -> p c s", c=2),
                                                g.Hn[:, :, half(n_)], OP.add))
        tz.append(t)
    sb_ = view(g.small, 192, 2)
    t = g.V(g.dve.tensor_scalar(sb_, g.vec[:, VCOL["L0_ffn_wd_b"]:VCOL["L0_ffn_wd_b"] + 2], vcol(g, "L0_ffn_scale"),
                                None, OP.mult))
    ex, gd = view(w, 14 * K, 2, NT), view(w, 16 * K, 2, NT)

    def ev(m, ps, t2):
        g.W(g.act, t2, t)
        te = g.A(g.act.activation(ex[:, m, :], ps, ACT.Exp, scale=vcol(g, "L0_ffn_scale"), bias=sb_[:, m:m + 1]))
        g.W(g.dve, te)
        u = g.V(g.dve.tensor_scalar(gd[:, m, :], ex[:, m, :], 0.0, float(np.finfo(np.float32).eps),
                                    OP.is_equal, OP.mult))
        g.W(g.dve, u)
        u = g.V(g.dve.tensor_tensor(ex[:, m, :], ex[:, m, :], gd[:, m, :], OP.add))
        g.W(g.act, u)
        u = g.A(g.act.activation(ex[:, m, :], ex[:, m, :], ACT.Ln))
        v_ = g.V(g.dve.tensor_tensor(g.X[:, m, :], g.X[:, m, :], g.Hn[:, m, :], OP.add))
        g.W(g.dve, u, v_)
        u = g.V(g.dve.tensor_tensor(g.X[:, m, :], g.X[:, m, :], ex[:, m, :], OP.add))
        g.resid = [u, u]
        return te
    project(g, WD, zb, DC, DC, ev, tuple(tz))



def l1_attn(g):
    a, w, K = g.a, g.work, 1024
    A, Bt = g.WA, g.WB
    tw = load(g, g.d_w, Bt[:, 0:2048], a["w_l1_attn"])
    W = {n: view(Bt, i * 512, 2, 256) for i, n in enumerate(("k", "v", "r", "o"))}
    hp = view(Bt, 2048, 2, B, S + 1)
    sq, tmp = view(w, 0, 2, NT), view(w, 2 * K, NT)
    z = g.G(g.pool.memset(hp[:, :, :, 0:1], 0.0))
    t1 = layernorm(g, g.X, g.Hn, g.resid, sq, tmp, put=lambda c, n: hp[:, c, n, 1:])
    om = view(g.small, 0, 8)
    mixed = {"k": view(w, 0, 2, B, S), "v": view(w, 3 * K, 2, B, S), "r": view(w, 5 * K, 2, B, S)}
    g.W(g.dve, z, t1)
    tm = {}
    for q, n in enumerate("kvr"):
        col = VCOL["L1_attn_time_mix_" + n]
        t = g.V(g.dve.tensor_scalar(om[:, 2 * q:2 * q + 2], g.vec[:, col:col + 2], -1.0, 1.0, OP.mult, OP.add))
        for c in range(DC):
            t2 = g.V(g.dve.tensor_scalar(mixed[n][:, c], hp[:, c, :, 1:], vcol(g, "L1_attn_time_mix_" + n, c), None,
                                         OP.mult))
            g.W(g.dve, t, t2)
            tm[n] = g.V(g.dve.scalar_tensor_tensor(out=mixed[n][:, c], in0=hp[:, c, :, 0:S],
                                                   scalar=om[:, 2 * q + c:2 * q + c + 1], in1=mixed[n][:, c],
                                                   op0=OP.mult, op1=OP.add))
    k, v, r = (view(w, o * K, 2, NT) for o in (7, 9, 11))
    flat = {n: x.rearrange("p c b s -> p c (b s)") for n, x in mixed.items()}
    g.W(g.pe, tw)

    def copy_to(dst, func=ACT.Copy):
        def ev(m, ps, t):
            g.W(g.act, t)
            return g.A(g.act.activation(dst[:, m, :], ps, func))
        return ev
    tk = project(g, W["k"], flat["k"], DC, DC, copy_to(k), tm["k"])
    tv = project(g, W["v"], flat["v"], DC, DC, copy_to(v), tm["v"])
    tr = project(g, W["r"], flat["r"], DC, DC, copy_to(r, ACT.Sigmoid), tm["r"])
    pb = view(A, 0, 2, B, S + 1)
    qb = view(A, 2100, 2, B, S + 1)
    wb = view(w, 13 * K, S)
    ones = view(w, 13 * K + S, S)
    t = g.V(g.dve.memset(ones, 1.0))
    t0 = g.V(g.dve.memset(pb[:, :, :, 0:1], -BIG))
    t0 = g.V(g.dve.memset(qb[:, :, :, 0:1], 0.0))
    g.W(g.dve, t, t0, tk)
    for c in range(DC):
        t = g.V(g.dve.tensor_scalar(wb, ones, vcol(g, "L1_attn_time_decay", c), None, OP.mult))
        g.W(g.dve, t)
        for b in range(B):
            t = g.V(g.dve.tensor_tensor_scan(pb[:, c, b, 1:], wb, k[:, c, half(b)], -BIG, OP.add, OP.max))
        g.W(g.dve, t)
    tp = t
    uk, mx, so, sc = (view(w, o * K, 2, B, S) for o in (0, 3, 5, 14))
    sp, sn = view(A, 4200, 2, B, S), view(g.WB, 4200 - 100, 2, B, S)
    kb = k.rearrange("p c (b s) -> p c b s", b=B)
    vb = v.rearrange("p c (b s) -> p c b s", b=B)
    g.W(g.dve, g.now("pe"))

    g.W(g.pool, tk, tp, g.now("pe"))
    LOW = float(np.exp(np.float64(-30.0)))
    g.W(g.act, tk, g.now("pe"))
    t_uk = [g.A(g.act.activation(uk[:, c], kb[:, c], ACT.Identity, bias=vcol(g, "L1_attn_time_first", c)))
            for c in range(DC)]
    tsp, tsn, tso, tsc = {}, {}, {}, {}

    def exp_in_place(x, t):
        g.W(g.act, t)
        return g.A(g.act.activation(x, x, ACT.Exp))
    for c in range(DC):
        p0, p1 = pb[:, c, :, 0:S], pb[:, c, :, 1:]
        t_new = g.G(g.pool.tensor_tensor(sn[:, c], kb[:, c], p1, OP.subtract))
        t = g.V(g.dve.scalar_tensor_tensor(out=sp[:, c], in0=p0, scalar=vcol(g, "L1_attn_time_decay", c),
                                           in1=p1, op0=OP.add, op1=OP.subtract))
        g.W(g.dve, t)
        t = g.V(g.dve.tensor_scalar(sp[:, c], sp[:, c], -30.0, None, OP.max))
        tsp[c] = exp_in_place(sp[:, c], t)
        g.W(g.dve, t_uk[c])
        t = g.V(g.dve.tensor_tensor(mx[:, c], p0, uk[:, c], OP.max))
        g.W(g.dve, t)
        g.W(g.pool, t)
        t_cur = g.G(g.pool.tensor_tensor(sc[:, c], uk[:, c], mx[:, c], OP.subtract))
        t = g.V(g.dve.tensor_tensor(so[:, c], p0, mx[:, c], OP.subtract))
        tsn[c] = exp_in_place(sn[:, c], t_new)
        tso[c] = exp_in_place(so[:, c], t)
        tsc[c] = exp_in_place(sc[:, c], t_cur)
    g.W(g.dve, tv)
    g.W(g.pool, tv, tr)
    t_sum, t_cv, t_r = {}, {}, {}
    for c in range(DC):
        g.W(g.dve, tsc[c])
        t = g.V(g.dve.tensor_scalar(sc[:, c], sc[:, c], LOW, None, OP.max))
        g.W(g.dve, t, tso[c])
        t_sum[c] = g.V(g.dve.scalar_tensor_tensor(out=mx[:, c], in0=so[:, c], scalar=LOW, in1=sc[:, c], op0=OP.max,
                                                  op1=OP.add))
        g.W(g.pool, t_sum[c])
        t_cv[c] = g.G(g.pool.tensor_tensor(sc[:, c], sc[:, c], vb[:, c], OP.mult))
    for c in range(DC):
        g.W(g.act, t_sum[c])
        t_r[c] = g.A(g.act.activation(uk[:, c], mx[:, c], ACT.Ln, bias=g.e9))
    for c in range(DC):
        g.W(g.act, t_r[c])
        t = g.A(g.act.activation(uk[:, c], uk[:, c], ACT.Exp, scale=-1.0))
        g.W(g.pool, t)
        t_r[c] = g.G(g.pool.tensor_tensor(uk[:, c], uk[:, c], r[:, c].rearrange("p (b s) -> p b s", b=B), OP.mult))
    for c in range(DC):
        g.W(g.dve, tsn[c], tsp[c])
        t = g.V(g.dve.scalar_tensor_tensor(out=sn[:, c], in0=sn[:, c], scalar=LOW, in1=vb[:, c], op0=OP.max,
                                           op1=OP.mult))
        g.W(g.dve, t)
        for b in range(B):
            tq = g.V(g.dve.tensor_tensor_scan(qb[:, c, b, 1:], sp[:, c, b], sn[:, c, b], 0.0, OP.mult, OP.add))
        g.W(g.dve, tq)
        t = g.V(g.dve.scalar_tensor_tensor(out=so[:, c], in0=so[:, c], scalar=LOW, in1=qb[:, c, :, 0:S], op0=OP.max,
                                           op1=OP.mult))
        g.W(g.dve, t, t_cv[c])
        t = g.V(g.dve.tensor_tensor(so[:, c], so[:, c], sc[:, c], OP.add))
        g.W(g.dve, t, t_r[c])
        t = g.V(g.dve.tensor_tensor(so[:, c], so[:, c], uk[:, c], OP.mult))
    project(g, W["o"], so.rearrange("p c b s -> p c (b s)"), DC, DC, add_resid(g), t)


def l1_xattn(g):
    a, w, K = g.a, g.work, 1024
    A, Bt = g.WA, g.WB
    tw = load(g, g.d_w, Bt[:, 0:1024], a["w_l1_xattn"])
    W = [view(Bt, 0, 2, D), view(Bt, 512, 2, D)]
    mraw, madd = view(Bt, 1024, B, S2).bitcast(I32), view(Bt, 1024 + 2 * K, B, S2)
    tmk = load(g, g.d_w2, mraw, a["mask1"].partition_broadcast(P))
    sq, tmp = view(w, 0, 2, NT), view(w, 2 * K, NT)
    u = view(w, 3 * K, 2, NT)
    tu = list(layernorm(g, g.X, u, g.resid, sq, tmp))
    g.W(g.dve, tmk)
    tmk = g.V(g.dve.tensor_scalar(madd, mraw, 0.0, FMIN, OP.is_equal, OP.mult))
    key = view(w, 5 * K, 2, NT)
    prob = [view(w, (7 + j) * K, S2) for j in range(3)]
    PT = [view(w, (10 + j) * K, 8, P) for j in range(2)]
    out = [view(w, 12 * K + j * D, D) for j in range(2)]
    sm = view(g.small, 0, 64)
    bank = [g.ps[:, z * S:(z + 1) * S] for z in range(8)]
    s_psum = [g.ps[:, 0:1024], g.ps[:, 1024:2048]]
    t_psum, o_psum, f_psum = bank[4:6], bank[6][:, 0:D], bank[7][:, 0:D]
    g.W(g.dve, tmk)
    g.W(g.pe, tw)
    g.W(g.pe, g.ring)
    units = [(hop, b, qt) for hop in range(2) for b in range(B) for qt in range(4)]
    T = {}
    done = lambda name, i: T.get((name, i))
    n_s = n_t = 0
    tq = load(g, g.d_next, A[:, 0:4096], a["w_l1_ffn"])
    for step in range(len(units) + 3):
        if step in (4, 8):
            j = step // 4 - 1
            g.quantized[j] = quantize(g, A[:, j * 2048:(j + 1) * 2048],
                                      view(A, 4096 + j * K, K).bitcast(BF16), A[:, 6144:8192],
                                      view(g.small, 200 + 4 * j, 4), tq)
        i = step
        if i < len(units):
            hop, b, qt = units[i]
            q0 = b * S + qt * P
            if qt == 0:
                z, n_s = n_s % 2, n_s + 1
                g.W(g.pe, tu[b], T.get(("s_free", z)))
                for m in range(DC):
                    for c in range(DC):
                        mm = g.pe.matmul(s_psum[z][:, half(m)], W[hop][:, c, m * P:(m + 1) * P], u[:, c, half(b)],
                                         start=c == 0, stop=c == 1)
                g.W(g.act, g.E(mm))
                T["s_free", z] = g.A(g.act.activation(key[:, :, half(b)], s_psum[z].rearrange("p (c s) -> p c s", c=2),
                                                      ACT.Copy))
                g.W(g.pe, T["s_free", z])
            z, n_s = n_s % 2, n_s + 1
            ps, p = s_psum[z], prob[i % 3]
            nm, su, rs = (sm[:, o + i % 4:o + i % 4 + 1] for o in (0, 8, 16))
            g.W(g.pe, T.get(("s_free", z)))
            for hf in range(2):
                for c in range(DC):
                    mm = g.pe.matmul(ps[:, half(hf)], key[:, c, q0:q0 + P],
                                     g.ctxT[:, c, b * S2 + hf * S:b * S2 + (hf + 1) * S], start=c == 0, stop=c == 1)
            g.W(g.dve, g.E(mm), done("turn", i - 3), done("exp", i - 4))
            t = T["s_free", z] = g.V(g.dve.tensor_tensor_reduce(p, ps, madd[:, b, :], -1.0, BIG * 3e8, OP.add, OP.min,
                                                                nm))
            g.W(g.act, t, done("recip", i - 4))
            t = T["exp", i] = g.A(g.act.activation(p, p, ACT.Exp, scale=-1.0, bias=nm, accum_out=su))
            g.W(g.dve, t, done("put", i - 4))
            T["recip", i] = g.V(g.dve.reciprocal(rs, su))
        i = step - 1
        if 0 <= i < len(units):
            g.W(g.pe, done("exp", i))
            for hf in range(2):
                z, n_t = n_t % 2, n_t + 1
                g.W(g.pe, T.get(("t_free", z)))
                for kt in range(4):
                    k0 = hf * S + kt * P
                    mm = g.pe.transpose(t_psum[z][:, kt * P:(kt + 1) * P], prob[i % 3][:, k0:k0 + P], g.iden[:, :])
                t = T["turn", i] = g.E(mm)
                g.W(g.act, t, done("pv", i - 2))
                T["t_free", z] = T["turned", i] = g.A(g.act.activation(
                    PT[i % 2][:, 4 * hf:4 * hf + 4, :].rearrange("p k t -> p (k t)"), t_psum[z], ACT.Copy))
        i = step - 3
        if i >= 0:
            hop, b, qt = units[i]
            q0 = b * S + qt * P
            g.W(g.pe, done("put", i), done("add", i - 1))
            for m in range(DC):
                mm = g.pe.transpose(f_psum[:, m * P:(m + 1) * P], out[i % 2][:, m * P:(m + 1) * P], g.iden[:, :])
            t = T["finish", i] = g.E(mm)
            g.W(g.dve, t)
            tu[b] = T["add", i] = g.V(g.dve.tensor_tensor(u[:, :, q0:q0 + P], u[:, :, q0:q0 + P],
                                                          f_psum.rearrange("p (c t) -> p c t", c=2), OP.add))
        i = step - 2
        if 0 <= i < len(units):
            b = units[i][1]
            g.W(g.pe, done("turned", i), done("put", i - 1))
            for kt in range(8):
                mm = g.pe.matmul(o_psum, PT[i % 2][:, kt, :], g.ctxK[:, b * 8 + kt, :], start=kt == 0, stop=kt == 7)
            t = T["pv", i] = g.E(mm)
            g.W(g.act, t, done("recip", i), done("finish", i - 2))
            T["put", i] = g.A(g.act.activation(out[i % 2], o_psum, ACT.Copy, scale=sm[:, 16 + i % 4:17 + i % 4]))
    g.W(g.dve, tu)
    t = g.V(g.dve.tensor_tensor(g.X, g.X, u, OP.add))
    g.resid = [t, t]


def scale_of(g, sc, ready):
    am, s, inv, al = (sc[:, i:i + 1] for i in range(4))
    g.W(g.pool, ready)
    t = g.G(g.pool.partition_all_reduce(al, am, P, bass.bass_isa.ReduceOp.max))
    g.W(g.dve, t)
    t = g.V(g.dve.tensor_scalar(s, al, 1e-6, 1.0 / 127, OP.max, OP.mult))
    g.W(g.dve, t)
    t = g.V(g.dve.reciprocal(inv, s))
    g.W(g.dve, t)
    return inv


def quantize(g, src, dst, tmp, sc, ready):
    g.W(g.dve, ready)
    t = g.V(g.dve.tensor_reduce(sc[:, 0:1], src, AX.X, OP.max, apply_absolute_value=True))
    inv = scale_of(g, sc, t)
    t = g.V(g.dve.tensor_scalar(tmp, src, inv, ROUND, OP.mult, OP.add))
    g.W(g.dve, t)
    return g.V(g.dve.tensor_scalar(dst, tmp, ROUND, None, OP.subtract))


def l1_ffn(g):
    a, w, K = g.a, g.work, 1024
    A, Bt = g.WA, g.WB
    W1q = view(A, 4096, K).bitcast(BF16)
    W2q = view(A, 4096 + K, K).bitcast(BF16)
    tb = Bt[:, 0:8192]
    sc = [view(g.small, o, 4) for o in (200, 204, 8, 12)]
    tw1, tw2 = g.quantized
    sq, tmp = view(w, 0, 2, NT), view(w, 2 * K, NT)
    t1 = layernorm(g, g.X, g.Hn, g.resid, sq, tmp)
    hq = view(w, 3 * K, K).bitcast(BF16)
    tx = quantize(g, g.Hn.rearrange("p c t -> p (c t)"), hq, tb[:, 4096:6144], sc[2], t1)
    ss = view(g.small, 32, 2)
    b1s, b2s = view(g.small, 40, 8), view(g.small, 50, 2)
    g.W(g.dve, tx, tw2)
    t = g.V(g.dve.tensor_tensor(ss[:, 0:1], sc[0][:, 1:2], sc[2][:, 1:2], OP.mult))
    g.W(g.dve, t)
    col = VCOL["L1_ffn_b1"]
    tb1 = g.V(g.dve.tensor_scalar(b1s, g.vec[:, col:col + 8], ss[:, 0:1], None, OP.mult))
    hid = view(w, 4 * K, FC, NT)

    def ev1(m, ps, t):
        g.W(g.act, t, tb1)
        return g.A(g.act.activation(hid[:, m, :], ps, ACT.Gelu, scale=ss[:, 0:1], bias=b1s[:, m:m + 1]))
    am8 = view(g.small, 64, FC)
    tm = []

    def ev1_max(m, ps, t):
        t = ev1(m, ps, t)
        g.W(g.dve, t)
        tm.append(g.V(g.dve.tensor_reduce(am8[:, m:m + 1], hid[:, m, :], AX.X, OP.max, apply_absolute_value=True)))
        return t
    th = project(g, W1q.rearrange("p (c f) -> p c f", c=2), hq.rearrange("p (c t) -> p c t", c=2), DC, FC, ev1_max,
                 [tx, tw1])
    hidq = view(w, 12 * K, 4 * K).bitcast(BF16).rearrange("p (c t) -> p c t", c=FC)
    am, s_, inv, al = (sc[3][:, i:i + 1] for i in range(4))
    g.W(g.dve, tm)
    t = g.V(g.dve.tensor_reduce(am, am8, AX.X, OP.max))
    inv = scale_of(g, sc[3], t)
    W2v = W2q.rearrange("p (c f) -> p c f", c=FC)
    i0, ps0 = slot(g)
    i1, ps1 = slot(g)
    g.W(g.pe, tw2)
    rounded = {}
    for k in range(FC):
        tmp2 = tb[:, (k % 2) * K:(k % 2 + 1) * K]
        g.W(g.dve, rounded.get(k - 2))
        t = g.V(g.dve.tensor_scalar(tmp2, hid[:, k, :], inv, ROUND, OP.mult, OP.add))
        g.W(g.dve, t)
        t = rounded[k] = g.V(g.dve.tensor_scalar(hidq[:, k, :], tmp2, ROUND, None, OP.subtract))
        g.W(g.pe, t)
        for m, ps in enumerate((ps0, ps1)):
            for n in range(B):
                mm = g.pe.matmul(ps[:, half(n)], W2v[:, k, m * P:(m + 1) * P], hidq[:, k, half(n)], start=k == 0,
                                 stop=k == FC - 1)
    tp = g.E(mm)
    t = g.V(g.dve.tensor_tensor(ss[:, 1:2], sc[1][:, 1:2], sc[3][:, 1:2], OP.mult))
    g.W(g.dve, t)
    col = VCOL["L1_ffn_b2"]
    t = g.V(g.dve.tensor_scalar(b2s, g.vec[:, col:col + 2], ss[:, 1:2], None, OP.mult))
    g.W(g.dve, t)
    o = view(w, 0, 2, NT)
    g.W(g.dve, tp)
    for m, (i, ps) in enumerate(((i0, ps0), (i1, ps1))):
        t = g.ring[i] = g.V(g.dve.tensor_scalar(o[:, m, :], ps, ss[:, 1:2], b2s[:, m:m + 1], OP.mult, OP.add))
        g.W(g.dve, t)
        t = g.V(g.dve.tensor_tensor(g.X[:, m, :], g.X[:, m, :], o[:, m, :], OP.add))
        g.resid = [t, t]



def norm_for(g):
    w, K = g.work, 1024
    return layernorm(g, g.X, g.Hn, g.resid, view(w, 0, 2, NT), view(w, 2 * K, NT))


def fixed_in_place(g, x, tmp, n_cols, t, pre):
    g.W(g.dve, t)
    t = g.V(g.dve.tensor_scalar(x, x, pre, FXMAX, OP.mult, OP.min))
    g.W(g.dve, t)
    t = g.V(g.dve.tensor_scalar(x, x, -FXMAX, None, OP.max))
    g.W(g.act, t)
    t = g.A(g.act.activation(tmp, x, ACT.Sign))
    g.W(g.dve, t)
    ti = tmp.bitcast(I32)
    t = g.V(g.dve.scalar_tensor_tensor(out=ti, in0=tmp, scalar=-HALF, in1=x, op0=OP.mult, op1=OP.add))
    g.W(g.dve, t)
    return g.V(g.dve.tensor_scalar(x, ti, 1.0 / FX, None, OP.mult))


class Stages:
    pass


ATTEND_AGE = dict(scores=0, max=1, exp=2, mult=3, turn=4, pv=5, put=6, finish=7,
                  pv2=6, gather=7, fold=8, spread=9)


def attend(g, c, old, new, hook=None):
    T, n_u = {}, c.units
    done = lambda name, i: T.get((name, i))

    def due(stage):
        i = step - ATTEND_AGE[stage]
        return i, (new if i >= 0 else old) and i < n_u
    n_turn = [0]
    for step in range(n_u if new else ATTEND_AGE["spread" if c.thin else "finish"]):
        if hook:
            hook(step, T, done)
        i, on = due("exp")
        if on:
            p = c.prob[i % c.NP][:, 0:c.keys(i)]
            g.W(g.act, done("max", i))
            T["exp", i] = g.A(g.act.activation(p, p, ACT.Exp, scale=-1.0, bias=c.minmax[:, i % 8:i % 8 + 1],
                                               accum_out=c.sums[:, i % 8:i % 8 + 1]))
        i, on = due("put")
        if on and not c.thin:
            g.W(g.act, done("pv", i), done("mult", i))
            T["put", i] = g.A(g.act.activation(c.out(i), c.o_psum[i % 2][:, 0:c.dh], ACT.Copy,
                                               scale=c.recip[:, i % 16:i % 16 + 1]))
        i, on = due("gather")
        if on and c.thin and i % 4 == 3:
            z = i // 4 % 2
            g.W(g.act, done("pv", i), done("fold", i - 8))
            T["gather", i] = g.A(g.act.activation(c.partial[z], c.o_psum[0], ACT.Copy))
        i, on = due("spread")
        if on and c.thin and i % 4 == 3:
            g.W(g.dve, done("fold", i), done("mult", i))
            r = c.recip[:, i % 16 - 3:i % 16 + 1].unsqueeze(2).broadcast_to([P, 4, c.dh])
            t = g.V(g.dve.tensor_tensor(c.out(i), c.o_psum[1][:, 0:4 * c.dh].rearrange("p (q d) -> p q d", q=4), r,
                                        OP.mult))
            for j in range(4):
                T["put", i - j] = t
        i, on = due("mult")
        if on:
            g.W(g.dve, done("exp", i), done("put", i - 16))
            T["mult", i] = g.V(g.dve.reciprocal(c.recip[:, i % 16:i % 16 + 1], c.sums[:, i % 8:i % 8 + 1]))
            if c.mult is not None:
                p = c.prob[i % c.NP][:, 0:c.keys(i)]
                x, n4 = c.mult(i), c.keys(i) * 5 // 8
                g.W(g.pool, done("exp", i))
                T["mult2", i] = g.G(g.pool.tensor_tensor(p[:, n4:], p[:, n4:], x[:, n4:], OP.mult))
                T["mult", i] = g.V(g.dve.tensor_tensor(p[:, 0:n4], p[:, 0:n4], x[:, 0:n4], OP.mult))
        i, on = due("max")
        if on:
            n = c.keys(i)
            g.W(g.dve, done("scores", i), done("turn", i - c.NP), done("exp", i - 8))
            T["max", i] = g.V(g.dve.tensor_tensor_reduce(c.prob[i % c.NP][:, 0:n], c.s_psum[i % c.NS][:, 0:n], c.add(i),
                                                         -1.0, BIG * 3e8, OP.add, OP.min,
                                                         c.minmax[:, i % 8:i % 8 + 1]))
        i, on = due("scores")
        if on:
            g.W(g.pe, done("max", i - c.NS))
            T["scores", i] = g.E(c.scores(i, c.s_psum[i % c.NS], T))
        i, on = due("turn")
        if on:
            n = c.keys(i)
            g.W(g.pe, done("mult", i), done("mult2", i), done("exp", i))
            for o in range(0, n, S):
                z = n_turn[0] % 2
                n_turn[0] += 1
                nt = (min(n, o + S) - o) // P
                g.W(g.pe, T.get(("turn_free", z)))
                for kt in range(nt):
                    mm = g.pe.transpose(c.t_psum[z][:, kt * P:(kt + 1) * P],
                                        c.prob[i % c.NP][:, o + kt * P:o + (kt + 1) * P], g.iden[:, :])
                t = T["turn", i] = g.E(mm)
                eng = g.dve if c.share and i % 4 in c.share else g.act
                if c.thin:
                    dst = c.PT[i // 4 % 2][:, o // P:o // P + nt, i % 4 * P:(i % 4 + 1) * P]
                    g.W(eng, t, done("pv", i - i % 4 - 5))
                else:
                    dst = c.PT[i % 2][:, o // P:o // P + nt, :]
                    g.W(eng, t, done("pv", i - 2))
                from_psum = c.t_psum[z][:, 0:nt * P].rearrange("p (k t) -> p k t", t=P)
                T["turn_free", z] = T["turned", i] = (g.V(g.dve.tensor_copy(dst, from_psum)) if eng is g.dve else
                                                      g.A(g.act.activation(dst, from_psum, ACT.Copy)))
        i, on = due("finish")
        if on and c.finish and c.finish(i):
            tile, dst = c.finish(i)
            z = n_turn[0] % 2
            n_turn[0] += 1
            g.W(g.pe, done("put", i), T.get(("turn_free", z)))
            for qt in range(4):
                mm = g.pe.transpose(c.t_psum[z][:, qt * P:(qt + 1) * P], tile[:, qt, :], g.iden[:, :])
            g.W(g.act, g.E(mm))
            T["turn_free", z] = g.A(g.act.activation(dst, c.t_psum[z], ACT.Copy))
        i, on = due("pv")
        if on and c.thin and i % 4 == 3:
            g.W(g.pe, [done("turned", i - j) for j in range(4)], done("gather", i - 4))
            c.before_v(i, T)
            nt = c.keys(i) // P
            for kt in range(min(nt, 4)):
                mm = g.pe.matmul(c.o_psum[0][32 * kt:32 * kt + 32, :], c.v(i, kt), c.PT[i // 4 % 2][:, kt, :],
                                 start=True, stop=kt >= nt - 4)
            T["pv", i] = g.E(mm)
        i, on = due("pv2")
        if on and c.thin and i % 4 == 3 and c.keys(i) > S:
            for kt in range(4, c.keys(i) // P):
                mm = g.pe.matmul(c.o_psum[0][32 * (kt - 4):32 * (kt - 4) + 32, :], c.v(i, kt),
                                 c.PT[i // 4 % 2][:, kt, :], start=False, stop=True)
            T["pv", i] = g.E(mm)
        i, on = due("fold")
        if on and c.thin and i % 4 == 3:
            g.W(g.pe, done("gather", i), done("put", i - 4))
            for qt in range(4):
                mm = g.pe.matmul(c.o_psum[1][:, qt * c.dh:(qt + 1) * c.dh],
                                 c.partial[i // 4 % 2][:, qt * P:(qt + 1) * P], c.fold, start=True, stop=True)
            T["fold", i] = g.E(mm)
        i, on = due("pv")
        if on and not c.thin:
            nt = c.keys(i) // P
            g.W(g.pe, done("turned", i), done("put", i - 2))
            if c.before_v:
                c.before_v(i, T)
            for kt in range(nt):
                mm = g.pe.matmul(c.o_psum[i % 2][:, 0:c.dh], c.PT[i % 2][:, kt, :], c.v(i, kt),
                                 start=kt == 0, stop=kt == nt - 1)
            T["pv", i] = g.E(mm)
    return T


def thin_heads(g, name):
    a, w, K = g.a, g.work, 1024
    grouped = name == "L2_xattn"
    keys, causal = (S2, False) if grouped else (S, True)
    nk, NK, dh = keys // P, B * keys, D // H
    src = g.ctxT if grouped else g.Hn
    ROWS = 6 * dh
    scr_q = g.nc.dram_tensor("parts_q_" + name, (H + 1, 3, dh, NT), BF16, kind="Internal").ap()
    scr_k = g.nc.dram_tensor("parts_k_" + name, (H + 1, 6, dh, NK), BF16, kind="Internal").ap()
    PARTS = {"q": (0, 1, 2), "k": (0, 0, 0, 1, 1, 2)}
    W = [view(g.extra, 512 * j, 2, D) for j in range(4)]
    bv, bqk = g.wst[:, 0:D], g.wst[:, D:D + 4]
    load(g, g.d_w, g.extra[:, 0:2048], a["w_" + name])
    load(g, g.d_w, bqk, a["bqk_" + name])
    load(g, g.d_w, view(g.small, 128, dh), a["fold"])
    tw = load(g, g.d_w, bv, a["bv_" + name].partition_broadcast(P))
    if grouped:
        G, NEG = view(g.WA, 0, B, 4, S2), view(g.WB, 0, B, 4, S2)
        tG = load(g, g.d_w2, G, a["group"].rearrange("b (q p) k -> p b q k", p=P))
        tG = load(g, g.d_w2, NEG.bitcast(I32), a["mask2"].rearrange("b (q p) k -> p b q k", p=P))
        scale = 0.25
    else:
        g.G(g.pool.memset(g.WB[:, 2 * K:6 * K], 0.0))
        rel = view(g.WB, 0, S)
        bias = [view(g.WB, (1 + z) * S, S) for z in range(2)]
        slope = [g.small[:, 64 + z:65 + z] for z in range(2)]
        tG = load(g, g.d_w2, rel, a["rel"])
        rt = view(g.small, 100, 1)
        t = g.V(g.dve.reciprocal(rt, vcol(g, "L3_attn_temperature")))
        g.W(g.dve, t)
        scale = rt
        g.W(g.dve, g.V(g.dve.tensor_scalar(rt, rt, 0.25, None, OP.mult)))
    v = view(w, 0, B * nk, D)
    t_ln = norm_for_at(g, 4 * K)
    g.W(g.pe, tw)
    g.W(g.dve, tw)

    qs = [view(w, 4 * K + z * S, S).bitcast(BF16) for z in range(2)]
    ks = [view(w, (5 + z) * K, K).bitcast(BF16) for z in range(2)]

    def fetch(ch, z, head):
        for blk, n in ((0, 3), (3, 2), (5, 1)):
            g.dma(ch, qs[z][blk * dh:(blk + n) * dh, 0:NT], scr_q[head, 0:n].rearrange("j f t -> (j f) t"))
        t = g.dma(ch, ks[z][0:ROWS, 0:NK], scr_k[head].rearrange("j f t -> (j f) t"))
        if not grouped:
            t = g.dma(ch, slope[z], a["slopes"][bass.ds(head, 1)].partition_broadcast(P))
        return t

    QP = view(w, 7 * K, 3, DC, NT // 2).bitcast(BF16)
    KP = view(w, 10 * K, 3, DC, NK // 2).bitcast(BF16)
    g.ring = [None] * 4
    rest = [view(w, 16 * K + j * S, S) for j in range(6)]
    rest_free = [None] * 3
    n_c = 0
    t_parts, t_scr = {}, {}
    for m in range(DC):
        for part, wj, x, n_tok, dst in (("q", 0, g.Hn, NT, QP), ("k", 1, src, NK, KP)):
            for t0 in range(0, n_tok, S):
                z = n_c % 3
                n_c += 1
                i, ps = slot(g)
                if x is g.Hn:
                    g.W(g.pe, t_ln[t0 // S])
                for c in range(DC):
                    mm = g.pe.matmul(ps[:, 0:S], W[wj][:, c, m * P:(m + 1) * P], x[:, c, t0:t0 + S], start=c == 0,
                                     stop=c == 1)
                g.W(g.act, g.E(mm))
                g.W(g.act, rest_free[z])
                y, r = rest[2 * z], rest[2 * z + 1]
                hi, mid, lo = (dst[:, j, m, t0:t0 + S] for j in range(3))
                col = bqk[:, 2 * wj + m:2 * wj + m + 1]
                if part == "q":
                    g.W(g.dve, g.now("pe"), rest_free[z])
                    t = g.V(g.dve.tensor_scalar(y, ps[:, 0:S], col, scale, OP.add, OP.mult))
                else:
                    t = g.A(g.act.activation(y, ps[:, 0:S], ACT.Identity, bias=col))
                g.ring[i] = t
                g.W(g.act, t)
                t = g.A(g.act.activation(hi, y, ACT.Copy))
                g.W(g.dve, t)
                t = g.V(g.dve.tensor_tensor(r, y, hi, OP.subtract))
                g.W(g.pool, t)
                t = g.G(g.pool.tensor_scalar(mid, r, 1.0, 0.0, OP.mult, OP.add))
                g.W(g.dve, t)
                t = rest_free[z] = g.V(g.dve.tensor_tensor(lo, r, mid, OP.subtract))
                t_parts[part] = t
            scr = scr_q if part == "q" else scr_k
            if (part, m) == ("k", 1):
                g.W(g.sp, t_scr[0], t_ln)
                t0 = fetch(g.d_w, 0, 0)
            g.W(g.sp, t_parts[part])
            if m:
                rows = len(PARTS[part]) * dh
                flat = dst.rearrange("p j c t -> p (j c t)")[0:rows, 0:n_tok]
                g.dma(g.d_scr2, scr[H].rearrange("j f t -> (j f) t"), flat)
            for blk, j in enumerate(PARTS[part]):
                t_scr[m] = g.dma((g.d_scr, g.d_scr2)[m], scr[8 * m:8 * m + 8, blk], dst[:, j, m])
    if grouped:
        g.W(g.dve, tG)
        nf = NEG.rearrange("p b q k -> p (b q k)")
        t = g.V(g.dve.tensor_scalar(nf, nf.bitcast(I32), -1.0, 1.0, OP.mult, OP.add))
        g.W(g.dve, t)
        t = g.V(g.dve.tensor_scalar(nf, nf, -1e9, None, OP.mult))
        g.W(g.dve, t)
    for k0 in range(0, B * nk, 4):
        i, ps = slot(g)
        for j in range(4):
            for c in range(DC):
                mm = g.pe.matmul(ps[:, j * D:(j + 1) * D], src[:, c, (k0 + j) * P:(k0 + j + 1) * P], W[2][:, c, :],
                                 start=c == 0, stop=c == 1)
        g.W(g.dve, g.E(mm))
        tv = g.ring[i] = g.V(g.dve.tensor_tensor(v[:, k0:k0 + 4, :], ps.rearrange("p (k d) -> p k d", k=4),
                                                 bv.unsqueeze(1).broadcast_to([P, 4, D]), OP.add))
    g.meet(t_scr[0], t_scr[1])
    for e in (g.dve, g.pool):
        g.W(e, tG)

    vh = [view(w, 17 * K + 512 * z, B * nk, 32) for z in range(2)]
    O = view(w, 7 * K, 8, D)
    HEADS = 4
    c = Stages()
    c.share = () if grouped else (1, 3)
    c.thin, c.units, c.NP, c.NS, c.dh, c.finish = True, HEADS * B * 4, 4096 // keys, 2048 // keys, dh, None
    spare = g.ctxK.rearrange("p k d -> p (k d)")
    c.prob = [spare[:, j * keys:(j + 1) * keys] for j in range(c.NP)]
    c.PT = [view(w, (9 + 4 * j) * K, nk, S) if grouped else view(g.WB, (2 + 2 * j) * K, nk, S) for j in range(2)]
    c.partial = [view(w, 18 * K + j * S, S) for j in range(2)]
    c.fold = view(g.small, 128, dh)
    c.s_psum = [g.ps[:, z * keys:(z + 1) * keys] for z in range(c.NS)]
    c.t_psum = [g.ps[:, (4 + z) * S:(5 + z) * S] for z in range(2)]
    c.o_psum = [g.ps[:, (6 + z) * S:(7 + z) * S] for z in range(2)]
    c.minmax, c.sums, c.recip = (g.small[:, o:o + n] for o, n in ((0, 8), (8, 8), (16, 16)))
    where = lambda i: (i // 8 % 2, i % 8 // 4, i % 4)
    c.keys = lambda i: (i % 4 + 1) * P if causal else keys

    for buf in vh:
        zero = g.V(g.dve.memset(buf, 0.0))
    for e in (g.act, g.pe):
        g.W(e, zero)

    def iteration(first, old, new, ch0=None, ch1=None):
        if grouped:
            c.add = lambda i: NEG[:, where(i)[1], where(i)[2], :]
            c.mult = lambda i: G[:, where(i)[1], where(i)[2], :]
        else:
            c.add = lambda i: bias[where(i)[0]][:, S - c.keys(i):S]
            c.mult = None

        def scores(i, ps, T):
            h, b, qt = where(i)
            n = c.keys(i)
            q0 = b * S + qt * P
            if i and i % 8 == 0:
                g.W(g.pe, T["stack", i // 8])
            for o in range(0, n, S):
                e_ = min(n, o + S)
                mm = g.pe.matmul(ps[:, o:e_], qs[h][0:ROWS, q0:q0 + P], ks[h][0:ROWS, b * keys + o:b * keys + e_],
                                 start=True, stop=True)
            return mm
        c.scores = scores
        c.v = lambda i, kt: vh[where(i)[0]][:, where(i)[1] * nk + kt, :]

        def before_v(i, T):
            if i >= 0 and i % 8 == 3:
                g.W(g.pe, T["vh", i // 8])
        c.before_v = before_v

        def out(i):
            _, b, qt = where(i)
            head = first + i // 8
            return O[:, b * 4:b * 4 + 4, bass.ds(head * dh, dh)]
        c.out = out

        def hook(step, T, done):
            if not new:
                return
            j, rem = divmod(step, 8)
            z = (j + 1) % 2
            if rem == min(j, 1):
                g.W(g.sp, done("scores", 8 * j - 1), T.get(("bias", j - 1), first_bias if not old else None))
                T["stack", j + 1] = fetch((ch0, ch1)[z], z, first + j + 1)
            if rem == 4 and not grouped:
                g.W(g.pool, T["stack", j + 1], done("max", 8 * j - 1))
                T["bias", j + 1] = g.G(g.pool.tensor_scalar(bias[z], rel, slope[z], 1.0, OP.mult, OP.mult))
            if rem == 1 and j and not grouped:
                g.W(g.dve, T["bias", j])
            if step == 0 or rem == 6 and j < HEADS - 1:
                j = 0 if step == 0 else j + 1
                g.W(g.act, done("pv", 8 * (j - 1) - 1))
                T["vh", j] = g.A(g.act.activation(vh[j % 2][:, :, 0:dh], v[:, :, bass.ds((first + j) * dh, dh)],
                                                  ACT.Copy))
        T = attend(g, c, old, new, hook)
        if new:
            g.W(g.pe, T["stack", HEADS])
    g.W(g.pe, t0)
    first_bias = None
    if not grouped:
        g.W(g.pool, t0)
        first_bias = g.G(g.pool.tensor_scalar(bias[0], rel, slope[0], 1.0, OP.mult, OP.mult))
        g.W(g.dve, first_bias)
    iteration(0, False, True, g.d_w, g.d_w2)
    with g.fori(H // HEADS - 1) as i:
        iteration(HEADS * i + HEADS, True, True, g.d_st, g.d_st2)
    iteration(H, True, False)

    g.meet()
    oT = view(w, 9 * K, DC, NT)
    for m in range(DC):
        i, ps = slot(g)
        for qt in range(8):
            mm = g.pe.transpose(ps[:, qt * P:(qt + 1) * P], O[:, qt, m * P:(m + 1) * P], g.iden[:, :])
        g.W(g.act, g.E(mm))
        t = g.ring[i] = g.A(g.act.activation(oT[:, m, :], ps, ACT.Copy))
    project(g, W[3], oT, DC, DC, add_resid(g, name + ("_wo_b" if grouped else "_b_proj")), t)


def wide_heads(g, name):
    a, w, K = g.a, g.work, 1024
    nh, rows, nk, G = 2, 64, S // P, MHA[name]["groups"]
    q = [[view(w, (4 * s + h) * K, NT) for h in range(nh)] for s in range(2)]
    kT = [view(w, (4 * s + 2) * K, NT) for s in range(2)]
    v = [view(w, (4 * s + 3) * K, B, nk, P) for s in range(2)]
    O = [[view(w, 8 * K + (2 * s + b) * S, 4, P) for b in range(B)] for s in range(2)]
    weights = [g.wst[:, 0:898], g.wst2[:, 0:898]]
    causal, wo, oT = view(g.WB, 0, S), view(g.WB, S, G, D), view(g.WA, 0, G, NT)
    c = Stages()
    c.share = ()
    c.thin, c.units, c.NP, c.NS, c.dh, c.before_v, c.mult = False, 2 * B * nh * 4, 8, 2, 64, None, None
    c.prob = [view(w, 10 * K + j * S, S) for j in range(8)]
    c.PT = [view(w, 14 * K + j * S, nk, P) for j in range(2)]
    bank = [g.ps[:, z * S:(z + 1) * S] for z in range(8)]
    c.s_psum, c.t_psum, c.o_psum, p_bank = bank[0:2], bank[2:4], bank[4:6], bank[6:8]
    c.minmax, c.sums, c.recip = (g.small[:, o:o + n] for o, n in ((0, 8), (8, 8), (16, 16)))
    units = [(s, b, h, qt) for s in range(2) for b in range(B) for h in range(nh) for qt in range(4)]
    per = c.units // 2
    c.keys = lambda i: (i % 4 + 1) * P
    c.add = lambda i: causal[:, S - c.keys(i):S]

    def fetch(ch, s, group, *after):
        g.W(g.sp, *after)
        return g.dma(ch, weights[s], a["w_" + name][group])

    def project_group(s, T):
        W = [view(weights[s], 256 * j, 2, P) for j in range(3)]
        bv, bqk = weights[s][:, 768:896], weights[s][:, 896:898]
        free, out = [None] * 2, []
        for n_c, (what, n) in enumerate([("q", 0), ("k", 0), ("q", 1), ("k", 1), ("v", 0), ("v", 1)]):
            ps = p_bank[n_c % 2]
            g.W(g.pe, free[n_c % 2])
            if what == "v":
                for j in range(4):
                    for x in range(DC):
                        k0 = n * S2 + j * P
                        mm = g.pe.matmul(ps[:, j * P:(j + 1) * P], g.ctxT[:, x, k0:k0 + P], W[2][:, x, :],
                                         start=x == 0, stop=x == 1)
            else:
                src, t0 = (g.Hn, n * S) if what == "q" else (g.ctxT, n * S2)
                for x in range(DC):
                    mm = g.pe.matmul(ps, W[what == "k"][:, x, :], src[:, x, t0:t0 + S], start=x == 0, stop=x == 1)
            t = g.E(mm)
            yield
            if what == "q":
                g.W(g.dve, t)
                for h in range(nh):
                    r = slice(h * rows, (h + 1) * rows)
                    t = g.V(g.dve.tensor_scalar(q[s][h][r, half(n)], ps[r], bqk[r, 0:1], 0.125, OP.add, OP.mult))
            elif what == "k":
                g.W(g.act, t)
                t = g.A(g.act.activation(kT[s][:, half(n)], ps, ACT.Identity, bias=bqk[:, 1:2]))
            else:
                g.W(g.dve, t)
                t = g.V(g.dve.tensor_tensor(v[s][:, n], ps.rearrange("p (k d) -> p k d", k=4),
                                            bv.unsqueeze(1).broadcast_to([P, 4, P]), OP.add))
            free[n_c % 2] = t
            out.append(t)
            yield
        T["projected", s] = out

    def iteration(first, old, new, ch0=None, ch1=None):
        running = []

        def scores(i, ps, T):
            s, b, h, qt = units[i]
            n, q0 = c.keys(i), b * S + qt * P
            if i == per:
                g.W(g.pe, T["projected", 1])
            return g.pe.matmul(ps[:, 0:n], q[s][h][:, q0:q0 + P], kT[s][:, b * S:b * S + n], start=True, stop=True)
        c.scores = scores
        c.v = lambda i, kt: v[units[i % c.units][0]][:, units[i % c.units][1], kt,
                                                     units[i % c.units][2] * rows:(units[i % c.units][2] + 1) * rows]

        def out(i):
            s, b, h, qt = units[i % c.units]
            return O[s][b][:, qt, h * rows:(h + 1) * rows]
        c.out = out

        def finish(i):
            s, b, h, qt = units[i % c.units]
            if (h, qt) != (1, 3):
                return None
            return O[s][b], oT[:, (first if i >= 0 else first - 2) + s, half(b)]
        c.finish = finish

        def hook(step, T, done):
            if not new:
                return
            if not old and step in (6, 14):
                j = int(step == 14)
                W = g.WB[:, 2560 + 2048 * j:2560 + 2048 * (j + 1)]
                g.ternary[j] = ternary(g, W, W, view(w, 15 * K, 2048), view(g.small, 200 + 4 * j, 4), t_ffn)
            if step == 0:
                T["w0"] = fetch(ch0, 0, first + 2, g.now("pe", "dve", "act"))
                running.append(project_group(1, T))
            if step == per:
                T["w1"] = fetch(ch1, 1, first + 3, g.now("pe", "dve", "act"))
                g.W(g.pe, T["w0"])
                g.W(g.dve, T["w0"])
                g.W(g.act, T["w0"])
                running.append(project_group(0, T))
                g.W(g.dve, done("scores", per - 1))
                g.W(g.act, done("scores", per - 1))
            if step == 6:
                g.W(g.dve, done("pv", -1))
            if step == per + 6:
                g.W(g.dve, done("pv", per - 1))
            for r in list(running):
                if next(r, "end") == "end":
                    running.remove(r)
        T = attend(g, c, old, new, hook)
        if new:
            for e in (g.pe, g.dve, g.act):
                g.W(e, T["w1"])
        for r in running:
            for _ in r:
                pass

    tc = load(g, g.d_w2, causal, a["causal"])
    tw = load(g, g.d_w2, wo, a["wo_" + name])
    t_ffn = load(g, g.d_next, g.WB[:, 2560:6656], a["w_l3_ffn"])
    t0, t1 = fetch(g.d_w, 0, 0), fetch(g.d_scr, 1, 1)
    tn = layernorm(g, g.X, g.Hn, g.resid, view(w, 12 * K, 2, NT), view(w, 14 * K, NT))
    for s in range(2):
        for h in range(nh):
            z = g.G(g.pool.memset(q[s][h], 0.0))
    g.meet(tn, tw, t0, t1)
    first_group = {}
    for _ in project_group(0, first_group):
        pass
    g.W(g.pe, first_group["projected", 0])
    iteration(0, False, True, g.d_w, g.d_w2)
    with g.fori(G // 2 - 1) as i:
        iteration(2 * i + 2, True, True, g.d_st, g.d_st2)
    iteration(G, True, False)
    g.ring = [None] * 4
    g.W(g.pe, g.now("act", "dve"))
    project(g, wo, oT, G, DC, add_resid(g, name + "_bo"), None)


def norm_for_at(g, off):
    w, K = g.work, 1024
    return layernorm(g, g.X, g.Hn, g.resid, view(w, off, 2, NT), view(w, off + 2 * K, NT))


def fixed_attention(g, oT, t_weights):
    a, w, K, A = g.a, g.work, 1024, g.WA
    nh, rows, nk, G = 2, 64, S // P, MHA["L2_attn"]["groups"]
    q = [[view(w, (4 * s + h) * K, NT) for h in range(nh)] for s in range(2)]
    kT = [view(w, (4 * s + 2) * K, NT) for s in range(2)]
    v = [view(w, (4 * s + 3) * K, B, nk, P) for s in range(2)]
    NE, NA, NS = 16, 8, 4
    ex = [view(w, 8 * K + j * S, S) for j in range(NE)]
    total = [view(w, 16 * K + j * S, S) for j in range(2)]
    diag = [view(w, 17 * K + j * S, S) for j in range(2)]
    sign = [view(w, 18 * K + j * S, S) for j in range(2)]
    attn = [view(A, j * S, S) for j in range(NA)]
    score = [view(A, (8 + j) * S, S).bitcast(I32) for j in range(NS)]
    whole = [view(A, (12 + j) * S, S).bitcast(I32) for j in range(2)]
    oy, osign = view(A, 14 * S, S), view(A, 15 * S, S)
    py, psign = ([view(g.extra, (2 * x + j) * S, S) for j in range(2)] for x in range(2))
    weights = [g.wst[:, 0:898], g.wst2[:, 0:898]]
    step_col, minus_half = g.small[:, 0:1], g.small[:, 1:2]
    recip = [g.small[:, 8 + 8 * j:12 + 8 * j] for j in range(2)]
    bank = [g.ps[:, i * S:(i + 1) * S] for i in range(8)]
    s_bank, r_bank, o_bank, p_bank = bank[0:3], bank[3:5], bank[5], bank[6:8]
    tiles = [(s, b, h, kt) for s in range(2) for b in range(B) for h in range(nh) for kt in range(nk)]
    n_t, per = len(tiles), B * nh * nk
    AGE = dict(scores=0, trunc=1, clip=2, exp=3, add=4, sum=5, diag=6, R=7, norm=11, int=12, conv=13, pv=15,
               out=17, osign=18, oint=19, oput=20)

    def chunk(s, what, n, z, ready):
        W = [view(weights[s], 256 * i, 2, P) for i in range(3)]
        ps = p_bank[z]
        g.W(g.pe, chunk.psum_free[z])
        if what == "v":
            for j in range(4):
                for c in range(DC):
                    k0 = n * S + j * P
                    mm = g.pe.matmul(ps[:, j * P:(j + 1) * P], g.Hn[:, c, k0:k0 + P], W[2][:, c, :],
                                     start=c == 0, stop=c == 1)
        else:
            for c in range(DC):
                mm = g.pe.matmul(ps, W[what == "k"][:, c, :], g.Hn[:, c, half(n)], start=c == 0, stop=c == 1)
        t = g.E(mm)
        yield
        g.W(g.act, t, chunk.free[z])
        g.A(g.act.activation(py[z], ps, ACT.Copy, scale=FX))
        t = chunk.psum_free[z] = g.A(g.act.activation(psign[z], ps, ACT.Sign))
        yield
        g.W(g.dve, t)
        t = g.V(g.dve.tensor_scalar(py[z], py[z], FXMAX, -FXMAX, OP.min, OP.max))
        g.W(g.dve, t)
        ni = psign[z].bitcast(I32)
        t = g.V(g.dve.scalar_tensor_tensor(out=ni, in0=psign[z], scalar=-HALF, in1=py[z], op0=OP.mult, op1=OP.add))
        g.W(g.dve, t, ready())
        if what == "q":
            for h in range(nh):
                r = slice(h * rows, (h + 1) * rows)
                t = g.V(g.dve.tensor_scalar(q[s][h][r, half(n)], ni[r], 0.125, None, OP.mult))
        else:
            dst = kT[s][:, half(n)] if what == "k" else v[s][:, n].rearrange("p k d -> p (k d)")
            t = g.V(g.dve.tensor_scalar(dst, ni, 1.0 / FX, None, OP.mult))
        chunk.free[z] = t
        yield t

    QK, V_ = [("q", 0), ("k", 0), ("q", 1), ("k", 1)], [("v", 0), ("v", 1)]

    def chunks(s, which, ready):
        running, toks = [], []
        todo = list(enumerate(which))
        while todo or running:
            running = [r for r in running if not isinstance(chunks_step(r, toks), Tok)]
            if todo and len(running) < 2:
                z, (what, n) = todo.pop(0)
                r = chunk(s, what, n, z % 2, ready)
                next(r)
                running.append(r)
            if running:
                yield
                chunks_step(running[-1], toks)
                yield
        g.projected = toks

    def chunks_step(r, toks):
        t = next(r)
        if isinstance(t, Tok):
            toks.append(t)
        return t

    def body(first, old, new, fetch_even=None, fetch_odd=None):
        chunk.psum_free, chunk.free = [None] * 2, [None] * 2
        T, running = {}, {}
        done = lambda name, i: T.get((name, i))
        plan = {0: ("v0", 0, V_, None),
                4: ("qk1", 1, QK, None),
                16: ("v1", 1, V_, lambda: done("pv", -1)),
                20: ("qk0", 0, QK, lambda: done("qk", per - 1))} if new else {}

        def due(stage):
            i = step - AGE[stage]
            return i, (new if i >= 0 else old) and i < n_t

        def head_due(stage):
            i, on = due(stage)
            return i // nk, on and i % nk == nk - 1
        for step in range(n_t if new else AGE["oput"] + 1):
            if step in plan:
                key, s, which, ready = plan[step]
                if key == "qk0":
                    g.W(g.pe, t_even)
                running[key] = chunks(s, which, ready or (lambda: None))
            for key in list(running):
                if next(running[key], "end") == "end":
                    T["projected", key] = g.projected
                    del running[key]
                    if key == "v0" and fetch_even:
                        t_even = fetch_even(g.now("pe"))
                    if key == "v1" and fetch_odd:
                        t_odd = fetch_odd(g.now("pe"))
            for stage in ("out", "osign", "oint", "oput"):
                i, on = due(stage)
                s, b, h, kt = tiles[i % n_t]
                if not (on and (h, kt) == (1, nk - 1)):
                    continue
                on_ = osign.bitcast(I32)
                if stage == "out":
                    g.W(g.dve, done("pv", i), done("oput", i - per // 2))
                    T[stage, i] = g.V(g.dve.tensor_scalar(oy, o_bank, FXMAX, -FXMAX, OP.min, OP.max))
                elif stage == "osign":
                    g.W(g.act, done("out", i))
                    T[stage, i] = g.A(g.act.activation(osign, oy, ACT.Sign))
                elif stage == "oint":
                    g.W(g.dve, done("osign", i))
                    T[stage, i] = g.V(g.dve.scalar_tensor_tensor(out=on_, in0=osign, scalar=-HALF, in1=oy,
                                                                 op0=OP.mult, op1=OP.add))
                else:
                    g.W(g.act, done("oint", i))
                    group = (first if i >= 0 else first - 2) + s
                    T[stage, i] = g.A(g.act.activation(oT[:, group, half(b)], on_, ACT.Copy, scale=1.0 / FX))
            i, on = due("exp")
            if on:
                g.W(g.act, done("clip", i))
                T["exp", i] = g.A(g.act.activation(ex[i % NE], ex[i % NE], ACT.Exp, scale=1.0 / FX))
            i, on = due("int")
            if on:
                g.W(g.act, done("norm", i), done("conv", i - 2))
                T["int", i] = g.A(g.act.activation(whole[i % 2], ex[i % NE], ACT.Identity, bias=minus_half))
            i, on = due("add")
            if on and i % nk > 0:
                u = i // nk
                g.W(g.pool, done("exp", i), done("exp", i - 1), done("sum", u - 2), done("add", i - 1))
                in0 = ex[(i - 1) % NE] if i % nk == 1 else total[u % 2]
                T["add", i] = g.G(g.pool.tensor_tensor(total[u % 2], in0, ex[i % NE], OP.add))
            i, on = due("conv")
            if on:
                g.W(g.pool, done("int", i), done("pv", i - NA))
                T["conv", i] = g.G(g.pool.tensor_scalar(attn[i % NA], whole[i % 2], 1.0, 0.0, OP.mult, OP.add))
            i, on = due("clip")
            if on:
                g.W(g.dve, done("trunc", i), done("int", i - NE))
                T["clip", i] = g.V(g.dve.tensor_scalar(ex[i % NE], score[i % NS], FXMAX, -FXMAX, OP.min, OP.max))
            i, on = due("norm")
            if on:
                g.W(g.dve, done("R", i // nk))
                T["norm", i] = g.V(g.dve.tensor_tensor(ex[i % NE], ex[i % NE], r_bank[i // nk % 2], OP.mult))
            u, on = head_due("diag")
            if on:
                g.W(g.dve, done("sum", u), done("diag", u - 2))
                t = g.V(g.dve.reciprocal(recip[u % 2], r_bank[u % 2][:, 0:4]))
                g.W(g.pool, t, done("R", u - 2))
                for j in range(4):
                    T["diag", u] = g.G(g.pool.tensor_scalar(diag[u % 2][:, j * P:(j + 1) * P], g.iden[:, :],
                                                            recip[u % 2][:, j:j + 1], 1.0, OP.mult, OP.mult))
            i, on = due("trunc")
            if on:
                ps = s_bank[i % n_t % 3]
                g.W(g.act, done("qk", i), done("trunc", i - 2))
                t = g.A(g.act.activation(sign[i % 2], ps, ACT.Sign))
                g.W(g.dve, t, done("clip", i - NS))
                T["trunc", i] = g.V(g.dve.scalar_tensor_tensor(out=score[i % NS], in0=sign[i % 2], scalar=-HALF,
                                                               in1=ps, op0=OP.mult, op1=OP.add))
            i = step
            if new:
                s, b, h, kt = tiles[i]
                if i == per:
                    g.W(g.pe, T["projected", "qk1"])
                g.W(g.pe, done("trunc", i - 3 if i >= 3 else (-2, -1, -3)[i]))
                T["qk", i] = g.E(g.pe.matmul(s_bank[i % 3], kT[s][:, b * S + kt * P:b * S + (kt + 1) * P],
                                             q[s][h][:, half(b)], start=True, stop=True))
            u, on = head_due("sum")
            if on:
                g.W(g.pe, done("add", u * nk + nk - 1), done("norm", (u - 2) * nk + nk - 1))
                for j in range(4):
                    mm = g.pe.matmul(r_bank[u % 2][:, j:j + 1], total[u % 2][:, j * P:(j + 1) * P], step_col,
                                     start=True, stop=True)
                T["sum", u] = g.E(mm)
            u, on = head_due("R")
            if on:
                g.W(g.pe, done("diag", u))
                T["R", u] = g.E(g.pe.matmul(r_bank[u % 2], g.ones[:, :], diag[u % 2], start=True, stop=True))
            i, on = due("pv")
            if on and tiles[i % n_t][2] == 1 and i % 2 == 1:
                s, b, h, kt = tiles[i % n_t]
                if i == nk + 1:
                    g.W(g.pe, T["projected", "v0"])
                if i == per + nk + 1:
                    g.W(g.pe, T["projected", "v1"])
                g.W(g.pe, done("conv", i), done("out", i - kt - nk - 1))
                for k2 in (kt - 1, kt):
                    for h2 in range(nh):
                        j = i - kt + k2 - nk * (1 - h2)
                        mm = g.pe.matmul(o_bank[h2 * rows:(h2 + 1) * rows, :],
                                         v[s][:, b, k2, h2 * rows:(h2 + 1) * rows], attn[j % NA],
                                         start=k2 == 0, stop=k2 == nk - 1)
                t = g.E(mm)
                for j in (i, i - 1, i - nk, i - nk - 1):
                    T["pv", j] = t
        for key in list(running):
            for _ in running[key]:
                pass
        if new and fetch_odd:
            g.W(g.pe, t_odd)

    wsrc = a["w_L2_attn"]

    def fetch(ch, s, group):
        def go(after=None):
            g.W(g.sp, after)
            return g.dma(ch, weights[s], wsrc[group])
        return go
    g.V(g.dve.memset(step_col, 1.0 / FX))
    g.V(g.dve.memset(minus_half, -HALF))
    for s in range(2):
        for h in range(nh):
            z = g.G(g.pool.memset(q[s][h], 0.0))
    g.W(g.dve, z)
    g.W(g.pe, t_weights, g.now("dve"))
    chunk.psum_free, chunk.free = [None] * 2, [None] * 2
    for _ in chunks(0, QK, lambda: None):
        pass
    g.W(g.pe, g.projected)
    body(0, False, True, fetch(g.d_w, 0, 2), fetch(g.d_w2, 1, 3))
    with g.fori(G // 2 - 1) as i:
        body(2 * i + 2, True, True, fetch(g.d_st, 0, 2 * i + 4), fetch(g.d_st2, 1, 2 * i + 5))
    wo = view(w, 0, G, D)
    tw = load(g, g.d_w, wo, a["wo_L2_attn"])
    body(G, True, False)
    return wo, tw


def l2_attn(g):
    t = [load(g, ch, buf[:, 0:898], g.a["w_L2_attn"][group])
         for group, (ch, buf) in enumerate(((g.d_w, g.wst), (g.d_w2, g.wst2)))]
    tn = norm_for(g)
    g.meet(tn)
    oT = view(g.WB, 0, 8, NT)
    wo, tw = fixed_attention(g, oT, t)
    g.W(g.pe, tw, g.now("act"))
    y, z = view(g.work, 8 * 1024, 2, NT), view(g.work, 10 * 1024, 2, NT)
    g.meet()
    g.ring = [None] * 4

    def ev(m, ps, t):
        g.W(g.act, t)
        t = t0 = g.A(g.act.activation(y[:, m, :], ps, ACT.Identity, bias=vcol(g, "L2_attn_b_proj", m)))
        t = fixed_in_place(g, y[:, m, :], z[:, m, :], NT, t, FX)
        g.W(g.dve, t)
        t = g.V(g.dve.tensor_tensor(g.X[:, m, :], g.X[:, m, :], y[:, m, :], OP.add))
        g.resid = [t, t]
        return t0
    project(g, wo, oT, 8, DC, ev, None)


def l2_xattn(g):
    thin_heads(g, "L2_xattn")


def l2_ffn(g):
    a, w, K = g.a, g.work, 1024
    M = 64
    Bt = g.WB
    win, w1, w2, wo = view(Bt, 0, 2, M), view(Bt, 128, FF), view(Bt, 1200, FC, M), view(Bt, 1800, D)
    load(g, g.d_w, win, a["l2f_win"])
    load(g, g.d_w, w1[0:M], a["l2f_w1"])
    load(g, g.d_w, w2, a["l2f_w2"])
    tw = load(g, g.d_w, wo[0:M], a["l2f_wout"])
    t1 = norm_for(g)
    s = view(w, 3 * K, NT)
    hid = view(w, 4 * K, FC, NT)
    g2 = view(w, 12 * K, NT)
    g.W(g.pe, tw)

    def thin(wT, rhs, kts, dst, bias, ready):
        i, ps = slot(g)
        for n in range(B):
            g.W(g.pe, ready)
            for k in range(kts):
                mm = g.pe.matmul(ps[0:M, half(n)], wT[:, k, :], rhs[:, k, half(n)], start=k == 0, stop=k == kts - 1)
        t = g.E(mm)
        g.W(g.act, t)
        t = g.ring[i] = g.A(g.act.activation(dst[0:M], ps[0:M], ACT.Identity, bias=vcol(g, bias)[0:M]))
        return t
    t = thin(win, g.Hn, DC, s, "L2_ffn_bin_", t1)
    for m in range(FC):
        i, ps = slot(g)
        g.W(g.pe, t)
        for n in range(B):
            mm = g.pe.matmul(ps[:, half(n)], w1[0:M, m * P:(m + 1) * P], s[0:M, half(n)], start=True, stop=True)
        tp = g.E(mm)
        g.W(g.act, tp)
        th = g.ring[i] = g.A(g.act.activation(hid[:, m, :], ps, ACT.Relu, bias=vcol(g, "L2_ffn_b1", m)))
    t = thin(w2, hid, FC, g2, "L2_ffn_b2", th)
    ev = add_resid(g, "L2_ffn_bout")
    for m in range(DC):
        i, ps = slot(g)
        g.W(g.pe, t)
        for n in range(B):
            mm = g.pe.matmul(ps[:, half(n)], wo[0:M, m * P:(m + 1) * P], g2[0:M, half(n)], start=True, stop=True)
        g.ring[i] = ev(m, ps, g.E(mm))


def l3_attn(g):
    thin_heads(g, "L3_attn")


def l3_xattn(g):
    wide_heads(g, "L3_xattn")


def ternary(g, src, dst, tmp, sc, ready):
    n = P * 2048
    am, s, inv, al = (sc[:, i:i + 1] for i in range(4))
    g.W(g.dve, ready)
    t = g.V(g.dve.tensor_reduce(am, src, AX.X, OP.add, apply_absolute_value=True))
    g.W(g.pool, t)
    t = g.G(g.pool.partition_all_reduce(al, am, P, bass.bass_isa.ReduceOp.add))
    g.W(g.dve, t)
    t = g.V(g.dve.tensor_scalar(s, al, 1.0 / n, 1e-8, OP.mult, OP.max))
    g.W(g.dve, t)
    t = g.V(g.dve.reciprocal(inv, s))
    g.W(g.dve, t)
    t = g.V(g.dve.tensor_scalar(tmp, src, inv, ROUND, OP.mult, OP.add))
    g.W(g.dve, t)
    t = g.V(g.dve.tensor_scalar(tmp, tmp, ROUND, 1.0, OP.subtract, OP.min))
    g.W(g.dve, t)
    return g.V(g.dve.tensor_scalar(dst, tmp, -1.0, None, OP.max))


def l3_ffn(g):
    a, w, K = g.a, g.work, 1024
    W1, W2 = g.WB[:, 2560:4608], g.WB[:, 4608:6656]
    tw1, tw2 = g.ternary
    t1 = norm_for(g)
    hid = view(w, 4 * K, FC, NT)

    def ev1(m, ps, t):
        g.W(g.act, t)
        return g.A(g.act.activation(hid[:, m, :], ps, ACT.Gelu, bias=vcol(g, "L3_ffn_b1", m)))
    g.W(g.pe, tw1)
    th = project(g, W1.rearrange("p (c f) -> p c f", c=2), g.Hn, DC, FC, ev1, t1)
    g.W(g.pe, tw2)
    project(g, W2.rearrange("p (c f) -> p c f", c=FC), hid, FC, DC, add_resid(g, "L3_ffn_b2"), th[-1])


STAGES = [l0_attn, l0_xattn, l0_ffn, l1_attn, l1_xattn, l1_ffn, l2_attn, l2_xattn, l2_ffn, l3_attn, l3_xattn, l3_ffn]



def kxm(w):
    k, m = w.shape
    return np.ascontiguousarray(w.reshape(k // P, P, m).transpose(1, 0, 2))


def head_pack(w, rows, dh):
    k = w.shape[0]
    out = np.zeros((k, H, rows), w.dtype)
    out[:, :, :dh] = w.reshape(k, H, dh)
    return out.reshape(k, H * rows)


def lay_out(i):
    f = np.float32
    o = {}
    o["xT"] = np.ascontiguousarray(i["x"].reshape(NT, D).T)
    o["ctx_keys"] = np.ascontiguousarray(i["ctx_1024"].reshape(B * S2, D))
    o["ctxT"] = np.ascontiguousarray(o["ctx_keys"].T)
    o["ident"] = np.eye(P, dtype=f)
    o["blockdiag"] = np.kron(np.eye(P // 16, dtype=f), np.ones((16, 16), f))
    vec = dict(i)
    for j in range(4):
        vec[f"cw{j}"] = i["L0_attn_conv_w"][:, 0, j]
    vec["gamma"] = np.repeat(i["L0_attn_gamma_attn"].reshape(H), D // H)
    vec["L2_ffn_b1"] = i["L2_ffn_b1"].reshape(FF)
    V = np.zeros((P, NVEC), f)
    for n in VEC256:
        V[:, VCOL[n]:VCOL[n] + 2] = vec[n].reshape(2, P).T
    for n in VEC1024:
        V[:, VCOL[n]:VCOL[n] + 8] = vec[n].reshape(8, P).T
    for n in ("L2_ffn_bin_", "L2_ffn_b2"):
        V[:64, VCOL[n]] = vec[n]
    for n in ("L0_ffn_scale", "L3_attn_temperature"):
        V[:, VCOL[n]] = vec[n][0]
    o["vecs"] = V

    def packs(*ws):
        return np.concatenate([kxm(np.ascontiguousarray(w)).reshape(P, -1) for w in ws], axis=1)
    o["w_l0_attn"] = packs(*(i["L0_attn_" + n].T for n in ("qk_w", "v_w", "g_w", "o_w", "gate_w", "up_w", "down_w")))
    idx = np.linspace(0.0, 1.0, D // H, dtype=f)
    freqs = (f(10.0) ** idx)[None, :] * np.arange(H, dtype=f)[:, None]
    ang = np.arange(S, dtype=f)[:, None] * freqs.reshape(1, D)
    o["cos"] = np.ascontiguousarray(np.cos(ang.astype(np.float64)).astype(f).T)
    o["l0f_AT"] = np.ascontiguousarray(i["L0_ffn_A"].transpose(2, 0, 1).reshape(R_, E_ * L_))
    o["l0f_B"] = np.ascontiguousarray(i["L0_ffn_B"].transpose(1, 0, 2))
    o["l0f_gate"] = kxm(i["L0_ffn_w_gate"])
    o["l0f_wt"] = kxm(np.ascontiguousarray(i["L0_ffn_wt_w"].T))
    o["l0f_wd"] = kxm(np.ascontiguousarray(i["L0_ffn_wd_w"].T))
    o["l0f_wtb"] = i["L0_ffn_wt_b"]
    o["rank"] = np.tile(np.arange(E_, 0, -1, dtype=f), (P, 1))
    o["w_l1_attn"] = packs(*(i["L1_attn_W_" + n].T for n in "kvro"))
    o["w_l1_xattn"] = packs(i["L1_xattn_W0"].T, i["L1_xattn_W1"].T)
    o["mask1"] = np.ascontiguousarray(i["mask_BxS2_if1"])
    o["w_l1_ffn"] = packs(i["L1_ffn_w1"].T, i["L1_ffn_w2"].T)
    o["w_l3_ffn"] = packs(i["L3_ffn_W1"].T, i["L3_ffn_W2"].T)
    o["group"] = np.ascontiguousarray(i["fside_BxSxS2_0"])
    o["mask2"] = np.ascontiguousarray(i["mask_BxSxS2_ik1"])
    z1024 = np.zeros(1024, f)
    M = 64
    o["l2f_win"] = kxm(i["L2_ffn_Win"])
    w1, w2 = np.zeros((M, M, 16), f), np.zeros((M, 16, M), f)
    for m in range(M):
        w1[m, m], w2[m, :, m] = i["L2_ffn_W1"][m], i["L2_ffn_W2"][m]
    o["l2f_w1"] = w1.reshape(M, FF)
    o["l2f_w2"] = kxm(w2.reshape(FF, M))
    o["l2f_wout"] = np.ascontiguousarray(i["L2_ffn_Wout"])
    wqkv = i["L2_attn_w_qkv"].reshape(3, 1024, D)
    wa, ba = i["L3_attn_W_attn"].reshape(D, 3, D), i["L3_attn_b_attn"].reshape(3, D)
    heads = {
        "L2_attn": ([wqkv[j].T for j in range(3)], [z1024] * 3, i["L2_attn_w_proj"].T),
        "L2_xattn": ([i[f"L2_xattn_w{n}_k"] for n in "qkv"], [i[f"L2_xattn_w{n}_b"] for n in "qkv"], i["L2_xattn_wo_k"]),
        "L3_attn": ([wa[:, j] for j in range(3)], [ba[j] for j in range(3)], i["L3_attn_W_proj"]),
        "L3_xattn": ([i["L3_xattn_W" + n].T for n in "qkv"], [i["L3_xattn_b" + n] for n in "qkv"], i["L3_xattn_Wo"].T),
    }
    for n, (ws, bs, wo) in heads.items():
        if MHA[n]["dh"] == 16:
            o["w_" + n] = packs(*ws, wo)
            o["bqk_" + n] = np.concatenate([x.reshape(2, P).T for x in bs[:2]], axis=1)
            o["bv_" + n] = np.ascontiguousarray(bs[2])
            continue
        G, rows, dh = MHA[n]["groups"], MHA[n]["rows"], MHA[n]["dh"]
        wp = [kxm(head_pack(w, rows, dh)).reshape(P, DC, G, P) for w in ws]
        o["w_" + n] = np.zeros((G + 2, P, 3 * DC * P + P + 2), f)
        o["w_" + n][:G, :, :768] = np.stack(wp).transpose(3, 1, 0, 2, 4).reshape(G, P, 3 * DC * P)
        bp = [head_pack(b[None], rows, dh).reshape(G, P) for b in bs]
        o["w_" + n][:G, :, 768:896] = bp[2][:, None, :]
        o["w_" + n][:G, :, 896:898] = np.stack(bp[:2], axis=2)
        o["wo_" + n] = kxm(np.ascontiguousarray(head_pack(np.ascontiguousarray(wo.T), rows, dh).T))
    j = np.arange(S)[None, :] - (S - P) - np.arange(P)[:, None]
    o["fold"] = np.tile(np.eye(32, 16, dtype=f), (4, 1))
    o["rel"] = np.where(j <= 0, j, -1e30).astype(f)
    o["causal"] = np.where(j <= 0, 0, -1e30).astype(f)
    start = 2.0 ** (-2.0 ** (-(np.log2(H) - 3)))
    o["slopes"] = np.array([start * start ** h for h in range(H + 1)], f)
    return o


def kernel(**inputs):
    import concourse.bacc as bacc
    from concourse.bass_utils import run_bass_kernel_spmd

    arrays = lay_out({k: np.asarray(v) for k, v in inputs.items()})
    nc = bacc.Bacc("TRN2", target_bir_lowering=False, num_devices=1)
    a = {n: nc.dram_tensor("in_" + n, x.shape, mybir.dt.from_np(x.dtype), kind="ExternalInput").ap()
         for n, x in arrays.items()}
    a["out"] = nc.dram_tensor("out_x", (D, NT), F32, kind="ExternalOutput").ap()
    decoder(nc, a, range(len(STAGES)))
    r = run_bass_kernel_spmd(nc, [{"in_" + k: v for k, v in arrays.items()}], core_ids=[0])
    return np.ascontiguousarray(r.results[0]["out_x"].T).reshape(B, S, D)
```
